# Optimizing a Trainium2 kernel written in Bass

```python
import numpy as np
import jax
import jax.numpy as jnp

def _softmax(x, axis=-1):
    return jax.nn.softmax(x, axis=axis)

def _gelu(x):
    return jax.nn.gelu(x, approximate=True)

def _silu(x):
    return jax.nn.silu(x)

def _sigmoid(x):
    return jax.nn.sigmoid(x)

def _layernorm(x, axis=-1, eps=1e-05):
    m = jnp.mean(x, axis=axis, keepdims=True)
    v = jnp.var(x, axis=axis, keepdims=True)
    return (x - m) / jnp.sqrt(v + eps)

def _scatter_add(tgt, idx, src, axis=0):
    return tgt.at[idx].add(src)

def _segment_sum(src, seg, n):
    return jax.ops.segment_sum(src, seg, n)
kernel_name = 'mk_xattn_ffn_d2_seqx_r8_495026'

def setup_inputs(seed: int=0):
    np.random.seed(seed)
    _w = jnp.asarray

    def _rec_inputs():
        import jax
        import jax.numpy as jnp
        _rk = jax.random.key(seed)
        x = 7.22e-05 + 1 * jax.random.normal(jax.random.fold_in(_rk, 1), (64, 64, 128), jnp.float32)
        _lenS = 64 - jax.random.randint(jax.random.fold_in(_rk, 7), (64,), 0, max(1, 64 // 4) + 1, jnp.int32)
        _lenS2 = 64 - jax.random.randint(jax.random.fold_in(_rk, 8), (64,), 0, max(1, 64 // 4) + 1, jnp.int32)
        _ctx_1024P = jax.random.normal(jax.random.fold_in(_rk, 11), (64, 16, 128), jnp.float32)
        _ctx_1024c = jax.random.dirichlet(jax.random.fold_in(_rk, 511), 0.3 * jnp.ones((16,), jnp.float32), (64, 64))
        _ctx_1024t = jnp.einsum('bsk,bkd->bsd', _ctx_1024c, _ctx_1024P)
        _ctx_1024t = _ctx_1024t * jax.lax.rsqrt(jnp.mean(jnp.square(_ctx_1024t)) + 1e-12) * 0.953939
        ctx_1024 = 4.13588e-05 + 0.999923 * (_ctx_1024t + 0.3 * jax.random.normal(jax.random.fold_in(_rk, 611), (64, 64, 128), jnp.float32))
        _validS = jnp.arange(64)[None, :] < _lenS[:, None]
        _validS2 = jnp.arange(64)[None, :] < _lenS2[:, None]
        _causal = jnp.tril(jnp.ones((64, 64), dtype=bool))
        mask_Bx1x1xS2_bk0 = jnp.logical_not(jnp.broadcast_to(_validS2[:, None, None, :], (64, 1, 1, 64)))
        return (x, ctx_1024, mask_Bx1x1xS2_bk0)
    x, ctx_1024, mask_Bx1x1xS2_bk0 = _rec_inputs()

    def _L0_xattn_setup():
        import jax, jax.numpy as jnp
        import numpy as np
        B, LQ, LK = (4, 256, 256)
        DQ, DK, DO = (128, 128, 128)
        key = jax.random.key(seed)
        ks = jax.random.split(key, 9)
        s = 0.02
        return {'query_input': jax.random.normal(ks[0], (B, LQ, DQ), jnp.float32), 'key_input': jax.random.normal(ks[1], (B, LK, DK), jnp.float32), 'value_input': jax.random.normal(ks[2], (B, LK, DK), jnp.float32), 'Wq': jax.random.normal(ks[3], (DQ, DO), jnp.float32) * s, 'bq': jax.random.normal(ks[4], (DO,), jnp.float32) * s, 'Wk': jax.random.normal(ks[5], (DK, DO), jnp.float32) * s, 'bk': jax.random.normal(ks[6], (DO,), jnp.float32) * s, 'Wv': jax.random.normal(ks[7], (DK, DO), jnp.float32) * s, 'bv': jax.random.normal(ks[8], (DO,), jnp.float32) * s}
    _L0_xattn_all = _L0_xattn_setup()
    _L0_xattn_in = {k: v for k, v in _L0_xattn_all.items() if k in ('Wq', 'bq', 'Wk', 'bk', 'Wv', 'bv')}
    del _L0_xattn_all

    def _L0_ffn_setup():
        import jax, jax.numpy as jnp
        import numpy as np
        D = 128
        F = 128
        E = 8
        K = 2
        key = jax.random.key(seed)
        ks = jax.random.split(key, 8)
        s = 0.02
        return {'x': jax.random.normal(ks[0], (2, 256, D), jnp.float32), 'Wr': jax.random.normal(ks[1], (E, D), jnp.float32) * s, 'Wg': jax.random.normal(ks[2], (E, F, D), jnp.float32) * s, 'Wu': jax.random.normal(ks[3], (E, F, D), jnp.float32) * s, 'Wd': jax.random.normal(ks[4], (E, D, F), jnp.float32) * s, 'Sg': jax.random.normal(ks[5], (F, D), jnp.float32) * s, 'Su': jax.random.normal(ks[6], (F, D), jnp.float32) * s, 'Sd': jax.random.normal(ks[7], (D, F), jnp.float32) * s}
    _L0_ffn_all = _L0_ffn_setup()
    _L0_ffn_in = {k: v for k, v in _L0_ffn_all.items() if k in ('Wr', 'Wg', 'Wu', 'Wd', 'Sg', 'Su', 'Sd')}
    del _L0_ffn_all

    def _L1_xattn_setup():
        import jax, jax.numpy as jnp
        import numpy as np
        D_MODEL = 128
        N_HEADS = 16
        N_MEM = 64
        D_K = D_MODEL // N_HEADS
        key = jax.random.key(seed)
        ks = jax.random.split(key, 16)
        B, N = (2, 256)
        s = 1.0 / np.sqrt(D_MODEL)
        inp = {'q': jax.random.normal(ks[0], (B, N, D_MODEL), jnp.float32), 'k': jax.random.normal(ks[1], (B, N, D_MODEL), jnp.float32), 'v': jax.random.normal(ks[2], (B, N, D_MODEL), jnp.float32), 'attention_mask': jax.random.randint(ks[3], (B, 1, 1, N), 0, 2).astype(bool), 'Wq': jax.random.normal(ks[4], (D_MODEL, D_MODEL), jnp.float32) * s, 'bq': jnp.zeros((D_MODEL,), jnp.float32), 'Wk': jax.random.normal(ks[5], (D_MODEL, D_MODEL), jnp.float32) * s, 'bk': jnp.zeros((D_MODEL,), jnp.float32), 'Wv': jax.random.normal(ks[6], (D_MODEL, D_MODEL), jnp.float32) * s, 'bv': jnp.zeros((D_MODEL,), jnp.float32), 'Wo': jax.random.normal(ks[7], (D_MODEL, D_MODEL), jnp.float32) * s, 'bo': jnp.zeros((D_MODEL,), jnp.float32), 'm_k': jax.random.normal(ks[8], (1, N_MEM, D_MODEL), jnp.float32) * 0.01, 'm_v': jax.random.normal(ks[9], (1, N_MEM, D_MODEL), jnp.float32) * 0.01}
        return inp
    _L1_xattn_all = _L1_xattn_setup()
    _L1_xattn_in = {k: v for k, v in _L1_xattn_all.items() if k in ('Wq', 'bq', 'Wk', 'bk', 'Wv', 'bv', 'Wo', 'bo', 'm_k', 'm_v')}
    del _L1_xattn_all

    def _L1_ffn_setup():
        import jax, jax.numpy as jnp
        import numpy as np
        D = 128
        H = 4
        DF = 512
        E = 8
        EPS = 1e-05

        def _layer_norm(x, g, b):
            mu = jnp.mean(x, axis=-1, keepdims=True)
            var = jnp.mean(jnp.square(x - mu), axis=-1, keepdims=True)
            return (x - mu) * jax.lax.rsqrt(var + EPS) * g + b

        def _mha(x, Wqkv, bqkv, Wo, bo):
            S, B, _ = x.shape
            hd = D // H
            qkv = x @ Wqkv.T + bqkv
            q, k, v = jnp.split(qkv, 3, axis=-1)
            to_heads = lambda t: t.reshape(S, B, H, hd).transpose(1, 2, 0, 3)
            q, k, v = (to_heads(q), to_heads(k), to_heads(v))
            scores = jnp.einsum('bhqd,bhkd->bhqk', q, k) * (1.0 / np.sqrt(hd))
            att = jax.nn.softmax(scores, axis=-1)
            o = jnp.einsum('bhqk,bhkd->bhqd', att, v)
            o = o.transpose(2, 0, 1, 3).reshape(S, B, D)
            return o @ Wo.T + bo

        def _moe(x, Wg, W1, b1, W2, b2):
            S, B, _ = x.shape
            xf = x.reshape(S * B, D)
            logits = xf @ Wg.T
            idx = jnp.argmax(logits, axis=-1)
            out = jnp.zeros_like(xf)
            for e in range(E):
                m = (idx == e)[:, None].astype(xf.dtype)
                h = jax.nn.relu(xf @ W1[e] + b1[e])
                out = out + m * (h @ W2[e] + b2[e])
            return out.reshape(S, B, D)
        key = jax.random.key(seed)
        ks = jax.random.split(key, 16)
        S, B = (64, 8)
        s = lambda k, shape, fan: jax.random.normal(k, shape, jnp.float32) * (1.0 / np.sqrt(fan))
        return {'x': jax.random.normal(ks[0], (S, B, D), jnp.float32), 'Wqkv': s(ks[1], (3 * D, D), D), 'bqkv': jnp.zeros((3 * D,), jnp.float32), 'Wo': s(ks[2], (D, D), D), 'bo': jnp.zeros((D,), jnp.float32), 'g1': jnp.ones((D,), jnp.float32), 'be1': jnp.zeros((D,), jnp.float32), 'g2': jnp.ones((D,), jnp.float32), 'be2': jnp.zeros((D,), jnp.float32), 'Wg': s(ks[3], (E, D), D), 'W1': s(ks[4], (E, D, DF), D), 'b1': jnp.zeros((E, DF), jnp.float32), 'W2': s(ks[5], (E, DF, D), DF), 'b2': jnp.zeros((E, D), jnp.float32)}
    _L1_ffn_all = _L1_ffn_setup()
    _L1_ffn_in = {k: v for k, v in _L1_ffn_all.items() if k in ('Wqkv', 'bqkv', 'Wo', 'bo', 'g1', 'be1', 'g2', 'be2', 'Wg', 'W1', 'b1', 'W2', 'b2')}
    del _L1_ffn_all
    return {'x': x, 'ctx_1024': ctx_1024, 'mask_Bx1x1xS2_bk0': mask_Bx1x1xS2_bk0, 'L0_xattn_Wq': _L0_xattn_in['Wq'], 'L0_xattn_bq': _L0_xattn_in['bq'], 'L0_xattn_Wk': _L0_xattn_in['Wk'], 'L0_xattn_bk': _L0_xattn_in['bk'], 'L0_xattn_Wv': _L0_xattn_in['Wv'], 'L0_xattn_bv': _L0_xattn_in['bv'], 'L0_ffn_Wr': _L0_ffn_in['Wr'], 'L0_ffn_Wg': _L0_ffn_in['Wg'], 'L0_ffn_Wu': _L0_ffn_in['Wu'], 'L0_ffn_Wd': _L0_ffn_in['Wd'], 'L0_ffn_Sg': _L0_ffn_in['Sg'], 'L0_ffn_Su': _L0_ffn_in['Su'], 'L0_ffn_Sd': _L0_ffn_in['Sd'], 'L1_xattn_Wq': _L1_xattn_in['Wq'], 'L1_xattn_bq': _L1_xattn_in['bq'], 'L1_xattn_Wk': _L1_xattn_in['Wk'], 'L1_xattn_bk': _L1_xattn_in['bk'], 'L1_xattn_Wv': _L1_xattn_in['Wv'], 'L1_xattn_bv': _L1_xattn_in['bv'], 'L1_xattn_Wo': _L1_xattn_in['Wo'], 'L1_xattn_bo': _L1_xattn_in['bo'], 'L1_xattn_m_k': _L1_xattn_in['m_k'], 'L1_xattn_m_v': _L1_xattn_in['m_v'], 'L1_ffn_Wqkv': _L1_ffn_in['Wqkv'], 'L1_ffn_bqkv': _L1_ffn_in['bqkv'], 'L1_ffn_Wo': _L1_ffn_in['Wo'], 'L1_ffn_bo': _L1_ffn_in['bo'], 'L1_ffn_g1': _L1_ffn_in['g1'], 'L1_ffn_be1': _L1_ffn_in['be1'], 'L1_ffn_g2': _L1_ffn_in['g2'], 'L1_ffn_be2': _L1_ffn_in['be2'], 'L1_ffn_Wg': _L1_ffn_in['Wg'], 'L1_ffn_W1': _L1_ffn_in['W1'], 'L1_ffn_b1': _L1_ffn_in['b1'], 'L1_ffn_W2': _L1_ffn_in['W2'], 'L1_ffn_b2': _L1_ffn_in['b2']}

def reference(x, ctx_1024, mask_Bx1x1xS2_bk0, L0_xattn_Wq, L0_xattn_bq, L0_xattn_Wk, L0_xattn_bk, L0_xattn_Wv, L0_xattn_bv, L0_ffn_Wr, L0_ffn_Wg, L0_ffn_Wu, L0_ffn_Wd, L0_ffn_Sg, L0_ffn_Su, L0_ffn_Sd, L1_xattn_Wq, L1_xattn_bq, L1_xattn_Wk, L1_xattn_bk, L1_xattn_Wv, L1_xattn_bv, L1_xattn_Wo, L1_xattn_bo, L1_xattn_m_k, L1_xattn_m_v, L1_ffn_Wqkv, L1_ffn_bqkv, L1_ffn_Wo, L1_ffn_bo, L1_ffn_g1, L1_ffn_be1, L1_ffn_g2, L1_ffn_be2, L1_ffn_Wg, L1_ffn_W1, L1_ffn_b1, L1_ffn_W2, L1_ffn_b2):
    import jax
    import jax.numpy as jnp

    def _L0_xattn_ref(query_input, key_input, value_input, Wq, bq, Wk, bk, Wv, bv):
        import jax, jax.numpy as jnp
        import numpy as np
        B, LQ, LK = (4, 256, 256)
        DQ, DK, DO = (128, 128, 128)
        scale = jnp.asarray(DO, query_input.dtype) ** 0.5
        q = query_input @ Wq + bq
        k = key_input @ Wk + bk
        v = value_input @ Wv + bv
        attn = jnp.einsum('bqd,bkd->bqk', q, k) / scale
        attn = jax.nn.softmax(attn, axis=-1)
        return jnp.einsum('bqk,bkd->bqd', attn, v)

    def _L0_ffn_ref(x, Wr, Wg, Wu, Wd, Sg, Su, Sd):
        import jax, jax.numpy as jnp
        import numpy as np
        D = 128
        F = 128
        E = 8
        K = 2
        B, T, Dm = x.shape
        xf = x.reshape(-1, Dm)
        scores = jax.nn.softmax(xf @ Wr.T, axis=-1)
        top_s, top_i = jax.lax.top_k(scores, K)
        top_s = top_s / (top_s.sum(-1, keepdims=True) + 1e-08)
        combine = (jax.nn.one_hot(top_i, E, dtype=x.dtype) * top_s[..., None]).sum(1)
        gate = jnp.einsum('nd,efd->nef', xf, Wg)
        up = jnp.einsum('nd,efd->nef', xf, Wu)
        h = jax.nn.silu(gate) * up * combine[:, :, None]
        out = jnp.einsum('nef,edf->nd', h, Wd)
        shared = jax.nn.silu(xf @ Sg.T) * (xf @ Su.T) @ Sd.T
        return (out + shared).reshape(B, T, Dm)

    def _L1_xattn_ref(q, k, v, attention_mask, Wq, bq, Wk, bk, Wv, bv, Wo, bo, m_k, m_v):
        import jax, jax.numpy as jnp
        import numpy as np
        D_MODEL = 128
        N_HEADS = 16
        N_MEM = 64
        D_K = D_MODEL // N_HEADS
        B, Nq, D = q.shape
        nk = k.shape[1]
        H, dk, M = (N_HEADS, D_K, N_MEM)
        qh = (q @ Wq.T + bq).reshape(B, Nq, H, dk).transpose(0, 2, 1, 3)
        k_proj = k @ Wk.T + bk
        v_proj = v @ Wv.T + bv
        mk = jnp.broadcast_to(m_k * np.sqrt(dk), (B, M, D))
        mv = jnp.broadcast_to(m_v * np.sqrt(M), (B, M, D))
        kk = jnp.concatenate([k_proj, mk], axis=1)
        vv = jnp.concatenate([v_proj, mv], axis=1)
        kh = kk.reshape(B, nk + M, H, dk).transpose(0, 2, 1, 3)
        vh = vv.reshape(B, nk + M, H, dk).transpose(0, 2, 1, 3)
        scores = jnp.einsum('bhqd,bhkd->bhqk', qh, kh) / np.sqrt(dk)
        pad_mask = jnp.concatenate([jnp.broadcast_to(attention_mask, (B, 1, 1, nk)), jnp.zeros((B, 1, 1, M), bool)], axis=-1)
        scores = jnp.where(pad_mask, -jnp.inf, scores)
        p_attn = jax.nn.softmax(scores, axis=-1)
        out = jnp.einsum('bhqk,bhkd->bhqd', p_attn, vh)
        out = out.transpose(0, 2, 1, 3).reshape(B, Nq, D)
        return out @ Wo.T + bo

    def _L1_ffn_ref(x, Wqkv, bqkv, Wo, bo, g1, be1, g2, be2, Wg, W1, b1, W2, b2):
        import jax, jax.numpy as jnp
        import numpy as np
        D = 128
        H = 4
        DF = 512
        E = 8
        EPS = 1e-05

        def _layer_norm(x, g, b):
            mu = jnp.mean(x, axis=-1, keepdims=True)
            var = jnp.mean(jnp.square(x - mu), axis=-1, keepdims=True)
            return (x - mu) * jax.lax.rsqrt(var + EPS) * g + b

        def _mha(x, Wqkv, bqkv, Wo, bo):
            S, B, _ = x.shape
            hd = D // H
            qkv = x @ Wqkv.T + bqkv
            q, k, v = jnp.split(qkv, 3, axis=-1)
            to_heads = lambda t: t.reshape(S, B, H, hd).transpose(1, 2, 0, 3)
            q, k, v = (to_heads(q), to_heads(k), to_heads(v))
            scores = jnp.einsum('bhqd,bhkd->bhqk', q, k) * (1.0 / np.sqrt(hd))
            att = jax.nn.softmax(scores, axis=-1)
            o = jnp.einsum('bhqk,bhkd->bhqd', att, v)
            o = o.transpose(2, 0, 1, 3).reshape(S, B, D)
            return o @ Wo.T + bo

        def _moe(x, Wg, W1, b1, W2, b2):
            S, B, _ = x.shape
            xf = x.reshape(S * B, D)
            logits = xf @ Wg.T
            idx = jnp.argmax(logits, axis=-1)
            out = jnp.zeros_like(xf)
            for e in range(E):
                m = (idx == e)[:, None].astype(xf.dtype)
                h = jax.nn.relu(xf @ W1[e] + b1[e])
                out = out + m * (h @ W2[e] + b2[e])
            return out.reshape(S, B, D)
        y = _layer_norm(x + _mha(x, Wqkv, bqkv, Wo, bo), g1, be1)
        z = _layer_norm(y + _moe(y, Wg, W1, b1, W2, b2), g2, be2)
        return z
    x = x + _L0_xattn_ref(_layernorm(x, axis=-1), ctx_1024, ctx_1024, L0_xattn_Wq, L0_xattn_bq, L0_xattn_Wk, L0_xattn_bk, L0_xattn_Wv, L0_xattn_bv)
    x = x + _L0_ffn_ref(_layernorm(x, axis=-1), L0_ffn_Wr, L0_ffn_Wg, L0_ffn_Wu, L0_ffn_Wd, L0_ffn_Sg, L0_ffn_Su, L0_ffn_Sd)
    x = x + _L1_xattn_ref(_layernorm(x, axis=-1), ctx_1024, ctx_1024, mask_Bx1x1xS2_bk0, L1_xattn_Wq, L1_xattn_bq, L1_xattn_Wk, L1_xattn_bk, L1_xattn_Wv, L1_xattn_bv, L1_xattn_Wo, L1_xattn_bo, L1_xattn_m_k, L1_xattn_m_v)
    x = x + _L1_ffn_ref(_layernorm(x, axis=-1), L1_ffn_Wqkv, L1_ffn_bqkv, L1_ffn_Wo, L1_ffn_bo, L1_ffn_g1, L1_ffn_be1, L1_ffn_g2, L1_ffn_be2, L1_ffn_Wg, L1_ffn_W1, L1_ffn_b1, L1_ffn_W2, L1_ffn_b2)
    return x

_drawn_inputs = setup_inputs


def setup_inputs(seed=0):
    import zlib

    import numpy as np

    out = dict(_drawn_inputs(seed))
    spreads = {'L1_xattn_bq': (0.0, 0.1),
     'L1_xattn_bk': (0.0, 0.1),
     'L1_xattn_bv': (0.0, 0.1),
     'L1_xattn_bo': (0.0, 0.1),
     'L1_ffn_bqkv': (0.0, 0.1),
     'L1_ffn_bo': (0.0, 0.1),
     'L1_ffn_g1': (1.0, 0.2),
     'L1_ffn_be1': (0.0, 0.1),
     'L1_ffn_g2': (1.0, 0.2),
     'L1_ffn_be2': (0.0, 0.1),
     'L1_ffn_b1': (0.0, 0.271),
     'L1_ffn_b2': (0.0, 0.1)}
    factors = {'L0_xattn_Wq': 3.113,
     'L0_xattn_bq': 8.0,
     'L0_xattn_Wk': 3.499,
     'L0_xattn_bk': 64.0,
     'L1_xattn_m_k': 22.287,
     'L0_ffn_Wr': 2.772,
     'L0_ffn_Wg': 2.834,
     'L0_ffn_Wu': 2.745,
     'L0_ffn_Wd': 3.082}
    for name, (base, spread) in spreads.items():
        noise = np.random.default_rng([zlib.crc32(name.encode()), seed]).standard_normal(out[name].shape)
        drawn = base * np.exp(spread * noise) if base else spread * noise
        out[name] = jnp.asarray(drawn.astype(out[name].dtype))
    for name, factor in factors.items():
        out[name] = (out[name] * factor).astype(out[name].dtype)
    return out
```

```python
from contextlib import ExitStack

import numpy as np
import concourse.bass as bass
from concourse import mybir

ALU = mybir.AluOpType
ACT = mybir.ActivationFunctionType
AX = mybir.AxisListType
F32 = mybir.dt.float32
BF16 = mybir.dt.bfloat16
U8 = mybir.dt.uint8

P = 128
S = 64
B = 64
N = B * S
T = N // P
GT = 4
GW = GT * P
G = T // GT
EPS = 1e-5
H = 16
DK = P // H
M = 64
VW = DK + 1
NEG = -1e30
E = 8

WQ, WK, WV = range(3)
R_BV, R_XBV, R_XBO, R_QKVBV, R_BO, R_G1, R_BE1, R_G2, R_BE2 = range(9)
NROWS = 9
C_BQ, C_BK, C_XBQ, C_XBK, C_MBQ, C_MBK, C_HEAD = range(7)
C_HEAD4 = C_HEAD + 16
NCOLS = C_HEAD4 + 4


def wait(eng, sem, value):
    if isinstance(value, int) and value <= 0:
        return
    eng.wait_ge(sem, value)


def program(nc, x, ctxT, maskrow, wA, wB, wC, memT, mem, wF, w1, w2, b1, b2, rows, cols, out):
    with ExitStack() as ctx:
        def sb(name, shape, dt=F32):
            return ctx.enter_context(nc.sbuf_tensor(name, shape, dt))

        def sem(name):
            return ctx.enter_context(nc.semaphore(name))

        def pair(name):
            return [sem(f"{name}{i}") for i in range(2)]

        bank = ctx.enter_context(nc.psum_tensor("bank", [P, 8, 512], F32))
        X = sb("X", [P, T, P])
        wA_s = sb("wA_s", [P, 3, P])
        rows_s = sb("rows_s", [P, NROWS, P])
        cols_s = sb("cols_s", [P, NCOLS])
        ident = sb("ident", [P, P])
        neghalf = sb("neghalf", [P, GT])
        st = sb("st", [P, 2, GT, 6])
        lsum = sb("lsum", [P, 2, GT, 2])
        ldif = sb("ldif", [P, 2, GT])
        mean = sb("mean", [P, 2, GT])
        ve = sb("ve", [P, 2, GT])
        rstd = sb("rstd", [P, 2, GT])
        xn = sb("xn", [P, 2, GT, P])
        xnT = sb("xnT", [P, 2, GW])
        ctxb = sb("ctxb", [P, 2, GW])

        qT = sb("qT", [P, 2, GW])
        kT = sb("kT", [P, 2, GW])
        vS = sb("vS", [P, 2, GT, P])
        mx = sb("mx", [P, 2, GT])
        ss = sb("ss", [P, 2, GT, S])
        pbd = sb("pbd", [P, 2, GT, P])
        pT = sb("pT", [P, 2, GT, P])
        rs = sb("rs", [P, 2, GT])
        ri = sb("ri", [P, 2, GT])

        NE = E + 1
        big = sb("big", [P, E * 4 * P])
        wB_s = big[:, 0:3 * NE * P + E]
        wgate, wup, wdown = [wB_s[:, i * NE * P:(i + 1) * NE * P].rearrange("p (e f) -> p e f", e=NE)
                             for i in range(3)]
        wrouter = wB_s[:, 3 * NE * P:]
        desc = sb("desc", [P, GT, E])
        le = sb("le", [P, 2, GT, E])
        r8 = [sb(f"r8{i}", [P, GT, E]) for i in range(4)]
        r1 = [sb(f"r1{i}", [P, GT]) for i in range(6)]
        comb = sb("comb", [P, 2, GT, E])
        th = sb("th", [P, 2, GW])
        ga = sb("ga", [P, 2, GW])
        hT = sb("hT", [P, 2, GW])

        wC_s = sb("wC_s", [P, 4, P])
        maskb = sb("maskb", [P, N], U8)
        mrow = sb("mrow", [P, 2, GW], BF16)
        onesb = sb("onesb", [P, P], BF16)
        memT_s = sb("memT_s", [P, M])
        mem_s = sb("mem_s", [P, P])
        NB = GW // S
        arena = sb("arena", [P, 2 * NB * H * S])
        qx = arena[:].rearrange("p (i b c) -> p i b c", i=2, b=NB)
        kk = sb("kk", [P, 2, NB, S + M])
        v1 = sb("v1", [P, 2, NB, H * VW])
        cmx = sb("cmx", [P, 2, 4])
        csub = sb("csub", [P, 2, 4, P])
        cP = sb("cP", [P, 2, 4, P])
        cPT = sb("cPT", [P, 2, GW])
        crv = sb("crv", [P, H])
        cO = ga[:, 0, :]
        Oa = sb("Oa", [P, 2, GT, P])
        cOT = sb("cOT", [P, GW])

        H4, D4 = 4, P // 4
        x3 = nc.dram_tensor("x3", (N, P), F32, kind="Internal").ap()
        x3_t = x3.rearrange("(t p) d -> p t d", p=P)
        wF_s = sb("wF_s", [P, 4 * P + E])
        at = [0]

        def part(shape):
            n = int(np.prod(shape))
            v = arena[:, at[0]:at[0] + n]
            at[0] += n
            names = "abcd"[:len(shape)]
            return v.rearrange(f"p ({' '.join(names)}) -> p {' '.join(names)}", **dict(zip(names, shape)))
        xg = part([2, GT, P])
        dbq = sb("dbq", [P, 4])
        q4 = part([2, H4, GW])
        v4 = sb("v4", [P, 2, GT, H4 * (D4 + 1)])
        dmx = sb("dmx", [P, 2, 8])
        dsub = part([2, 8, S])
        dP = part([16, P])
        drv = sb("drv", [P, 2, 8])
        dOa = sb("dOa", [P, GT, P])
        z = sb("z", [P, GT, P])

        ys = xg
        mT = sb("mT", [P, GW])
        b1_s = sb("b1_s", [P, 4 * E])
        b2_s = sb("b2_s", [P, P])
        w1_s = big
        w2_s = part([E * 4 * P])
        h4 = q4
        yo = vS
        xr = pbd

        w_in = sem("w_in")
        id_zero, id_ready, const_ready = sem("id_zero"), sem("id_ready"), sem("const_ready")
        def sems(prefix, names, **more):
            return {n: sem(f"{prefix}_{n}") for n in names.split()} | more

        wB_in, wC_in = sem("wB_in"), sem("wC_in")
        LN = "bn ln rstd xn tr xnT "
        a = sems("a", LN + "q k v qT kT vS s mx sub exp sum ri ptr pT o xo", x=pair("a_x"), ctx=pair("a_ctx"))
        b = sems("b", LN + "logit lmax lsub lexp route comb gate up tanh act h down acc")
        c = sems("c", LN + "q k v mask qT kT vS s mx sub exp ptr pT pv oc bt rv on otr oT wo xa xo const memrow qx",
                 ctx=pair("c_ctx"))
        d = sems("d", LN + "q k v qT kT vS s mx sub exp ptr pT pv rv on otr oT wo z zb lg normed const bq", x=pair("d_x"))
        dn = sems("dn", LN)
        e = sems("e", LN + "ys logit route mtr mT bias yb up h down acc lg normed y", out=pair("e_out"), x=pair("e_x"))
        x3_out, wF_in = sem("x3_out"), sem("wF_in")

        x_t = x.rearrange("(t p) d -> p t d", p=P)

        def steps(eng, ahead, main):
            for part in ahead:
                part(0, 0, 0)

            def call(g, par, half, half1, last=False):
                def nxt(k):
                    if not last:
                        ahead[k](g + 1, 1 - par, half1)
                main(g, par, half, nxt)
            call(0, 0, 0, 0)
            with eng.Fori(0, (G - 2) // 2) as i:
                call(2 * i + 1, 1, i, i + 1)
                call(2 * i + 2, 0, i + 1, i + 1)
            call(G - 1, 1, (G - 1) // 2, None, last=True)

        def layer_norm_stats(dve, done, g, par):
            even, odd = st[:, par, :, 1:3], st[:, par, :, 4:6]
            nc.vector.tensor_tensor(lsum[:, par], even, odd, ALU.add)
            nc.vector.tensor_tensor(ldif[:, par], even[:, :, 0], odd[:, :, 0], ALU.subtract).then_inc(done, 1)
            dve.wait_ge(done, 4 * g + 1)
            nc.vector.tensor_scalar(mean[:, par], lsum[:, par, :, 0], 0.5, None, ALU.mult)
            nc.vector.tensor_tensor(ldif[:, par], ldif[:, par], ldif[:, par], ALU.mult).then_inc(done, 1)
            dve.wait_ge(done, 4 * g + 2)
            nc.vector.scalar_tensor_tensor(ve[:, par], ldif[:, par], P / 4.0, lsum[:, par, :, 1],
                                           ALU.mult, ALU.add).then_inc(done, 1)
            dve.wait_ge(done, 4 * g + 3)
            nc.vector.tensor_scalar(ve[:, par], ve[:, par], 1.0 / P, EPS, ALU.mult, ALU.add).then_inc(done, 1)

        def layer_norm_rows(dve, n, g, par, src=lambda g, t: X[:, g * GT + t, :]):
            for t in range(GT):
                i = nc.vector.bn_stats(st[:, par, t, :], src(g, t))
            i.then_inc(n["bn"], 1)
            dve.wait_ge(n["bn"], g + 1)
            layer_norm_stats(dve, n["ln"], g, par)
            dve.wait_ge(n["rstd"], g + 1)
            wait(dve, n["tr"], g - 1)
            for t in range(GT):
                i = nc.vector.tensor_scalar(xn[:, par, t, :], src(g, t), mean[:, par, t:t + 1],
                                            rstd[:, par, t:t + 1], ALU.subtract, ALU.mult)
            i.then_inc(n["xn"], 1)

        def layer_norm_affine(dve, n, g, par, src, out_rows, r_gain, r_bias):
            for t in range(GT):
                i = nc.vector.bn_stats(st[:, par, t, :], src(t))
            i.then_inc(n["bn"], 1)
            dve.wait_ge(n["bn"], g + 1)
            layer_norm_stats(dve, n["ln"], g, par)
            dve.wait_ge(n["rstd"], g + 1)
            for t in range(GT):
                i = nc.vector.tensor_scalar(xn[:, par, t, :], src(t), mean[:, par, t:t + 1],
                                            rstd[:, par, t:t + 1], ALU.subtract, ALU.mult)
            i.then_inc(n["xn"], 1)
            dve.wait_ge(n["xn"], g + 1)
            nc.vector.tensor_tensor(xn[:, par], xn[:, par], rows_s[:, r_gain:r_gain + 1, :].to_broadcast([P, GT, P]),
                                    ALU.mult).then_inc(n["lg"], 1)
            dve.wait_ge(n["lg"], g + 1)
            nc.vector.tensor_tensor(out_rows, xn[:, par], rows_s[:, r_bias:r_bias + 1, :].to_broadcast([P, GT, P]),
                                    ALU.add).then_inc(n["normed"], 1)

        def pool_rstd(pool, n, g, par):
            pool.wait_ge(n["ln"], 4 * (g + 1))
            nc.gpsimd.tensor_tensor(rstd[:, par, :], ve[:, par, :], neghalf[:], ALU.pow).then_inc(n["rstd"], 1)

        def transpose_xn(pe, n, g, par):
            for t in range(GT):
                i = nc.tensor.transpose(bank[:, 0, t * P:(t + 1) * P], xn[:, par, t, :], ident[:])
            i.then_inc(n["tr"], 1)

        block = ctx.enter_context(nc.Block())

        @block.sync
        def _(sp):
            sp.dma_start(wA_s[:], wA).then_inc(w_in, 16)
            sp.dma_start(rows_s[:], rows).then_inc(w_in, 16)
            sp.dma_start(cols_s[:], cols).then_inc(w_in, 16)

            def a_load(g, par, half):
                wait(sp, a["v"], g - 1)
                wait(sp, a["xn"], g - 1)
                sp.dma_start(X[:, bass.ds(g * GT, GT), :], x_t[:, bass.ds(g * GT, GT), :]).then_inc(a["x"][par], 16)
                sp.dma_start(ctxb[:, par, :], ctxT[:, bass.ds(g * GW, GW)]).then_inc(a["ctx"][par], 16)
            steps(sp, [a_load], lambda g, par, half, nxt: nxt(0))
            sp.dma_start(wB_s[:], wB).then_inc(wB_in, 16)
            sp.dma_start(wC_s[:], wC.rearrange("p (i d) -> p i d", i=4)).then_inc(wC_in, 16)
            sp.dma_start(memT_s[:], memT).then_inc(wC_in, 16)
            sp.dma_start(mem_s[M:P, :], mem).then_inc(wC_in, 16)
            sp.dma_start(maskb[:], bass.AP(maskrow.tensor, 0, [[0, P], [1, N]])).then_inc(wC_in, 16)
            sp.wait_ge(a["o"], G)

            def c_load(g, par, half):
                wait(sp, c["v"], 2 * g - 2)
                sp.dma_start(ctxb[:, par, :], ctxT[:, bass.ds(g * GW, GW)]).then_inc(c["ctx"][par], 16)
            def c_store(g, par, half, nxt):
                nxt(0)
                sp.wait_ge(c["xo"], g + 1)
                sp.dma_start(x3_t[:, bass.ds(g * GT, GT), :], X[:, bass.ds(g * GT, GT), :]).then_inc(x3_out, 16)
            steps(sp, [c_load], c_store)
            sp.dma_start(wF_s[:], wF).then_inc(wF_in, 16)
            sp.dma_start(b1_s[:], b1).then_inc(wF_in, 16)
            sp.dma_start(b2_s[0:E, :], b2).then_inc(wF_in, 16)
            sp.dma_start(w1_s[:], w1).then_inc(wF_in, 16)
            sp.dma_start(w2_s[:], w2).then_inc(wF_in, 16)

            sp.wait_ge(x3_out, 16 * G)

            def rows_of(dram, g, n):
                return dram.rearrange("(b g t n) d -> n b g t d", b=B, g=G, n=2)[n][:, bass.ds(g, 1)].rearrange(
                    "b g t d -> b (g t) d")

            def d_load(g, par, half):
                wait(sp, d["z"], g - 1)
                for n in range(2):
                    sp.dma_start(xg[n * S:(n + 1) * S, par], rows_of(x3, g, n)).then_inc(d["x"][par], 16)
            steps(sp, [d_load], lambda g, par, half, nxt: nxt(0))

            def e_store(g, par, half, nxt):
                nxt(0)
                sp.wait_ge(e["y"], g + 1)
                for n in range(2):
                    sp.dma_start(rows_of(out, g, n), yo[n * S:(n + 1) * S, par]).then_inc(e["out"][par], 16)

            def e_load(g, par, half):
                wait(sp, e["y"], g - 1)
                for n in range(2):
                    sp.dma_start(xr[n * S:(n + 1) * S, par], rows_of(x3, g, n)).then_inc(e["x"][par], 16)
            steps(sp, [e_load], e_store)
            for par in range(2):
                sp.wait_ge(e["out"][par], 16 * G)

        @block.gpsimd
        def _(pool):
            nc.gpsimd.memset(ident[:], 0.0).then_inc(id_zero, 1)
            pool.wait_ge(id_zero, 1)
            nc.gpsimd.affine_select(out=ident[:], in_=ident[:], compare_op=ALU.not_equal, fill=1.0, base=0,
                                    pattern=[[-1, P]], channel_multiplier=1).then_inc(id_ready, 1)
            nc.gpsimd.memset(neghalf[:], -0.5).then_inc(const_ready, 1)
            nc.gpsimd.memset(pbd[:], 0.0).then_inc(const_ready, 1)
            for k in range(E):
                i = nc.gpsimd.memset(desc[:, :, k:k + 1], float(E - k))
            i.then_inc(const_ready, 1)
            nc.gpsimd.memset(onesb[:], 1.0)
            nc.gpsimd.memset(v1[:], 1.0).then_inc(c["const"], 1)
            nc.gpsimd.memset(v4[:], 1.0).then_inc(d["const"], 1)
            pool.wait_ge(const_ready, 3)
            for n in (a, b, c):
                steps(pool, [lambda g, par, half: pool_rstd(pool, n, g, par)], lambda g, par, half, nxt: nxt(0))
            
            pool.wait_ge(c["s"], 16 * G)
            nc.gpsimd.memset(dP[:], 0.0).then_inc(d["const"], 1)

            def d_rstd(g, par, half, nxt):
                nxt(0)
                pool_rstd(pool, d, g, par)
            steps(pool, [lambda g, par, half: pool_rstd(pool, dn, g, par)], d_rstd)

            def e_copy(g, par, half):
                pool.wait_ge(d["normed"], g + 1)
                wait(pool, e["tr"], g - 1)
                nc.gpsimd.tensor_copy(ys[:, par], X[:, bass.ds(g * GT, GT), :]).then_inc(e["ys"], 1)

            def e_rstd(g, par, half, nxt):
                nxt(0)
                pool_rstd(pool, e, g, par)
            steps(pool, [e_copy], e_rstd)

        @block.vector
        def _(dve):
            def a_norm(g, par, half):
                dve.wait_ge(a["x"][par], 16 * (half + 1))
                layer_norm_rows(dve, a, g, par)

            def a_value(g, par, half):
                dve.wait_ge(a["v"], g + 1)
                wait(dve, a["o"], g - 1)
                nc.vector.tensor_tensor(vS[:, par], bank[:, 3, :].rearrange("p (t d) -> p t d", t=GT),
                                        rows_s[:, R_BV:R_BV + 1, :].to_broadcast([P, GT, P]), ALU.add).then_inc(a["vS"], 1)

            def a_main(g, par, half, nxt):
                dve.wait_ge(a["s"], g + 1)
                s = bank[:, 4, 0:GT * S].rearrange("p (t k) -> p t k", t=GT)
                nc.vector.tensor_reduce(mx[:, par, :], s, AX.X, ALU.max).then_inc(a["mx"], 1)
                dve.wait_ge(a["mx"], g + 1)
                wait(dve, a["exp"], g - 1)
                nc.vector.tensor_tensor(ss[:, par], s, mx[:, par, :].unsqueeze(2).to_broadcast([P, GT, S]),
                                        ALU.subtract).then_inc(a["sub"], 1)
                nxt(0)
                dve.wait_ge(a["exp"], g + 1)
                nc.vector.tensor_reduce(rs[:, par, :], pbd[:, par], AX.X, ALU.add).then_inc(a["sum"], 1)
                dve.wait_ge(a["sum"], g + 1)
                nc.vector.reciprocal(ri[:, par, :], rs[:, par, :]).then_inc(a["ri"], 1)
                nxt(1)
                dve.wait_ge(a["ri"], g + 1)
                dve.wait_ge(a["o"], g + 1)
                for t in range(GT):
                    xt = X[:, g * GT + t, :]
                    i = nc.vector.scalar_tensor_tensor(xt, bank[:, 6, t * P:(t + 1) * P], ri[:, par, t:t + 1], xt,
                                                       ALU.mult, ALU.add)
                i.then_inc(a["xo"], 1)
            dve.wait_ge(w_in, 16 * 3)
            steps(dve, [a_norm, a_value], a_main)

            def b_norm(g, par, half):
                dve.wait_ge(a["xo"], g + 1)
                layer_norm_rows(dve, b, g, par)

            def b_logits(g, par, half):
                lg = bank[:, 1, 0:GT * E].rearrange("p (t e) -> p t e", t=GT)
                dve.wait_ge(b["logit"], g + 1)
                nc.vector.tensor_reduce(r1[0][:], lg, AX.X, ALU.max).then_inc(b["lmax"], 1)
                dve.wait_ge(b["lmax"], g + 1)
                nc.vector.tensor_tensor(le[:, par], lg, r1[0][:].unsqueeze(2).to_broadcast([P, GT, E]),
                                        ALU.subtract).then_inc(b["lsub"], 1)

            ROUTE = 13

            def b_route(g, par, half):
                step = [0]

                def then(i):
                    step[0] += 1
                    i.then_inc(b["route"], 1)
                    dve.wait_ge(b["route"], ROUTE * g + step[0])

                def spread(v):
                    return v[:].unsqueeze(2).to_broadcast([P, GT, E])
                e8 = le[:, par]
                key, one1, rest, one2 = [v[:] for v in r8]
                total, m1, m2, k, den, r = r1
                dve.wait_ge(b["lexp"], g + 1)
                nc.vector.tensor_reduce(total[:], e8, AX.X, ALU.add)
                then(nc.vector.tensor_reduce(m1[:], e8, AX.X, ALU.max))
                then(nc.vector.tensor_tensor(key, e8, spread(m1), ALU.is_equal))
                then(nc.vector.tensor_tensor(key, key, desc[:], ALU.mult))
                then(nc.vector.tensor_reduce(k[:], key, AX.X, ALU.max))
                then(nc.vector.tensor_tensor(one1, key, spread(k), ALU.is_equal))
                then(nc.vector.scalar_tensor_tensor(rest, one1, -2.0, e8, ALU.mult, ALU.add))
                then(nc.vector.tensor_reduce(m2[:], rest, AX.X, ALU.max))
                nc.vector.tensor_tensor(den[:], m1[:], m2[:], ALU.add)
                then(nc.vector.tensor_tensor(key, rest, spread(m2), ALU.is_equal))
                nc.vector.scalar_tensor_tensor(den[:], total[:], 1e-8, den[:], ALU.mult, ALU.add)
                then(nc.vector.tensor_tensor(key, key, desc[:], ALU.mult))
                nc.vector.reciprocal(r[:], den[:])
                then(nc.vector.tensor_reduce(k[:], key, AX.X, ALU.max))
                then(nc.vector.tensor_tensor(one2, key, spread(k), ALU.is_equal))
                then(nc.vector.tensor_tensor(one2, one2, one1, ALU.add))
                wait(dve, b["acc"], NE * (g - 1))
                nc.vector.scalar_tensor_tensor(rest, one2, 0.5, e8, ALU.mult, ALU.mult).then_inc(b["route"], 1)
                dve.wait_ge(b["route"], ROUTE * g + ROUTE)
                nc.vector.tensor_tensor(comb[:, par], rest, spread(r), ALU.mult).then_inc(b["comb"], 1)

            def b_main(g, par, half, nxt):
                def accumulate(u):
                    w, pu = NE * g + u, (par + u) % 2
                    dve.wait_ge(b["down"], w + 1)
                    wait(dve, b["acc"], w)
                    if u == 0:
                        dve.wait_ge(b["comb"], g + 1)
                    if u == E:
                        xt = X[:, bass.ds(g * GT, GT), :] if not isinstance(g, int) else X[:, g * GT:(g + 1) * GT, :]
                        o = bank[:, 6 + pu, :].rearrange("p (t d) -> p t d", t=GT)
                        nc.vector.scalar_tensor_tensor(xt, o, 0.5, xt, ALU.mult, ALU.add).then_inc(b["acc"], 1)
                        return
                    for t in range(GT):
                        xt = X[:, g * GT + t, :]
                        i = nc.vector.scalar_tensor_tensor(xt, bank[:, 6 + pu, t * P:(t + 1) * P],
                                                           comb[:, par, t, u:u + 1], xt, ALU.mult, ALU.add)
                    i.then_inc(b["acc"], 1)

                for u in range(NE):
                    w, pu = NE * g + u, (par + u) % 2
                    dve.wait_ge(b["tanh"], w + 1)
                    nc.vector.scalar_tensor_tensor(ga[:, pu, :], th[:, pu, :], 1.0, bank[:, 2 + pu, :],
                                                   ALU.add, ALU.mult).then_inc(b["act"], 1)
                    dve.wait_ge(b["act"], w + 1)
                    dve.wait_ge(b["up"], w + 1)
                    wait(dve, b["down"], w - 1)
                    nc.vector.tensor_tensor(hT[:, pu, :], ga[:, pu, :], bank[:, 4 + pu, :], ALU.mult).then_inc(b["h"], 1)
                    if u:
                        accumulate(u - 1)
                    if u == 1:
                        nxt(0)
                    if u == 5:
                        nxt(1)
                    if u == 6:
                        nxt(2)
                accumulate(E)
            dve.wait_ge(const_ready, 3)
            steps(dve, [b_norm, b_logits, b_route], b_main)

            dve.wait_ge(wC_in, 16 * 4)
            dve.wait_ge(c["const"], 1)
            for par in range(2):
                nc.vector.tensor_scalar(kk[:, par, :, S:], memT_s[:].unsqueeze(1).to_broadcast([P, NB, M]),
                                        DK ** 0.5, None, ALU.mult)
                v = v1[M:P, par].rearrange("p b (h d) -> p b h d", h=H)
                for n in range(NB):
                    nc.vector.tensor_scalar(v[:, n, :, 0:DK], mem_s[M:P, :].rearrange("p (h d) -> p h d", h=H),
                                            M ** 0.5, None, ALU.mult)
            dve.wait_ge(b["acc"], NE * G)
            nc.vector.memset(bank[:, 7, :], 0.0).then_inc(c["memrow"], 1)

            def c_norm(g, par, half):
                dve.wait_ge(b["acc"], NE * (g + 1))
                layer_norm_rows(dve, c, g, par)
                wait(dve, c["s"], 16 * (g - 1))
                nc.vector.tensor_scalar(mrow[:, par, :], maskb[:, bass.ds(g * GW, GW)], NEG, None,
                                        ALU.mult).then_inc(c["mask"], 1)

            def c_heads(k):
                def part(g, par, half):
                    dve.wait_ge(c["qT"], g + 1)
                    wait(dve, c["s"], 16 * (g - 1))
                    for h in range(8 * k, 8 * k + 8):
                        i = nc.vector.tensor_scalar(qx[:, par, :, h * S:(h + 1) * S],
                                                    qT[:, par, :].rearrange("p (b s) -> p b s", b=NB),
                                                    cols_s[:, C_HEAD + h:C_HEAD + h + 1], None, ALU.mult)
                    if k:
                        i.then_inc(c["qx"], 1)
                return part

            def c_value(k):
                def part(g, par, half):
                    dve.wait_ge(c["v"], 2 * g + k + 1)
                    wait(dve, c["pv"], 16 * (g - 1))
                    nb = NB // 2
                    v = v1[0:S, par, k * nb:(k + 1) * nb, :].rearrange("p b (h d) -> p b h d", h=H)
                    bias = rows_s[0:S, R_XBV, :].rearrange("p (h d) -> p h d", h=H).unsqueeze(1)
                    for n in range(nb):
                        i = nc.vector.tensor_tensor(
                            v[:, n, :, 0:DK], bank[0:S, 0, n * P:(n + 1) * P].rearrange("p (h d) -> p h d", h=H),
                            rows_s[0:S, R_XBV, :].rearrange("p (h d) -> p h d", h=H), ALU.add)
                    i.then_inc(c["vS"], 1)
                return part

            def c_normalize(g, par, t):
                n = 4 * g + t
                o = bank[:, 6, :].rearrange("p (h d) -> p h d", h=H)
                dve.wait_ge(c["bt"], n + 1)
                nc.vector.reciprocal(crv[:], o[:, :, DK]).then_inc(c["rv"], 1)
                dve.wait_ge(c["rv"], n + 1)
                if t == 0:
                    wait(dve, c["otr"], g - 1)
                nc.vector.tensor_tensor(Oa[:, par, t, :].rearrange("p (h d) -> p h d", h=H), o[:, :, 0:DK],
                                        crv[:].unsqueeze(2).to_broadcast([P, H, DK]), ALU.mult).then_inc(c["on"], 1)

            def c_update(g):
                xt = X[:, bass.ds(g * GT, GT), :]
                dve.wait_ge(c["wo"], g + 1)
                nc.vector.tensor_tensor(xt, xt, bank[:, 0, :].rearrange("p (t d) -> p t d", t=GT),
                                        ALU.add).then_inc(c["xa"], 1)
                dve.wait_ge(c["xa"], g + 1)
                nc.vector.tensor_tensor(xt, xt, rows_s[:, R_XBO:R_XBO + 1, :].to_broadcast([P, GT, P]),
                                        ALU.add).then_inc(c["xo"], 1)

            def c_main(g, par, half, nxt):
                first = isinstance(g, int) and g == 0
                for j in range(16):
                    w, r = 16 * g + j, j % 4
                    s = bank[:, 2 + r, :].rearrange("p (u k) -> p u k", u=4)
                    dve.wait_ge(c["s"], w + 1)
                    nc.vector.tensor_reduce(cmx[:, j % 2, :], s, AX.X, ALU.max).then_inc(c["mx"], 1)
                    dve.wait_ge(c["mx"], w + 1)
                    wait(dve, c["exp"], w - 1)
                    nc.vector.tensor_tensor(csub[:, j % 2], s, cmx[:, j % 2, :].unsqueeze(2).to_broadcast([P, 4, P]),
                                            ALU.subtract).then_inc(c["sub"], 1)
                    if j == 2 and not first:
                        c_normalize(g - 1, 1 - par, 3)
                    if j == 3:
                        nxt(0)
                    if j == 5 and not first:
                        c_update(g - 1)
                    if j in (6, 10, 14):
                        c_normalize(g, par, j // 4 - 1)
                    if j == 8:
                        nxt(1)
                    if j == 9:
                        nxt(2)
                    if j == 12:
                        nxt(3)
                    if j == 13:
                        nxt(4)
            steps(dve, [c_norm, c_heads(0), c_heads(1), c_value(0), c_value(1)], c_main)
            c_normalize(G - 1, 1, 3)
            c_update(G - 1)

            dve.wait_ge(d["const"], 2)

            def d_norm(g, par, half):
                dve.wait_ge(d["x"][par], 32 * (half + 1))
                wait(dve, d["normed"], g - 1)
                layer_norm_rows(dve, dn, g, par, lambda g, t: xg[:, par, t, :])

            def d_value(g, par, half):
                dve.wait_ge(d["v"], g + 1)
                wait(dve, d["pv"], 4 * (g - 1))
                bias = rows_s[:, R_QKVBV, :].rearrange("p (h d) -> p h d", h=H4)
                for t in range(GT):
                    i = nc.vector.tensor_tensor(
                        v4[:, par, t, :].rearrange("p (h d) -> p h d", h=H4)[:, :, 0:D4],
                        bank[:, 1, t * P:(t + 1) * P].rearrange("p (h d) -> p h d", h=H4), bias, ALU.add)
                i.then_inc(d["vS"], 1)

            def d_main(g, par, half, nxt):
                for m in range(2):
                    s = bank[:, 4 + m, :].rearrange("p (u k) -> p u k", k=S)
                    dve.wait_ge(d["s"], 2 * g + m + 1)
                    nc.vector.tensor_reduce(dmx[:, m, :], s, AX.X, ALU.max).then_inc(d["mx"], 1)
                    dve.wait_ge(d["mx"], 2 * g + m + 1)
                    wait(dve, d["exp"], 2 * g + m - 1)
                    nc.vector.tensor_tensor(dsub[:, m], s, dmx[:, m, :].unsqueeze(2).to_broadcast([P, 8, S]),
                                            ALU.subtract).then_inc(d["sub"], 1)
                nxt(0)
                for m in range(2):
                    o = bank[:, 2 + m, 0:8 * (D4 + 1)].rearrange("p (h t d) -> p h t d", h=2, t=GT)
                    dve.wait_ge(d["pv"], 4 * g + 2 * m + 2)
                    nc.vector.reciprocal(drv[:, m].rearrange("p (h t) -> p h t", h=2), o[:, :, :, D4]).then_inc(d["rv"], 1)
                    dve.wait_ge(d["rv"], 2 * g + m + 1)
                    wait(dve, d["otr"], g)
                    for h in range(2):
                        i = nc.vector.tensor_tensor(
                            dOa[:, :, (2 * m + h) * D4:(2 * m + h + 1) * D4], o[:, h, :, 0:D4],
                            drv[:, m, h * GT:(h + 1) * GT].unsqueeze(2).to_broadcast([P, GT, D4]), ALU.mult)
                    i.then_inc(d["on"], 1)
                dve.wait_ge(d["wo"], g + 1)
                nc.vector.tensor_tensor(z[:], xn[:, par], bank[:, 3, :].rearrange("p (t d) -> p t d", t=GT),
                                        ALU.add).then_inc(d["z"], 1)
                dve.wait_ge(d["z"], g + 1)
                nc.vector.tensor_tensor(z[:], z[:], rows_s[:, R_BO:R_BO + 1, :].to_broadcast([P, GT, P]),
                                        ALU.add).then_inc(d["zb"], 1)
                dve.wait_ge(d["zb"], g + 1)
                layer_norm_affine(dve, d, g, par, lambda t: z[:, t, :], X[:, bass.ds(g * GT, GT), :], R_G1, R_BE1)
                nxt(1)
            steps(dve, [d_norm, d_value], d_main)

            def e_logits(g, par, half):
                lg = bank[:, 1, 0:GT * E].rearrange("p (t e) -> p t e", t=GT)
                key = r8[0][:]
                dve.wait_ge(e["logit"], g + 1)
                wait(dve, e["acc"], E * (g - 1))
                nc.vector.tensor_reduce(r1[0][:], lg, AX.X, ALU.max).then_inc(e["route"], 1)
                dve.wait_ge(e["route"], 5 * g + 1)
                nc.vector.tensor_tensor(key, lg, r1[0][:].unsqueeze(2).to_broadcast([P, GT, E]),
                                        ALU.is_equal).then_inc(e["route"], 1)
                dve.wait_ge(e["route"], 5 * g + 2)
                nc.vector.tensor_tensor(key, key, desc[:], ALU.mult).then_inc(e["route"], 1)
                dve.wait_ge(e["route"], 5 * g + 3)
                nc.vector.tensor_reduce(r1[1][:], key, AX.X, ALU.max).then_inc(e["route"], 1)
                dve.wait_ge(e["route"], 5 * g + 4)
                nc.vector.tensor_tensor(le[:, par], key, r1[1][:].unsqueeze(2).to_broadcast([P, GT, E]),
                                        ALU.is_equal).then_inc(e["route"], 1)

            def e_bias(g, par, half):
                y = X[:, bass.ds(g * GT, GT), :]
                dve.wait_ge(e["bias"], g + 1)
                dve.wait_ge(e["ys"], g + 1)
                nc.vector.tensor_tensor(y, y, bank[:, 7, :].rearrange("p (t d) -> p t d", t=GT),
                                        ALU.add).then_inc(e["yb"], 1)

            def e_main(g, par, half, nxt):
                for u in range(E):
                    w = E * g + u
                    if u == 0:
                        dve.wait_ge(e["yb"], g + 1)
                    dve.wait_ge(e["down"], w + 1)
                    wait(dve, e["acc"], w)
                    for t in range(GT):
                        xt = X[:, g * GT + t, :]
                        i = nc.vector.scalar_tensor_tensor(z[:, t, :] if u == E - 1 else xt,
                                                           bank[:, 4 + u % 2, t * P:(t + 1) * P],
                                                           le[:, par, t, u:u + 1], xt, ALU.mult, ALU.add)
                    i.then_inc(e["acc"], 1)
                    if u == 2:
                        nxt(0)
                    if u == 3:
                        nxt(1)
                dve.wait_ge(e["acc"], E * g + E)
                wait(dve, e["out"][par], 32 * half)
                layer_norm_affine(dve, e, g, par, lambda t: z[:, t, :], xn[:, par], R_G2, R_BE2)
                dve.wait_ge(e["normed"], g + 1)
                dve.wait_ge(e["x"][par], 32 * (half + 1))
                nc.vector.tensor_tensor(yo[:, par], xn[:, par], xr[:, par], ALU.add).then_inc(e["y"], 1)
            steps(dve, [e_logits, e_bias], e_main)

        @block.scalar
        def _(act):
            def a_xT(g, par, half):
                act.wait_ge(a["tr"], g + 1)
                wait(act, a["q"], g - 1)
                nc.scalar.copy(xnT[:, par, :], bank[:, 0, :]).then_inc(a["xnT"], 1)
                act.wait_ge(a["k"], g + 1)
                nc.scalar.activation(kT[:, par, :], bank[:, 2, :], ACT.Identity,
                                     bias=cols_s[:, C_BK:C_BK + 1]).then_inc(a["kT"], 1)

            def a_qT(g, par, half):
                act.wait_ge(a["q"], g + 1)
                nc.scalar.activation(qT[:, par, :], bank[:, 1, :], ACT.Identity,
                                     bias=cols_s[:, C_BQ:C_BQ + 1]).then_inc(a["qT"], 1)

            def a_main(g, par, half, nxt):
                act.wait_ge(a["sub"], g + 1)
                for n in range(2):
                    h = slice(n * S, (n + 1) * S)
                    i = nc.scalar.activation(pbd[h, par, :, n * S:(n + 1) * S], ss[h, par], ACT.Exp, scale=P ** -0.5)
                i.then_inc(a["exp"], 1)
                nxt(0)
                act.wait_ge(a["ptr"], g + 1)
                wait(act, a["o"], g - 1)
                nc.scalar.copy(pT[:, par].rearrange("p t k -> p (t k)"), bank[:, 5, :]).then_inc(a["pT"], 1)
                nxt(1)
            act.wait_ge(w_in, 16 * 3)
            act.wait_ge(const_ready, 2)
            steps(act, [a_xT, a_qT], a_main)

            def b_xT(g, par, half):
                act.wait_ge(b["tr"], g + 1)
                wait(act, b["up"], NE * (g - 1))
                nc.scalar.copy(xnT[:, par, :], bank[:, 0, :]).then_inc(b["xnT"], 1)

            def b_exp(g, par, half):
                act.wait_ge(b["lsub"], g + 1)
                nc.scalar.activation(le[:, par], le[:, par], ACT.Exp).then_inc(b["lexp"], 1)

            def b_main(g, par, half, nxt):
                for u in range(NE):
                    w, pu = NE * g + u, (par + u) % 2
                    act.wait_ge(b["gate"], w + 1)
                    wait(act, b["act"], w - 1)
                    nc.scalar.activation(th[:, pu, :], bank[:, 2 + pu, :], ACT.Tanh, scale=0.5).then_inc(b["tanh"], 1)
                    if u == 4:
                        nxt(0)
                    if u == 6:
                        nxt(1)
            steps(act, [b_xT, b_exp], b_main)

            act.wait_ge(c["memrow"], 1)

            def c_xT(g, par, half):
                act.wait_ge(c["tr"], g + 1)
                wait(act, c["q"], g - 1)
                nc.scalar.copy(xnT[:, par, :], bank[:, 0, :]).then_inc(c["xnT"], 1)

            def c_qT(g, par, half):
                act.wait_ge(c["q"], g + 1)
                wait(act, c["qx"], g - 1)
                nc.scalar.activation(qT[:, par, :], bank[:, 0, :], ACT.Identity,
                                     bias=cols_s[:, C_XBQ:C_XBQ + 1]).then_inc(c["qT"], 1)

            def c_kT(g, par, half):
                act.wait_ge(c["k"], g + 1)
                nc.scalar.activation(kk[:, par, :, 0:S], bank[:, 0, :].rearrange("p (b s) -> p b s", b=NB),
                                     ACT.Identity, bias=cols_s[:, C_XBK:C_XBK + 1]).then_inc(c["kT"], 1)

            def c_turned(w, j):
                act.wait_ge(c["ptr"], w + 1)
                wait(act, c["pv"], w - 1)
                nc.scalar.copy(cPT[:, j % 2, :], bank[:, 1 if j % 2 else 6, :]).then_inc(c["pT"], 1)

            def c_outputs(n):
                act.wait_ge(c["pv"], 4 * n + 4)
                wait(act, c["bt"], n)
                nc.scalar.copy(cO, bank[:, 7, :]).then_inc(c["oc"], 1)

            def c_oT(g):
                act.wait_ge(c["otr"], g + 1)
                wait(act, c["wo"], g)
                nc.scalar.copy(cOT[:], bank[:, 6, :]).then_inc(c["oT"], 1)

            def c_main(g, par, half, nxt):
                first = isinstance(g, int) and g == 0
                for j in range(16):
                    w = 16 * g + j
                    if j % 4 == 1 and not (first and j == 1):
                        c_outputs(4 * g + j // 4 - 1)
                    act.wait_ge(c["sub"], w + 1)
                    wait(act, c["ptr"], w - 1)
                    nc.scalar.activation(cP[:, j % 2], csub[:, j % 2], ACT.Exp, scale=DK ** -0.5).then_inc(c["exp"], 1)
                    if j or not first:
                        c_turned(w - 1, (j - 1) % 16)
                    if j == 3 and not first:
                        c_oT(g - 1)
                    if j == 6:
                        nxt(0)
                    if j == 8:
                        nxt(1)
                    if j == 10:
                        nxt(2)
            steps(act, [c_xT, c_qT, c_kT], c_main)
            c_turned(16 * G - 1, 15)
            c_outputs(4 * G - 1)
            c_oT(G - 1)

            act.wait_ge(wF_in, 16 * 5)
            act.wait_ge(d["const"], 2)

            def d_xT(g, par, half):
                act.wait_ge(dn["tr"], g + 1)
                wait(act, d["v"], g - 1)
                nc.scalar.copy(xnT[:, par, :], bank[:, 0, :]).then_inc(d["xnT"], 1)

            def d_qT(g, par, half):
                act.wait_ge(d["q"], g + 1)
                wait(act, d["s"], 2 * (g - 1))
                for h in range(H4):
                    i = nc.scalar.activation(q4[:, par, h, :], bank[:, 1, :], ACT.Identity, bias=dbq[:, h:h + 1],
                                             scale=cols_s[:, C_HEAD4 + h:C_HEAD4 + h + 1])
                i.then_inc(d["qT"], 1)
                act.wait_ge(d["k"], g + 1)
                nc.scalar.activation(kT[:, par, :], bank[:, 0, :], ACT.Identity,
                                     bias=cols_s[:, C_MBK:C_MBK + 1]).then_inc(d["kT"], 1)

            def d_main(g, par, half, nxt):
                for m in range(2):
                    act.wait_ge(d["sub"], 2 * g + m + 1)
                    wait(act, d["ptr"], 4 * (g - 1) + 2 * m + 2)
                    for n in range(2):
                        h = slice(n * S, (n + 1) * S)
                        i = nc.scalar.activation(dP[h, 8 * m:8 * m + 8, n * S:(n + 1) * S], dsub[h, m], ACT.Exp,
                                                 scale=D4 ** -0.5)
                    i.then_inc(d["exp"], 1)
                for h in range(H4):
                    w = 4 * g + h
                    act.wait_ge(d["ptr"], w + 1)
                    wait(act, d["pv"], w - 1)
                    nc.scalar.copy(cPT[:, h % 2, :], bank[:, 6 + h % 2, :]).then_inc(d["pT"], 1)
                    if h == 1:
                        nxt(0)
                act.wait_ge(d["otr"], g + 1)
                wait(act, d["wo"], g)
                nc.scalar.copy(cOT[:], bank[:, 2, :]).then_inc(d["oT"], 1)
                nxt(1)
            nc.scalar.activation(dbq[:], cols_s[:, C_HEAD4:C_HEAD4 + 4], ACT.Copy,
                                 scale=cols_s[:, C_MBQ:C_MBQ + 1]).then_inc(d["bq"], 1)
            act.wait_ge(d["bq"], 1)
            steps(act, [d_xT, d_qT], d_main)

            def e_xT(g, par, half):
                act.wait_ge(e["tr"], g + 1)
                wait(act, e["up"], 4 * E * (g - 1))
                nc.scalar.copy(xnT[:, par, :], bank[:, 0, :]).then_inc(e["xnT"], 1)

            def e_mT(g, par, half):
                act.wait_ge(e["mtr"], g + 1)
                wait(act, e["bias"], g)
                nc.scalar.copy(mT[0:E, :], bank[0:E, 0, :]).then_inc(e["mT"], 1)

            def e_main(g, par, half, nxt):
                for u in range(E):
                    for k in range(4):
                        w = 4 * (E * g + u) + k
                        act.wait_ge(e["up"], w + 1)
                        if k == 0:
                            wait(act, e["down"], E * g + u - 1)
                        nc.scalar.activation(h4[:, u % 2, k, :], bank[:, 2 + k % 2, :], ACT.Relu,
                                             bias=b1_s[:, 4 * u + k:4 * u + k + 1]).then_inc(e["h"], 1)
                    if u == 1:
                        nxt(0)
                    if u == 3:
                        nxt(1)
            steps(act, [e_xT, e_mT], e_main)

        @block.tensor
        def _(pe):
            def a_kv(g, par, half):
                pe.wait_ge(a["xn"], g + 1)
                wait(pe, a["xnT"], g)
                transpose_xn(pe, a, g, par)
                pe.wait_ge(a["ctx"][par], 16 * (half + 1))
                wait(pe, a["kT"], g)
                nc.tensor.matmul(bank[:, 2, :], wA_s[:, WK, :], ctxb[:, par, :], start=True, stop=True).then_inc(a["k"], 1)
                wait(pe, a["vS"], g)
                for t in range(GT):
                    i = nc.tensor.matmul(bank[:, 3, t * P:(t + 1) * P], ctxb[:, par, t * P:(t + 1) * P],
                                         wA_s[:, WV, :], start=True, stop=True)
                i.then_inc(a["v"], 1)

            def a_q(g, par, half):
                pe.wait_ge(a["xnT"], g + 1)
                wait(pe, a["qT"], g)
                nc.tensor.matmul(bank[:, 1, :], wA_s[:, WQ, :], xnT[:, par, :], start=True, stop=True).then_inc(a["q"], 1)

            def a_main(g, par, half, nxt):
                pe.wait_ge(a["qT"], g + 1)
                pe.wait_ge(a["kT"], g + 1)
                wait(pe, a["sub"], g)
                for t in range(GT):
                    for n in range(2):
                        k = (2 * t + n) * S
                        i = nc.tensor.matmul(bank[n * S:(n + 1) * S, 4, t * S:(t + 1) * S], qT[:, par, k:k + S],
                                             kT[:, par, k:k + S], start=True, stop=True)
                i.then_inc(a["s"], 1)
                nxt(0)
                pe.wait_ge(a["exp"], g + 1)
                wait(pe, a["pT"], g)
                for t in range(GT):
                    i = nc.tensor.transpose(bank[:, 5, t * P:(t + 1) * P], pbd[:, par, t, :], ident[:])
                i.then_inc(a["ptr"], 1)
                nxt(1)
                pe.wait_ge(a["pT"], g + 1)
                pe.wait_ge(a["vS"], g + 1)
                wait(pe, a["xo"], g)
                for t in range(GT):
                    i = nc.tensor.matmul(bank[:, 6, t * P:(t + 1) * P], pT[:, par, t, :], vS[:, par, t, :],
                                         start=True, stop=True)
                i.then_inc(a["o"], 1)
            pe.wait_ge(w_in, 16 * 3)
            pe.wait_ge(id_ready, 1)
            steps(pe, [a_kv, a_q], a_main)

            pe.wait_ge(a["xo"], G)
            pe.wait_ge(wB_in, 16)

            def b_turn(g, par, half):
                pe.wait_ge(b["xn"], g + 1)
                wait(pe, b["xnT"], g)
                transpose_xn(pe, b, g, par)

            def b_router(g, par, half):
                pe.wait_ge(b["xnT"], g + 1)
                wait(pe, b["lsub"], g)
                for t in range(GT):
                    i = nc.tensor.matmul(bank[:, 1, t * E:(t + 1) * E], xnT[:, par, t * P:(t + 1) * P], wrouter,
                                         start=True, stop=True)
                i.then_inc(b["logit"], 1)

            def b_main(g, par, half, nxt):
                def down(u):
                    w, pu = NE * g + u, (par + u) % 2
                    pe.wait_ge(b["h"], w + 1)
                    wait(pe, b["acc"], w - 1)
                    for t in range(GT):
                        i = nc.tensor.matmul(bank[:, 6 + pu, t * P:(t + 1) * P], hT[:, pu, t * P:(t + 1) * P],
                                             wdown[:, u, :], start=True, stop=True)
                    i.then_inc(b["down"], 1)

                if isinstance(g, int):
                    pe.wait_ge(b["xnT"], g + 1)
                for u in range(NE):
                    w, pu = NE * g + u, (par + u) % 2
                    wait(pe, b["act"], w - 1)
                    nc.tensor.matmul(bank[:, 2 + pu, :], wgate[:, u, :], xnT[:, par, :], start=True,
                                     stop=True).then_inc(b["gate"], 1)
                    wait(pe, b["h"], w - 1)
                    nc.tensor.matmul(bank[:, 4 + pu, :], wup[:, u, :], xnT[:, par, :], start=True,
                                     stop=True).then_inc(b["up"], 1)
                    if u:
                        down(u - 1)
                    if u == 3:
                        nxt(0)
                    if u == 5:
                        nxt(1)
                down(E)
            steps(pe, [b_turn, b_router], b_main)

            pe.wait_ge(b["acc"], NE * G)
            pe.wait_ge(c["memrow"], 1)

            def c_turn(g, par, half):
                pe.wait_ge(c["xn"], g + 1)
                wait(pe, c["xo"], g - 1)
                wait(pe, c["vS"], 2 * g)
                transpose_xn(pe, c, g, par)

            def c_q(g, par, half):
                pe.wait_ge(c["xnT"], g + 1)
                nc.tensor.matmul(bank[:, 0, :], wC_s[:, 0, :], xnT[:, par, :], start=True, stop=True).then_inc(c["q"], 1)

            def c_k(g, par, half):
                pe.wait_ge(c["ctx"][par], 16 * (half + 1))
                pe.wait_ge(c["qT"], g + 1)
                nc.tensor.matmul(bank[:, 0, :], wC_s[:, 1, :], ctxb[:, par, :], start=True, stop=True).then_inc(c["k"], 1)

            def c_v(k):
                def part(g, par, half):
                    pe.wait_ge(c["kT"], g + 1)
                    if k:
                        pe.wait_ge(c["vS"], 2 * g + 1)
                    for n in range(NB // 2):
                        m = (k * NB // 2 + n) * S
                        i = nc.tensor.matmul(bank[0:S, 0, n * P:(n + 1) * P], ctxb[:, par, m:m + S], wC_s[:, 2, :],
                                             start=True, stop=True)
                    i.then_inc(c["v"], 1)
                return part

            def c_scores(g, par, j):
                t, r = j // 4, j % 4
                w = 16 * g + j
                wait(pe, c["sub"], w - 3)
                pe.wait_ge(c["qx"], g + 1)
                pe.wait_ge(c["kT"], g + 1)
                pe.wait_ge(c["mask"], g + 1)
                o = bank[:, 2 + r, :].rearrange("p (b u k) -> p b u k", b=2, u=2)
                m = mrow[0:1, par, t * P:(t + 1) * P].rearrange("p (b s) -> p b s", b=2)
                nc.tensor.matmul(o[:, :, :, 0:S], onesb[0:1, :], m.unsqueeze(2).to_broadcast([1, 2, 2, S]),
                                 start=True, stop=False, skip_group_check=True)
                for b1 in range(2):
                    for u in range(2):
                        i = nc.tensor.matmul(o[:, b1, u, :],
                                             qx[:, par, 2 * t + b1, (2 * r + u) * P:(2 * r + u + 1) * P],
                                             kk[:, par, 2 * t + b1, :], start=False,
                                             stop=(b1 == 1 and u == 1), skip_group_check=True)
                i.then_inc(c["s"], 1)

            def c_pv(w, j, par, tiles):
                t, r = j // 4, j % 4
                pe.wait_ge(c["pT"], w + 1)
                wait(pe, c["oc"], tiles)
                for b1 in range(2):
                    for hh in range(4):
                        i = nc.tensor.matmul(bank[32 * hh:32 * hh + VW, 7, r * P + b1 * S:r * P + b1 * S + S],
                                             v1[:, par, 2 * t + b1, (4 * r + hh) * VW:(4 * r + hh + 1) * VW],
                                             cPT[:, j % 2, (4 * b1 + hh) * S:(4 * b1 + hh + 1) * S],
                                             start=True, stop=True)
                i.then_inc(c["pv"], 1)

            def c_back(n):
                pe.wait_ge(c["oc"], n + 1)
                for r in range(4):
                    i = nc.tensor.transpose(bank[:, 6, r * P:(r + 1) * P], cO[:, r * P:(r + 1) * P], ident[:])
                i.then_inc(c["bt"], 1)

            def c_otrans(g, par):
                pe.wait_ge(c["on"], 4 * (g + 1))
                for t in range(GT):
                    i = nc.tensor.transpose(bank[:, 6, t * P:(t + 1) * P], Oa[:, par, t, :], ident[:])
                i.then_inc(c["otr"], 1)

            def c_out(g):
                pe.wait_ge(c["oT"], g + 1)
                for t in range(GT):
                    i = nc.tensor.matmul(bank[:, 0, t * P:(t + 1) * P], cOT[:, t * P:(t + 1) * P], wC_s[:, 3, :],
                                         start=True, stop=True)
                i.then_inc(c["wo"], 1)

            def c_main(g, par, half, nxt):
                first = isinstance(g, int) and g == 0
                last = isinstance(g, int) and g == G - 1
                if first:
                    pe.wait_ge(c["vS"], 2)
                    for j in range(4):
                        c_scores(g, par, j)
                for j in range(16):
                    w = 16 * g + j
                    if j == 4:
                        wait(pe, c["oT"], g)
                    if j % 4 == 2 and not (first and j == 2):
                        wait(pe, c["on"], 4 * g + j // 4)
                    pe.wait_ge(c["exp"], w + 1)
                    wait(pe, c["pT"], w - 1)
                    for u in range(4):
                        i = nc.tensor.transpose(bank[:, 1 if j % 2 else 6, u * P:(u + 1) * P], cP[:, j % 2, u, :],
                                                ident[:])
                    i.then_inc(c["ptr"], 1)
                    if j:
                        pe.wait_ge(c["vS"], 2 * g + 2)
                        c_pv(w - 1, j - 1, par, 4 * g + (j - 1) // 4)
                    elif not first:
                        c_pv(w - 1, 15, 1 - par, 4 * g - 1)
                    if j == 2 and not first:
                        pe.wait_ge(c["pT"], w + 1)
                        c_otrans(g - 1, 1 - par)
                    if j == 3 and not first:
                        pe.wait_ge(c["vS"], 2 * g + 2)
                        c_out(g - 1)
                    if j == 5:
                        nxt(0)
                    if j == 7:
                        nxt(1)
                    if j == 9:
                        nxt(2)
                    if j == 11:
                        nxt(3)
                    if j == 12:
                        nxt(4)
                    if j < 12:
                        c_scores(g, par, j + 4)
                    elif not last:
                        c_scores(g + 1, 1 - par, j - 12)
                    if j % 4 == 1 and not (first and j == 1):
                        c_back(4 * g + j // 4 - 1)
            steps(pe, [c_turn, c_q, c_k, c_v(0), c_v(1)], c_main)
            pe.wait_ge(c["pT"], 16 * G)
            c_pv(16 * G - 1, 15, 1, 4 * G - 1)
            c_back(4 * G - 1)
            c_otrans(G - 1, 1)
            c_out(G - 1)

            pe.wait_ge(c["xo"], G)
            pe.wait_ge(wF_in, 16 * 5)

            def d_turn(g, par, half):
                pe.wait_ge(dn["xn"], g + 1)
                wait(pe, d["kT"], g)
                transpose_xn(pe, dn, g, par)
                wait(pe, d["vS"], g)
                pe.wait_ge(d["xnT"], g + 1)
                nc.tensor.matmul(bank[:, 1, :], wF_s[:, 0:P], xnT[:, par, :], start=True, stop=True).then_inc(d["q"], 1)
                nc.tensor.matmul(bank[:, 0, :], wF_s[:, P:2 * P], xnT[:, par, :], start=True, stop=True).then_inc(d["k"], 1)

            def d_v(g, par, half):
                pe.wait_ge(d["qT"], g + 1)
                for t in range(GT):
                    i = nc.tensor.matmul(bank[:, 1, t * P:(t + 1) * P], xnT[:, par, t * P:(t + 1) * P],
                                         wF_s[:, 2 * P:3 * P], start=True, stop=True)
                i.then_inc(d["v"], 1)

            def d_main(g, par, half, nxt):
                pe.wait_ge(d["kT"], g + 1)
                wait(pe, d["sub"], 2 * g)
                for m in range(2):
                    for h in range(2):
                        for t in range(GT):
                            for n in range(2):
                                k = (2 * t + n) * S
                                i = nc.tensor.matmul(
                                    bank[n * S:(n + 1) * S, 4 + m, (h * GT + t) * S:(h * GT + t + 1) * S],
                                    q4[:, par, 2 * m + h, k:k + S], kT[:, par, k:k + S], start=True, stop=True)
                    i.then_inc(d["s"], 1)

                def pv(h):
                    w = 4 * g + h
                    pe.wait_ge(d["pT"], w + 1)
                    pe.wait_ge(d["vS"], g + 1)
                    wait(pe, d["z"], g)
                    for t in range(GT):
                        k = (h % 2 * GT + t) * (D4 + 1)
                        i = nc.tensor.matmul(bank[:, 2 + h // 2, k:k + D4 + 1], cPT[:, h % 2, t * P:(t + 1) * P],
                                             v4[:, par, t, h * (D4 + 1):(h + 1) * (D4 + 1)], start=True, stop=True)
                    i.then_inc(d["pv"], 1)
                for h in range(H4):
                    w = 4 * g + h
                    if h % 2 == 0:
                        pe.wait_ge(d["exp"], 2 * g + h // 2 + 1)
                    wait(pe, d["pT"], w - 1)
                    for t in range(GT):
                        i = nc.tensor.transpose(bank[:, 6 + h % 2, t * P:(t + 1) * P], dP[:, h * GT + t, :], ident[:])
                    i.then_inc(d["ptr"], 1)
                    if h:
                        pv(h - 1)
                    if h == 1:
                        nxt(0)
                pv(3)
                pe.wait_ge(d["on"], 2 * g + 2)
                for t in range(GT):
                    i = nc.tensor.transpose(bank[:, 2, t * P:(t + 1) * P], dOa[:, t, :], ident[:])
                i.then_inc(d["otr"], 1)
                pe.wait_ge(d["oT"], g + 1)
                for t in range(GT):
                    i = nc.tensor.matmul(bank[:, 3, t * P:(t + 1) * P], cOT[:, t * P:(t + 1) * P], wF_s[:, 3 * P:4 * P],
                                         start=True, stop=True)
                i.then_inc(d["wo"], 1)
                nxt(1)
            steps(pe, [d_turn, d_v], d_main)

            pe.wait_ge(d["z"], G)

            def e_turn(g, par, half):
                pe.wait_ge(e["ys"], g + 1)
                wait(pe, e["mT"], g)
                for t in range(GT):
                    i = nc.tensor.transpose(bank[:, 0, t * P:(t + 1) * P], ys[:, par, t, :], ident[:])
                i.then_inc(e["tr"], 1)

            def e_router(g, par, half):
                pe.wait_ge(e["xnT"], g + 1)
                wait(pe, e["route"], 5 * g)
                for t in range(GT):
                    i = nc.tensor.matmul(bank[:, 1, t * E:(t + 1) * E], xnT[:, par, t * P:(t + 1) * P],
                                         wF_s[:, 4 * P:], start=True, stop=True)
                i.then_inc(e["logit"], 1)

            def e_bias(g, par, half):
                pe.wait_ge(e["route"], 5 * (g + 1))
                for t in range(GT):
                    i = nc.tensor.transpose(bank[0:E, 0, t * P:(t + 1) * P], le[:, par, t, :], ident[:])
                i.then_inc(e["mtr"], 1)
                pe.wait_ge(e["mT"], g + 1)
                wait(pe, e["yb"], g)
                for t in range(GT):
                    i = nc.tensor.matmul(bank[:, 7, t * P:(t + 1) * P], mT[0:E, t * P:(t + 1) * P], b2_s[0:E, :],
                                         start=True, stop=True)
                i.then_inc(e["bias"], 1)

            def e_main(g, par, half, nxt):
                def down(u):
                    w = E * g + u
                    pe.wait_ge(e["h"], 4 * (w + 1))
                    wait(pe, e["acc"], w - 1)
                    for t in range(GT):
                        for k in range(4):
                            i = nc.tensor.matmul(bank[:, 4 + u % 2, t * P:(t + 1) * P],
                                                 h4[:, u % 2, k, t * P:(t + 1) * P],
                                                 w2_s[:, (4 * u + k) * P:(4 * u + k + 1) * P],
                                                 start=(k == 0), stop=(k == 3))
                    i.then_inc(e["down"], 1)
                for u in range(E):
                    for k in range(4):
                        w = 4 * (E * g + u) + k
                        wait(pe, e["h"], w - 1)
                        nc.tensor.matmul(bank[:, 2 + k % 2, :], w1_s[:, (4 * u + k) * P:(4 * u + k + 1) * P],
                                         xnT[:, par, :], start=True, stop=True).then_inc(e["up"], 1)
                    if u:
                        down(u - 1)
                    if u == 1:
                        nxt(0)
                    if u == 2:
                        nxt(1)
                    if u == 3:
                        nxt(2)
                down(E - 1)
            steps(pe, [e_turn, e_router, e_bias], e_main)


def kernel(**inputs):
    import concourse.bacc as bacc
    from concourse.bass_utils import run_bass_kernel_spmd

    a = {k: np.asarray(v) for k, v in inputs.items()}
    cat = lambda parts: np.ascontiguousarray(np.concatenate([p.reshape(P, -1) for p in parts], axis=1))
    bqkv = a["L1_ffn_bqkv"].reshape(3, P)
    arrays = {
        "x": np.ascontiguousarray(a["x"].reshape(N, P)),
        "ctxT": np.ascontiguousarray(a["ctx_1024"].reshape(N, P).T),
        "maskrow": np.ascontiguousarray(a["mask_Bx1x1xS2_bk0"].reshape(1, N)),
        "wA": cat([a["L0_xattn_Wq"], a["L0_xattn_Wk"], a["L0_xattn_Wv"]]),
        "wB": cat([a["L0_ffn_Wg"].transpose(2, 0, 1), a["L0_ffn_Sg"].T, a["L0_ffn_Wu"].transpose(2, 0, 1),
                   a["L0_ffn_Su"].T, a["L0_ffn_Wd"].transpose(2, 0, 1), a["L0_ffn_Sd"].T, a["L0_ffn_Wr"].T]),
        "wC": cat([a["L1_xattn_Wq"].T, a["L1_xattn_Wk"].T, a["L1_xattn_Wv"].T, a["L1_xattn_Wo"].T]),
        "memT": np.ascontiguousarray(a["L1_xattn_m_k"][0].T),
        "mem": np.ascontiguousarray(a["L1_xattn_m_v"][0]),
        "wF": cat([a["L1_ffn_Wqkv"].T, a["L1_ffn_Wo"].T, a["L1_ffn_Wg"].T]),
        "w1": cat([a["L1_ffn_W1"].transpose(1, 0, 2)]),
        "w2": cat([a["L1_ffn_W2"].reshape(E, 4, P, P).transpose(2, 0, 1, 3)]),
        "b1": np.ascontiguousarray(a["L1_ffn_b1"].reshape(4 * E, P).T),
        "b2": np.ascontiguousarray(a["L1_ffn_b2"]),
        "rows": np.ascontiguousarray(np.broadcast_to(np.stack([
            a["L0_xattn_bv"], a["L1_xattn_bv"], a["L1_xattn_bo"], bqkv[2], a["L1_ffn_bo"], a["L1_ffn_g1"],
            a["L1_ffn_be1"], a["L1_ffn_g2"], a["L1_ffn_be2"]]).reshape(1, -1), (P, NROWS * P))),
        "cols": np.ascontiguousarray(np.stack([a["L0_xattn_bq"], a["L0_xattn_bk"], a["L1_xattn_bq"],
                                               a["L1_xattn_bk"], bqkv[0], bqkv[1]]
                                              + [(np.arange(P) // 8 == i).astype(np.float32)
                                                 for i in range(16)]
                                              + [(np.arange(P) // 32 == i).astype(np.float32)
                                                 for i in range(4)], axis=1)),
    }
    nc = bacc.Bacc("TRN2", target_bir_lowering=False, num_devices=1)
    args = [nc.dram_tensor("in_" + n, v.shape, mybir.dt.from_np(v.dtype), kind="ExternalInput").ap()
            for n, v in arrays.items()]
    out = nc.dram_tensor("out", (N, P), F32, kind="ExternalOutput").ap()
    program(nc, *args, out)
    r = run_bass_kernel_spmd(nc, [{"in_" + n: v for n, v in arrays.items()}], core_ids=[0])
    return r.results[0]["out"].reshape(B, S, P)
```

```python
from contextlib import ExitStack

import numpy as np
import concourse.bass as bass
from concourse import mybir

ALU = mybir.AluOpType
ACT = mybir.ActivationFunctionType
AX = mybir.AxisListType
F32 = mybir.dt.float32
BF16 = mybir.dt.bfloat16
U8 = mybir.dt.uint8

P = 128
S = 64
B = 64
N = B * S
T = N // P
GT = 4
GW = GT * P
G = T // GT
EPS = 1e-5
H = 16
DK = P // H
M = 64
VW = DK + 1
NEG = -1e30
E = 8
NT = T + E

WQ, WK, WV = range(3)
R_BV, R_XBV, R_XBO, R_QKVBV, R_BO, R_G1, R_BE1, R_G2, R_BE2 = range(9)
NROWS = 9
C_BQ, C_BK, C_XBQ, C_XBK, C_MBQ, C_MBK, C_HEAD = range(7)
C_HEAD4 = C_HEAD + 16
NCOLS = C_HEAD4 + 4


def wait(eng, sem, value):
    if isinstance(value, int) and value <= 0:
        return
    eng.wait_ge(sem, value)


def program(nc, x, ctxT, maskrow, wA, wB, wC, memT, mem, wF, w1, w2, b1, b2, rows, cols, out):
    with ExitStack() as ctx:
        def sb(name, shape, dt=F32):
            return ctx.enter_context(nc.sbuf_tensor(name, shape, dt))

        def sem(name):
            return ctx.enter_context(nc.semaphore(name))

        def pair(name):
            return [sem(f"{name}{i}") for i in range(2)]

        bank = ctx.enter_context(nc.psum_tensor("bank", [P, 8, 512], F32))
        X = sb("X", [P, T, P])
        wA_s = sb("wA_s", [P, 3, P])
        rows_s = sb("rows_s", [P, NROWS, P])
        cols_s = sb("cols_s", [P, NCOLS])
        ident = sb("ident", [P, P])
        neghalf = sb("neghalf", [P, GT])
        st = sb("st", [P, 2, GT, 6])
        lsum = sb("lsum", [P, 2, GT, 2])
        ldif = sb("ldif", [P, 2, GT])
        mean = sb("mean", [P, 2, GT])
        ve = sb("ve", [P, 2, GT])
        rstd = sb("rstd", [P, 2, GT])
        xn = sb("xn", [P, 2, GT, P])
        xnT = sb("xnT", [P, 2, GW])
        ctxb = sb("ctxb", [P, 2, GW])

        qT = sb("qT", [P, 2, GW])
        kT = sb("kT", [P, 2, GW])
        vS = sb("vS", [P, 2, GT, P])
        mx = sb("mx", [P, 2, GT])
        ss = sb("ss", [P, 2, GT, S])
        pbd = sb("pbd", [P, 2, GT, P])
        pT = sb("pT", [P, 2, GT, P])
        rs = sb("rs", [P, 2, GT])
        ri = sb("ri", [P, 2, GT])

        NE = E + 1
        big = sb("big", [P, E * 4 * P])
        wB_s = big[:, 0:3 * NE * P + E]
        wgate, wup, wdown = [wB_s[:, i * NE * P:(i + 1) * NE * P].rearrange("p (e f) -> p e f", e=NE)
                             for i in range(3)]
        wrouter = wB_s[:, 3 * NE * P:]
        desc = sb("desc", [P, GT, E])
        le = sb("le", [P, 2, GT, E])
        r8 = [sb(f"r8{i}", [P, GT, E]) for i in range(4)]
        r1 = [sb(f"r1{i}", [P, GT]) for i in range(6)]
        comb = sb("comb", [P, 2, GT, E])
        th = sb("th", [P, 2, GW])
        ga = sb("ga", [P, 2, GW])
        hT = sb("hT", [P, 2, GW])

        wC_s = sb("wC_s", [P, 4, P])
        maskb = sb("maskb", [P, N], U8)
        mrow = sb("mrow", [P, 2, GW], BF16)
        onesb = sb("onesb", [P, P], BF16)
        memT_s = sb("memT_s", [P, M])
        mem_s = sb("mem_s", [P, P])
        NB = GW // S
        arena = sb("arena", [P, 2 * NB * H * S])
        qx = arena[:].rearrange("p (i b c) -> p i b c", i=2, b=NB)
        kk = sb("kk", [P, 2, NB, S + M])
        v1 = sb("v1", [P, 2, NB, H * VW])
        cmx = sb("cmx", [P, 2, 4])
        csub = sb("csub", [P, 2, 4, P])
        cP = sb("cP", [P, 2, 4, P])
        cPT = sb("cPT", [P, 2, GW])
        crv = sb("crv", [P, H])
        cO = ga[:, 0, :]
        Oa = sb("Oa", [P, 2, GT, P])
        cOT = sb("cOT", [P, GW])

        H4, D4 = 4, P // 4
        x3 = nc.dram_tensor("x3", (N, P), F32, kind="Internal").ap()
        x3_t = x3.rearrange("(t p) d -> p t d", p=P)
        wF_s = sb("wF_s", [P, 4 * P + E])
        at = [0]

        def part(shape):
            n = int(np.prod(shape))
            v = arena[:, at[0]:at[0] + n]
            at[0] += n
            names = "abcd"[:len(shape)]
            return v.rearrange(f"p ({' '.join(names)}) -> p {' '.join(names)}", **dict(zip(names, shape)))
        xg = part([2, GT, P])
        dbq = sb("dbq", [P, 4])
        q4 = part([2, H4, GW])
        v4 = sb("v4", [P, 2, GT, H4 * (D4 + 1)])
        dmx = sb("dmx", [P, 2, 8])
        dsub = part([2, 8, S])
        dP = part([16, P])
        drv = sb("drv", [P, 2, 8])
        dOa = sb("dOa", [P, GT, P])
        z = ss[:].rearrange("p i t k -> p (i t k)").rearrange("p (t d) -> p t d", t=GT)

        ys = xg
        yT = ga[:, 1, :]
        mall = sb("mall", [P, T, E])
        xs = nc.dram_tensor("xs", (NT * P, P), F32, kind="Internal").ap()
        os = nc.dram_tensor("os", (NT * P, P), F32, kind="Internal").ap()
        b1_s = part([E * 4 * P])
        b2_s = hT[:].rearrange("p i w -> p (i w)")
        before = sb("before", [P, P])
        ones = sb("ones", [P, 2 * P])
        zero = sb("zero", [P, P])
        starts_i = sb("starts_i", [P, T], mybir.dt.int32)
        starts = sb("starts", [P, T])
        tiles_i = sb("tiles_i", [P, NT], mybir.dt.int32)
        tiles = sb("tiles", [P, NT])
        flat = csub[:].rearrange("p i u k -> p (i u k)")
        cum, cumx, pos = [flat[:, i * E * T:(i + 1) * E * T].rearrange("p (e t) -> p e t", e=E) for i in range(3)]
        big8 = th[:, 0, 0:NT * E].rearrange("p (j e) -> p j e", e=E)
        n8 = [sb(f"n8{i}", [P, E]) for i in range(5)]
        slotf = sb("slotf", [P, T])
        slot = sb("slot", [P, T], mybir.dt.uint32)
        tef = sb("tef", [P, NT])
        te = sb("te", [P, NT], mybir.dt.int32)
        xe = [xn[:, i, 0, :] for i in range(2)]
        xeT = [xnT[:, i, 0:P] for i in range(2)]
        he = [q4[:, i, 0, :] for i in range(2)]
        heT = [q4[:, i, 1, :] for i in range(2)]
        oe = [xn[:, i, 1, :] for i in range(2)]
        w1_s = big
        w2_s = part([E * 4 * P])
        og = big[:].rearrange("p (t d) -> p t d", t=T)
        yo = vS
        xr = pbd

        w_in = sem("w_in")
        id_zero, id_ready, const_ready = sem("id_zero"), sem("id_ready"), sem("const_ready")
        def sems(prefix, names, **more):
            return {n: sem(f"{prefix}_{n}") for n in names.split()} | more

        wB_in, wC_in = sem("wB_in"), sem("wC_in")
        stats, scales = sem("stats"), sem("scales")
        LN = "xn tr xnT "
        a = sems("a", LN + "q k v qT kT vS s mx sub exp ri ptr pT o xo", ln=stats, rstd=scales, past=0,
                 x=pair("a_x"), ctx=pair("a_ctx"))
        b = sems("b", LN + "logit lmax lsub lexp route comb gate up tanh act h down acc", ln=stats, rstd=scales, past=G)
        c = sems("c", LN + "q k v mask qT kT vS s mx sub exp ptr pT pv oc bt rv on otr oT wo xa xo const memrow qx",
                 ln=stats, rstd=scales, past=2 * G, ctx=pair("c_ctx"))
        d = sems("d", "ln rstd xnT q k v qT kT vS s mx sub exp ptr pT pv rv on otr oT wo z lg normed const bq ytr yT logit route ycopy",
                 past=0, x=pair("d_x"))
        dn = sems("dn", "ln rstd xn tr", past=0)
        m = sems("m", "tr xT h hb htr hT up o", x=pair("m_x"), out=pair("m_out"))
        r_step, r_sums, slots_ready = sem("r_step"), sem("r_sums"), sem("slots_ready")
        xs_zero, xs_in, io_ready = sem("xs_zero"), sem("xs_in"), sem("io_ready")
        e = sems("e", "add lg normed y", ln=stats, rstd=scales, past=3 * G, x=pair("e_x"), out=pair("e_out"), rows=pair("e_rows"))
        x3_out, wF_in = sem("x3_out"), sem("wF_in")

        x_t = x.rearrange("(t p) d -> p t d", p=P)

        def steps(eng, ahead, main):
            for part in ahead:
                part(0, 0, 0)

            def call(g, par, half, half1, last=False):
                def nxt(k):
                    if not last:
                        ahead[k](g + 1, 1 - par, half1)
                main(g, par, half, nxt)
            call(0, 0, 0, 0)
            with eng.Fori(0, (G - 2) // 2) as i:
                call(2 * i + 1, 1, i, i + 1)
                call(2 * i + 2, 0, i + 1, i + 1)
            call(G - 1, 1, (G - 1) // 2, None, last=True)

        def tile_steps(eng, step):
            for j in range(2):
                step(j, j, 0, NT - j)
            with eng.Fori(1, NT // 2 - 1) as i:
                for j in range(2):
                    step(2 * i + j, j, i, 3)
            for j in range(NT - 2, NT):
                step(j, j % 2, j // 2, NT - j)

        def layer_norm_stats(dve, n, g, par, src):
            def then(i, k):
                i.then_inc(n["ln"], 1)
                dve.wait_ge(n["ln"], 5 * (g + n["past"]) + k)
            for t in range(GT):
                i = nc.vector.bn_stats(st[:, par, t, :], src(t))
            then(i, 1)
            even, odd = st[:, par, :, 1:3], st[:, par, :, 4:6]
            nc.vector.tensor_tensor(lsum[:, par], even, odd, ALU.add)
            then(nc.vector.tensor_tensor(ldif[:, par], even[:, :, 0], odd[:, :, 0], ALU.subtract), 2)
            nc.vector.tensor_scalar(mean[:, par], lsum[:, par, :, 0], 0.5, None, ALU.mult)
            then(nc.vector.tensor_tensor(ldif[:, par], ldif[:, par], ldif[:, par], ALU.mult), 3)
            then(nc.vector.scalar_tensor_tensor(ve[:, par], ldif[:, par], P / 4.0, lsum[:, par, :, 1],
                                                ALU.mult, ALU.add), 4)
            nc.vector.tensor_scalar(ve[:, par], ve[:, par], 1.0 / P, EPS, ALU.mult, ALU.add).then_inc(n["ln"], 1)
            dve.wait_ge(n["rstd"], g + n["past"] + 1)

        def layer_norm_rows(dve, n, g, par, src=lambda g, t: X[:, g * GT + t, :]):
            layer_norm_stats(dve, n, g, par, lambda t: src(g, t))
            wait(dve, n["tr"], g - 1)
            for t in range(GT):
                i = nc.vector.tensor_scalar(xn[:, par, t, :], src(g, t), mean[:, par, t:t + 1],
                                            rstd[:, par, t:t + 1], ALU.subtract, ALU.mult)
            i.then_inc(n["xn"], 1)

        def layer_norm_affine(dve, n, g, par, src, out_rows, r_gain, r_bias):
            layer_norm_stats(dve, n, g, par, src)
            for t in range(GT):
                i = nc.vector.tensor_scalar(xn[:, par, t, :], src(t), mean[:, par, t:t + 1],
                                            rstd[:, par, t:t + 1], ALU.subtract, ALU.mult)
            i.then_inc(n["lg"], 1)
            dve.wait_ge(n["lg"], 2 * g + 1)
            nc.vector.tensor_tensor(xn[:, par], xn[:, par], rows_s[:, r_gain:r_gain + 1, :].to_broadcast([P, GT, P]),
                                    ALU.mult).then_inc(n["lg"], 1)
            dve.wait_ge(n["lg"], 2 * g + 2)
            nc.vector.tensor_tensor(out_rows, xn[:, par], rows_s[:, r_bias:r_bias + 1, :].to_broadcast([P, GT, P]),
                                    ALU.add).then_inc(n["normed"], 1)

        def pool_rstd(pool, n, g, par):
            pool.wait_ge(n["ln"], 5 * (g + n["past"] + 1))
            nc.gpsimd.tensor_tensor(rstd[:, par, :], ve[:, par, :], neghalf[:], ALU.pow).then_inc(n["rstd"], 1)

        def transpose_xn(pe, n, g, par):
            for t in range(GT):
                i = nc.tensor.transpose(bank[:, 0, t * P:(t + 1) * P], xn[:, par, t, :], ident[:])
            i.then_inc(n["tr"], 1)

        block = ctx.enter_context(nc.Block())

        @block.sync
        def _(sp):
            sp.dma_start(wA_s[:], wA).then_inc(w_in, 16)
            sp.dma_start(rows_s[:], rows).then_inc(w_in, 16)
            sp.dma_start(cols_s[:], cols).then_inc(w_in, 16)

            def a_load(g, par, half):
                wait(sp, a["v"], g - 1)
                wait(sp, a["xn"], g - 1)
                sp.dma_start(X[:, bass.ds(g * GT, GT), :], x_t[:, bass.ds(g * GT, GT), :]).then_inc(a["x"][par], 16)
                sp.dma_start(ctxb[:, par, :], ctxT[:, bass.ds(g * GW, GW)]).then_inc(a["ctx"][par], 16)
            steps(sp, [a_load], lambda g, par, half, nxt: nxt(0))
            sp.dma_start(wB_s[:], wB).then_inc(wB_in, 16)
            sp.dma_start(wC_s[:], wC.rearrange("p (i d) -> p i d", i=4)).then_inc(wC_in, 16)
            sp.dma_start(memT_s[:], memT).then_inc(wC_in, 16)
            sp.dma_start(mem_s[M:P, :], mem).then_inc(wC_in, 16)
            sp.dma_start(maskb[:], bass.AP(maskrow.tensor, 0, [[0, P], [1, N]])).then_inc(wC_in, 16)
            sp.wait_ge(const_ready, 3)
            sp.dma_start(xs.rearrange("(j p) d -> p j d", p=P),
                         zero[:].unsqueeze(1).to_broadcast([P, NT, P])).then_inc(xs_zero, 16)
            sp.wait_ge(a["o"], G)

            def c_load(g, par, half):
                wait(sp, c["v"], 2 * g - 2)
                sp.dma_start(ctxb[:, par, :], ctxT[:, bass.ds(g * GW, GW)]).then_inc(c["ctx"][par], 16)
            def c_store(g, par, half, nxt):
                nxt(0)
                sp.wait_ge(c["xo"], g + 1)
                sp.dma_start(x3_t[:, bass.ds(g * GT, GT), :], X[:, bass.ds(g * GT, GT), :]).then_inc(x3_out, 16)
            steps(sp, [c_load], c_store)
            sp.dma_start(wF_s[:], wF).then_inc(wF_in, 16)
            sp.dma_start(b1_s, bass.AP(b1.tensor, 0, [[0, P], [1, 4 * E * P]])).then_inc(wF_in, 16)
            sp.dma_start(b2_s, bass.AP(b2.tensor, 0, [[0, P], [1, E * P]])).then_inc(wF_in, 16)
            sp.dma_start(w1_s[:], w1).then_inc(wF_in, 16)
            sp.dma_start(w2_s[:], w2).then_inc(wF_in, 16)

            sp.wait_ge(x3_out, 16 * G)

            def rows_of(dram, g, n):
                return dram.rearrange("(b g t n) d -> n b g t d", b=B, g=G, n=2)[n][:, bass.ds(g, 1)].rearrange(
                    "b g t d -> b (g t) d")

            def d_load(g, par, half):
                wait(sp, d["ytr"], g - 1)
                wait(sp, d["ycopy"], g - 1)
                for n in range(2):
                    sp.dma_start(xg[n * S:(n + 1) * S, par], rows_of(x3, g, n)).then_inc(d["x"][par], 16)
            steps(sp, [d_load], lambda g, par, half, nxt: nxt(0))

            def m_load(j, par, half):
                wait(sp, m["tr"], j - 1)
                sp.dma_start(xe[par], xs[bass.ds(j * P, P), :]).then_inc(m["x"][par], 16)

            def m_store(j, par, half):
                sp.wait_ge(m["o"], j + 1)
                sp.dma_start(os[bass.ds(j * P, P), :], oe[par]).then_inc(m["out"][par], 16)

            def m_step(j, par, half, left):
                if left > 2:
                    m_load(j + 2, par, half + 1)
                m_store(j, par, half)
            sp.wait_ge(xs_in, 16 * T)
            m_load(0, 0, 0)
            m_load(1, 1, 0)
            tile_steps(sp, m_step)

            def e_load(g, par, half):
                wait(sp, e["y"], g - 1)
                for n in range(2):
                    sp.dma_start(xr[n * S:(n + 1) * S, par], rows_of(x3, g, n)).then_inc(e["x"][par], 16)

            def e_store(g, par, half, nxt):
                nxt(0)
                sp.wait_ge(e["y"], g + 1)
                for n in range(2):
                    sp.dma_start(rows_of(out, g, n), yo[n * S:(n + 1) * S, par]).then_inc(e["out"][par], 16)
            steps(sp, [e_load], e_store)
            for par in range(2):
                sp.wait_ge(e["out"][par], 16 * G)

        @block.gpsimd
        def _(pool):
            nc.gpsimd.memset(ident[:], 0.0).then_inc(id_zero, 1)
            pool.wait_ge(id_zero, 1)
            nc.gpsimd.affine_select(out=ident[:], in_=ident[:], compare_op=ALU.not_equal, fill=1.0, base=0,
                                    pattern=[[-1, P]], channel_multiplier=1).then_inc(id_ready, 1)
            nc.gpsimd.memset(neghalf[:], -0.5).then_inc(const_ready, 1)
            nc.gpsimd.memset(pbd[:], 0.0).then_inc(const_ready, 1)
            for k in range(E):
                i = nc.gpsimd.memset(desc[:, :, k:k + 1], float(E - k))
            i.then_inc(const_ready, 1)
            nc.gpsimd.memset(zero[:], 0.0)
            nc.gpsimd.memset(ones[:], 1.0).then_inc(io_ready, 1)
            pool.wait_ge(io_ready, 1)
            nc.gpsimd.affine_select(out=before[:], in_=ones[:, 0:P], compare_op=ALU.is_gt, fill=0.0, base=0,
                                    pattern=[[1, P]], channel_multiplier=-1)
            nc.gpsimd.iota(starts_i[:], pattern=[[P, T]], base=0, channel_multiplier=0)
            nc.gpsimd.iota(tiles_i[:], pattern=[[1, NT]], base=0, channel_multiplier=0).then_inc(io_ready, 1)
            pool.wait_ge(io_ready, 2)
            nc.gpsimd.tensor_copy(starts[:], starts_i[:])
            nc.gpsimd.tensor_copy(tiles[:], tiles_i[:]).then_inc(io_ready, 1)
            nc.gpsimd.memset(onesb[:], 1.0)
            nc.gpsimd.memset(v1[:], 1.0).then_inc(c["const"], 1)
            nc.gpsimd.memset(v4[:], 1.0).then_inc(d["const"], 1)
            pool.wait_ge(const_ready, 3)
            for n in (a, b, c):
                steps(pool, [lambda g, par, half: pool_rstd(pool, n, g, par)], lambda g, par, half, nxt: nxt(0))
            
            pool.wait_ge(c["s"], 16 * G)
            nc.gpsimd.memset(dP[:], 0.0).then_inc(d["const"], 1)

            def d_rstd(g, par, half, nxt):
                nxt(0)
                pool_rstd(pool, d, g, par)
                pool.wait_ge(d["normed"], g + 1)
                nc.gpsimd.tensor_copy(X[:, bass.ds(g * GT, GT), :], ys[:, par]).then_inc(d["ycopy"], 1)
            steps(pool, [lambda g, par, half: pool_rstd(pool, dn, g, par)], d_rstd)

            pool.wait_ge(slots_ready, 1)
            pool.wait_ge(xs_zero, 16)
            pool.wait_ge(d["ycopy"], G)
            for t in range(T):
                pool.indirect_dma_start(xs, bass.IndirectOffsetOnAxis(ap=slot[:, t:t + 1], axis=0),
                                        X[:, t, :], None).then_inc(xs_in, 16)
            for par in range(2):
                pool.wait_ge(m["out"][par], 16 * (NT // 2))
            for g in range(G):
                if g >= 2:
                    pool.wait_ge(e["rows"][g % 2], 16 * GT * (g // 2))
                for t in range(g * GT, (g + 1) * GT):
                    pool.indirect_dma_start(og[:, t, :], None, os,
                                            bass.IndirectOffsetOnAxis(ap=slot[:, t:t + 1], axis=0)
                                            ).then_inc(e["rows"][g % 2], 16)
                if g:
                    pool_rstd(pool, e, g - 1, (g - 1) % 2)
            pool_rstd(pool, e, G - 1, 1)

        @block.vector
        def _(dve):
            def a_norm(g, par, half):
                dve.wait_ge(a["x"][par], 16 * (half + 1))
                layer_norm_rows(dve, a, g, par)

            def a_value(g, par, half):
                dve.wait_ge(a["v"], g + 1)
                wait(dve, a["o"], g - 1)
                nc.vector.tensor_tensor(vS[:, par], bank[:, 3, :].rearrange("p (t d) -> p t d", t=GT),
                                        rows_s[:, R_BV:R_BV + 1, :].to_broadcast([P, GT, P]), ALU.add).then_inc(a["vS"], 1)

            def a_main(g, par, half, nxt):
                dve.wait_ge(a["s"], g + 1)
                s = bank[:, 4, 0:GT * S].rearrange("p (t k) -> p t k", t=GT)
                nc.vector.tensor_reduce(mx[:, par, :], s, AX.X, ALU.max).then_inc(a["mx"], 1)
                dve.wait_ge(a["mx"], g + 1)
                wait(dve, a["exp"], g - 1)
                nc.vector.tensor_tensor(ss[:, par], s, mx[:, par, :].unsqueeze(2).to_broadcast([P, GT, S]),
                                        ALU.subtract).then_inc(a["sub"], 1)
                nxt(0)
                dve.wait_ge(a["exp"], g + 1)
                nc.vector.tensor_reduce(rs[:, par, :], pbd[:, par], AX.X, ALU.add).then_inc(a["ri"], 1)
                dve.wait_ge(a["ri"], 2 * g + 1)
                nc.vector.reciprocal(ri[:, par, :], rs[:, par, :]).then_inc(a["ri"], 1)
                nxt(1)
                dve.wait_ge(a["ri"], 2 * g + 2)
                dve.wait_ge(a["o"], g + 1)
                for t in range(GT):
                    xt = X[:, g * GT + t, :]
                    i = nc.vector.scalar_tensor_tensor(xt, bank[:, 6, t * P:(t + 1) * P], ri[:, par, t:t + 1], xt,
                                                       ALU.mult, ALU.add)
                i.then_inc(a["xo"], 1)
            dve.wait_ge(w_in, 16 * 3)
            steps(dve, [a_norm, a_value], a_main)

            def b_norm(g, par, half):
                dve.wait_ge(a["xo"], g + 1)
                layer_norm_rows(dve, b, g, par)

            def b_logits(g, par, half):
                lg = bank[:, 1, 0:GT * E].rearrange("p (t e) -> p t e", t=GT)
                dve.wait_ge(b["logit"], g + 1)
                nc.vector.tensor_reduce(r1[0][:], lg, AX.X, ALU.max).then_inc(b["lmax"], 1)
                dve.wait_ge(b["lmax"], g + 1)
                nc.vector.tensor_tensor(le[:, par], lg, r1[0][:].unsqueeze(2).to_broadcast([P, GT, E]),
                                        ALU.subtract).then_inc(b["lsub"], 1)

            ROUTE = 13

            def b_route(g, par, half):
                step = [0]

                def then(i):
                    step[0] += 1
                    i.then_inc(b["route"], 1)
                    dve.wait_ge(b["route"], ROUTE * g + step[0])

                def spread(v):
                    return v[:].unsqueeze(2).to_broadcast([P, GT, E])
                e8 = le[:, par]
                key, one1, rest, one2 = [v[:] for v in r8]
                total, m1, m2, k, den, r = r1
                dve.wait_ge(b["lexp"], g + 1)
                nc.vector.tensor_reduce(total[:], e8, AX.X, ALU.add)
                then(nc.vector.tensor_reduce(m1[:], e8, AX.X, ALU.max))
                then(nc.vector.tensor_tensor(key, e8, spread(m1), ALU.is_equal))
                then(nc.vector.tensor_tensor(key, key, desc[:], ALU.mult))
                then(nc.vector.tensor_reduce(k[:], key, AX.X, ALU.max))
                then(nc.vector.tensor_tensor(one1, key, spread(k), ALU.is_equal))
                then(nc.vector.scalar_tensor_tensor(rest, one1, -2.0, e8, ALU.mult, ALU.add))
                then(nc.vector.tensor_reduce(m2[:], rest, AX.X, ALU.max))
                nc.vector.tensor_tensor(den[:], m1[:], m2[:], ALU.add)
                then(nc.vector.tensor_tensor(key, rest, spread(m2), ALU.is_equal))
                nc.vector.scalar_tensor_tensor(den[:], total[:], 1e-8, den[:], ALU.mult, ALU.add)
                then(nc.vector.tensor_tensor(key, key, desc[:], ALU.mult))
                nc.vector.reciprocal(r[:], den[:])
                then(nc.vector.tensor_reduce(k[:], key, AX.X, ALU.max))
                then(nc.vector.tensor_tensor(one2, key, spread(k), ALU.is_equal))
                then(nc.vector.tensor_tensor(one2, one2, one1, ALU.add))
                wait(dve, b["acc"], NE * (g - 1))
                nc.vector.scalar_tensor_tensor(rest, one2, 0.5, e8, ALU.mult, ALU.mult).then_inc(b["route"], 1)
                dve.wait_ge(b["route"], ROUTE * g + ROUTE)
                nc.vector.tensor_tensor(comb[:, par], rest, spread(r), ALU.mult).then_inc(b["comb"], 1)

            def b_main(g, par, half, nxt):
                def accumulate(u):
                    w, pu = NE * g + u, (par + u) % 2
                    dve.wait_ge(b["down"], w + 1)
                    wait(dve, b["acc"], w)
                    if u == 0:
                        dve.wait_ge(b["comb"], g + 1)
                    if u == E:
                        xt = X[:, bass.ds(g * GT, GT), :] if not isinstance(g, int) else X[:, g * GT:(g + 1) * GT, :]
                        o = bank[:, 6 + pu, :].rearrange("p (t d) -> p t d", t=GT)
                        nc.vector.scalar_tensor_tensor(xt, o, 0.5, xt, ALU.mult, ALU.add).then_inc(b["acc"], 1)
                        return
                    for t in range(GT):
                        xt = X[:, g * GT + t, :]
                        i = nc.vector.scalar_tensor_tensor(xt, bank[:, 6 + pu, t * P:(t + 1) * P],
                                                           comb[:, par, t, u:u + 1], xt, ALU.mult, ALU.add)
                    i.then_inc(b["acc"], 1)

                for u in range(NE):
                    w, pu = NE * g + u, (par + u) % 2
                    dve.wait_ge(b["tanh"], w + 1)
                    nc.vector.scalar_tensor_tensor(ga[:, pu, :], th[:, pu, :], 1.0, bank[:, 2 + pu, :],
                                                   ALU.add, ALU.mult).then_inc(b["act"], 1)
                    dve.wait_ge(b["act"], w + 1)
                    dve.wait_ge(b["up"], w + 1)
                    wait(dve, b["down"], w - 1)
                    nc.vector.tensor_tensor(hT[:, pu, :], ga[:, pu, :], bank[:, 4 + pu, :], ALU.mult).then_inc(b["h"], 1)
                    if u:
                        accumulate(u - 1)
                    if u == 1:
                        nxt(0)
                    if u == 5:
                        nxt(1)
                    if u == 6:
                        nxt(2)
                accumulate(E)
            dve.wait_ge(const_ready, 3)
            steps(dve, [b_norm, b_logits, b_route], b_main)

            dve.wait_ge(wC_in, 16 * 4)
            dve.wait_ge(c["const"], 1)
            for par in range(2):
                nc.vector.tensor_scalar(kk[:, par, :, S:], memT_s[:].unsqueeze(1).to_broadcast([P, NB, M]),
                                        DK ** 0.5, None, ALU.mult)
                v = v1[M:P, par].rearrange("p b (h d) -> p b h d", h=H)
                for n in range(NB):
                    nc.vector.tensor_scalar(v[:, n, :, 0:DK], mem_s[M:P, :].rearrange("p (h d) -> p h d", h=H),
                                            M ** 0.5, None, ALU.mult)
            dve.wait_ge(b["acc"], NE * G)
            nc.vector.memset(bank[:, 7, :], 0.0).then_inc(c["memrow"], 1)

            def c_norm(g, par, half):
                dve.wait_ge(b["acc"], NE * (g + 1))
                layer_norm_rows(dve, c, g, par)
                wait(dve, c["s"], 16 * (g - 1))
                nc.vector.tensor_scalar(mrow[:, par, :], maskb[:, bass.ds(g * GW, GW)], NEG, None,
                                        ALU.mult).then_inc(c["mask"], 1)

            def c_heads(k):
                def part(g, par, half):
                    dve.wait_ge(c["qT"], g + 1)
                    wait(dve, c["s"], 16 * (g - 1))
                    for h in range(8 * k, 8 * k + 8):
                        i = nc.vector.tensor_scalar(qx[:, par, :, h * S:(h + 1) * S],
                                                    qT[:, par, :].rearrange("p (b s) -> p b s", b=NB),
                                                    cols_s[:, C_HEAD + h:C_HEAD + h + 1], None, ALU.mult)
                    if k:
                        i.then_inc(c["qx"], 1)
                return part

            def c_value(k):
                def part(g, par, half):
                    dve.wait_ge(c["v"], 2 * g + k + 1)
                    wait(dve, c["pv"], 16 * (g - 1))
                    nb = NB // 2
                    v = v1[0:S, par, k * nb:(k + 1) * nb, :].rearrange("p b (h d) -> p b h d", h=H)
                    bias = rows_s[0:S, R_XBV, :].rearrange("p (h d) -> p h d", h=H).unsqueeze(1)
                    for n in range(nb):
                        i = nc.vector.tensor_tensor(
                            v[:, n, :, 0:DK], bank[0:S, 0, n * P:(n + 1) * P].rearrange("p (h d) -> p h d", h=H),
                            rows_s[0:S, R_XBV, :].rearrange("p (h d) -> p h d", h=H), ALU.add)
                    i.then_inc(c["vS"], 1)
                return part

            def c_normalize(g, par, t):
                n = 4 * g + t
                o = bank[:, 6, :].rearrange("p (h d) -> p h d", h=H)
                dve.wait_ge(c["bt"], n + 1)
                nc.vector.reciprocal(crv[:], o[:, :, DK]).then_inc(c["rv"], 1)
                dve.wait_ge(c["rv"], n + 1)
                if t == 0:
                    wait(dve, c["otr"], g - 1)
                nc.vector.tensor_tensor(Oa[:, par, t, :].rearrange("p (h d) -> p h d", h=H), o[:, :, 0:DK],
                                        crv[:].unsqueeze(2).to_broadcast([P, H, DK]), ALU.mult).then_inc(c["on"], 1)

            def c_update(g):
                xt = X[:, bass.ds(g * GT, GT), :]
                dve.wait_ge(c["wo"], g + 1)
                nc.vector.tensor_tensor(xt, xt, bank[:, 0, :].rearrange("p (t d) -> p t d", t=GT),
                                        ALU.add).then_inc(c["xa"], 1)
                dve.wait_ge(c["xa"], g + 1)
                nc.vector.tensor_tensor(xt, xt, rows_s[:, R_XBO:R_XBO + 1, :].to_broadcast([P, GT, P]),
                                        ALU.add).then_inc(c["xo"], 1)

            def c_main(g, par, half, nxt):
                first = isinstance(g, int) and g == 0
                for j in range(16):
                    w, r = 16 * g + j, j % 4
                    s = bank[:, 2 + r, :].rearrange("p (u k) -> p u k", u=4)
                    dve.wait_ge(c["s"], w + 1)
                    nc.vector.tensor_reduce(cmx[:, j % 2, :], s, AX.X, ALU.max).then_inc(c["mx"], 1)
                    dve.wait_ge(c["mx"], w + 1)
                    wait(dve, c["exp"], w - 1)
                    nc.vector.tensor_tensor(csub[:, j % 2], s, cmx[:, j % 2, :].unsqueeze(2).to_broadcast([P, 4, P]),
                                            ALU.subtract).then_inc(c["sub"], 1)
                    if j == 2 and not first:
                        c_normalize(g - 1, 1 - par, 3)
                    if j == 3:
                        nxt(0)
                    if j == 5 and not first:
                        c_update(g - 1)
                    if j in (6, 10, 14):
                        c_normalize(g, par, j // 4 - 1)
                    if j == 8:
                        nxt(1)
                    if j == 9:
                        nxt(2)
                    if j == 12:
                        nxt(3)
                    if j == 13:
                        nxt(4)
            steps(dve, [c_norm, c_heads(0), c_heads(1), c_value(0), c_value(1)], c_main)
            c_normalize(G - 1, 1, 3)
            c_update(G - 1)

            dve.wait_ge(d["const"], 2)

            def d_norm(g, par, half):
                dve.wait_ge(d["x"][par], 32 * (half + 1))
                wait(dve, d["normed"], g - 1)
                layer_norm_rows(dve, dn, g, par, lambda g, t: xg[:, par, t, :])

            def d_value(g, par, half):
                dve.wait_ge(d["v"], g + 1)
                wait(dve, d["pv"], 4 * (g - 1))
                bias = rows_s[:, R_QKVBV, :].rearrange("p (h d) -> p h d", h=H4)
                for t in range(GT):
                    i = nc.vector.tensor_tensor(
                        v4[:, par, t, :].rearrange("p (h d) -> p h d", h=H4)[:, :, 0:D4],
                        bank[:, 1, t * P:(t + 1) * P].rearrange("p (h d) -> p h d", h=H4), bias, ALU.add)
                i.then_inc(d["vS"], 1)

            def d_route(g):
                lg = bank[:, 3, 0:GT * E].rearrange("p (t e) -> p t e", t=GT)
                key = r8[0][:]
                dve.wait_ge(d["logit"], g + 1)
                nc.vector.tensor_reduce(r1[0][:], lg, AX.X, ALU.max).then_inc(d["route"], 1)
                dve.wait_ge(d["route"], 5 * g + 1)
                nc.vector.tensor_tensor(key, lg, r1[0][:].unsqueeze(2).to_broadcast([P, GT, E]),
                                        ALU.is_equal).then_inc(d["route"], 1)
                dve.wait_ge(d["route"], 5 * g + 2)
                nc.vector.tensor_tensor(key, key, desc[:], ALU.mult).then_inc(d["route"], 1)
                dve.wait_ge(d["route"], 5 * g + 3)
                nc.vector.tensor_reduce(r1[1][:], key, AX.X, ALU.max).then_inc(d["route"], 1)
                dve.wait_ge(d["route"], 5 * g + 4)
                nc.vector.tensor_tensor(mall[:, bass.ds(g * GT, GT), :], key,
                                        r1[1][:].unsqueeze(2).to_broadcast([P, GT, E]),
                                        ALU.is_equal).then_inc(d["route"], 1)

            def d_main(g, par, half, nxt):
                for m in range(2):
                    s = bank[:, 4 + m, :].rearrange("p (u k) -> p u k", k=S)
                    dve.wait_ge(d["s"], 2 * g + m + 1)
                    nc.vector.tensor_reduce(dmx[:, m, :], s, AX.X, ALU.max).then_inc(d["mx"], 1)
                    dve.wait_ge(d["mx"], 2 * g + m + 1)
                    wait(dve, d["exp"], 2 * g + m - 1)
                    nc.vector.tensor_tensor(dsub[:, m], s, dmx[:, m, :].unsqueeze(2).to_broadcast([P, 8, S]),
                                            ALU.subtract).then_inc(d["sub"], 1)
                nxt(0)
                if not (isinstance(g, int) and g == 0):
                    d_route(g - 1)
                for m in range(2):
                    o = bank[:, 2 + m, 0:8 * (D4 + 1)].rearrange("p (h t d) -> p h t d", h=2, t=GT)
                    dve.wait_ge(d["pv"], 4 * g + 2 * m + 2)
                    nc.vector.reciprocal(drv[:, m].rearrange("p (h t) -> p h t", h=2), o[:, :, :, D4]).then_inc(d["rv"], 1)
                    dve.wait_ge(d["rv"], 2 * g + m + 1)
                    wait(dve, d["otr"], g)
                    for h in range(2):
                        i = nc.vector.tensor_tensor(
                            dOa[:, :, (2 * m + h) * D4:(2 * m + h + 1) * D4], o[:, h, :, 0:D4],
                            drv[:, m, h * GT:(h + 1) * GT].unsqueeze(2).to_broadcast([P, GT, D4]), ALU.mult)
                    i.then_inc(d["on"], 1)
                dve.wait_ge(d["wo"], g + 1)
                nc.vector.tensor_tensor(z, xn[:, par], bank[:, 3, :].rearrange("p (t d) -> p t d", t=GT),
                                        ALU.add).then_inc(d["z"], 1)
                dve.wait_ge(d["z"], 2 * g + 1)
                nc.vector.tensor_tensor(z, z, rows_s[:, R_BO:R_BO + 1, :].to_broadcast([P, GT, P]),
                                        ALU.add).then_inc(d["z"], 1)
                dve.wait_ge(d["z"], 2 * g + 2)
                layer_norm_affine(dve, d, g, par, lambda t: z[:, t, :], ys[:, par], R_G1, R_BE1)
                nxt(1)
            steps(dve, [d_norm, d_value], d_main)
            d_route(G - 1)

            count = [0]

            def then(i):
                count[0] += 1
                i.then_inc(r_step, 1)
                dve.wait_ge(r_step, count[0])
            rank = bank[:, 0, 0:E * T].rearrange("p (e t) -> p e t", e=E)
            total = bank[:, 1, 0:E * T]
            has = mall[:].rearrange("p t e -> p e t")
            n_e, used, upto, adjust, n_tmp = [v[:] for v in n8]
            dve.wait_ge(r_sums, 2)
            dve.wait_ge(io_ready, 3)
            then(nc.vector.tensor_tensor_scan(cum[:].rearrange("p e t -> p (e t)"), ones[:, 0:E * T], total, 0.0,
                                              ALU.mult, ALU.add))
            then(nc.vector.tensor_tensor(cumx[:], cum[:], total.rearrange("p (e t) -> p e t", e=E), ALU.subtract))
            then(nc.vector.tensor_tensor(n_e, cum[:, :, T - 1], cumx[:, :, 0], ALU.subtract))
            then(nc.vector.tensor_tensor(pos[:], n_e.unsqueeze(2).to_broadcast([P, E, T]),
                                         starts[:].unsqueeze(1).to_broadcast([P, E, T]), ALU.is_gt))
            then(nc.vector.tensor_reduce(used, pos[:], AX.X, ALU.add))
            then(nc.vector.tensor_tensor_scan(upto, ones[:, 0:E], used, 0.0, ALU.mult, ALU.add))
            then(nc.vector.tensor_tensor(n_tmp, upto, used, ALU.subtract))
            nc.vector.tensor_tensor(big8[:], upto.unsqueeze(1).to_broadcast([P, NT, E]),
                                    tiles[:].unsqueeze(2).to_broadcast([P, NT, E]), ALU.is_le)
            then(nc.vector.scalar_tensor_tensor(adjust, n_tmp, float(P), cumx[:, :, 0], ALU.mult, ALU.subtract))
            nc.vector.tensor_reduce(tef[:], big8[:], AX.X, ALU.add)
            then(nc.vector.tensor_tensor(pos[:], rank, cumx[:], ALU.add))
            then(nc.vector.tensor_tensor(pos[:], pos[:], adjust.unsqueeze(2).to_broadcast([P, E, T]), ALU.add))
            nc.vector.tensor_scalar(te[:], tef[:], float(E - 1), None, ALU.min)
            then(nc.vector.tensor_tensor(pos[:], pos[:], has, ALU.mult))
            then(nc.vector.tensor_reduce(slotf[:], pos[:].rearrange("p e t -> p t e"), AX.X, ALU.add))
            nc.vector.tensor_copy(slot[:], slotf[:]).then_inc(slots_ready, 1)

            dve.wait_ge(slots_ready, 1)

            def m_hidden(j, par):
                expert = dve.value_load(te[0:1, bass.ds(j, 1)], min_val=0, max_val=E - 1)
                dve.wait_ge(m["h"], j + 1)
                wait(dve, m["htr"], j - 1)
                nc.vector.tensor_tensor(he[par], bank[:, 1 + par, :], b1_s[:, bass.ds(expert * 4 * P, 4 * P)],
                                        ALU.add).then_inc(m["hb"], 1)

            def m_output(j, par, half):
                expert = dve.value_load(te[0:1, bass.ds(j, 1)], min_val=0, max_val=E - 1)
                dve.wait_ge(m["up"], j + 1)
                wait(dve, m["out"][par], 16 * half)
                nc.vector.tensor_tensor(oe[par], bank[:, 5 + par, 0:P], b2_s[:, bass.ds(expert * P, P)],
                                        ALU.add).then_inc(m["o"], 1)

            def m_step(j, par, half, left):
                if left > 1:
                    m_hidden(j + 1, 1 - par)
                m_output(j, par, half)
            m_hidden(0, 0)
            tile_steps(dve, m_step)

            def e_main(g, par, half, nxt):
                dve.wait_ge(e["rows"][par], 16 * GT * (half + 1))
                nc.vector.tensor_tensor(z, og[:, bass.ds(g * GT, GT), :], X[:, bass.ds(g * GT, GT), :],
                                        ALU.add).then_inc(e["add"], 1)
                dve.wait_ge(e["add"], g + 1)
                layer_norm_affine(dve, e, g, par, lambda t: z[:, t, :], xn[:, par], R_G2, R_BE2)
                dve.wait_ge(e["normed"], g + 1)
                dve.wait_ge(e["x"][par], 32 * (half + 1))
                wait(dve, e["out"][par], 32 * half)
                nc.vector.tensor_tensor(yo[:, par], xn[:, par], xr[:, par], ALU.add).then_inc(e["y"], 1)
            steps(dve, [], e_main)

        @block.scalar
        def _(act):
            def a_xT(g, par, half):
                act.wait_ge(a["tr"], g + 1)
                wait(act, a["q"], g - 1)
                nc.scalar.copy(xnT[:, par, :], bank[:, 0, :]).then_inc(a["xnT"], 1)
                act.wait_ge(a["k"], g + 1)
                nc.scalar.activation(kT[:, par, :], bank[:, 2, :], ACT.Identity,
                                     bias=cols_s[:, C_BK:C_BK + 1]).then_inc(a["kT"], 1)

            def a_qT(g, par, half):
                act.wait_ge(a["q"], g + 1)
                nc.scalar.activation(qT[:, par, :], bank[:, 1, :], ACT.Identity,
                                     bias=cols_s[:, C_BQ:C_BQ + 1]).then_inc(a["qT"], 1)

            def a_main(g, par, half, nxt):
                act.wait_ge(a["sub"], g + 1)
                for n in range(2):
                    h = slice(n * S, (n + 1) * S)
                    i = nc.scalar.activation(pbd[h, par, :, n * S:(n + 1) * S], ss[h, par], ACT.Exp, scale=P ** -0.5)
                i.then_inc(a["exp"], 1)
                nxt(0)
                act.wait_ge(a["ptr"], g + 1)
                wait(act, a["o"], g - 1)
                nc.scalar.copy(pT[:, par].rearrange("p t k -> p (t k)"), bank[:, 5, :]).then_inc(a["pT"], 1)
                nxt(1)
            act.wait_ge(w_in, 16 * 3)
            act.wait_ge(const_ready, 2)
            steps(act, [a_xT, a_qT], a_main)

            def b_xT(g, par, half):
                act.wait_ge(b["tr"], g + 1)
                wait(act, b["up"], NE * (g - 1))
                nc.scalar.copy(xnT[:, par, :], bank[:, 0, :]).then_inc(b["xnT"], 1)

            def b_exp(g, par, half):
                act.wait_ge(b["lsub"], g + 1)
                nc.scalar.activation(le[:, par], le[:, par], ACT.Exp).then_inc(b["lexp"], 1)

            def b_main(g, par, half, nxt):
                for u in range(NE):
                    w, pu = NE * g + u, (par + u) % 2
                    act.wait_ge(b["gate"], w + 1)
                    wait(act, b["act"], w - 1)
                    nc.scalar.activation(th[:, pu, :], bank[:, 2 + pu, :], ACT.Tanh, scale=0.5).then_inc(b["tanh"], 1)
                    if u == 4:
                        nxt(0)
                    if u == 6:
                        nxt(1)
            steps(act, [b_xT, b_exp], b_main)

            act.wait_ge(c["memrow"], 1)

            def c_xT(g, par, half):
                act.wait_ge(c["tr"], g + 1)
                wait(act, c["q"], g - 1)
                nc.scalar.copy(xnT[:, par, :], bank[:, 0, :]).then_inc(c["xnT"], 1)

            def c_qT(g, par, half):
                act.wait_ge(c["q"], g + 1)
                wait(act, c["qx"], g - 1)
                nc.scalar.activation(qT[:, par, :], bank[:, 0, :], ACT.Identity,
                                     bias=cols_s[:, C_XBQ:C_XBQ + 1]).then_inc(c["qT"], 1)

            def c_kT(g, par, half):
                act.wait_ge(c["k"], g + 1)
                nc.scalar.activation(kk[:, par, :, 0:S], bank[:, 0, :].rearrange("p (b s) -> p b s", b=NB),
                                     ACT.Identity, bias=cols_s[:, C_XBK:C_XBK + 1]).then_inc(c["kT"], 1)

            def c_turned(w, j):
                act.wait_ge(c["ptr"], w + 1)
                wait(act, c["pv"], w - 1)
                nc.scalar.copy(cPT[:, j % 2, :], bank[:, 1 if j % 2 else 6, :]).then_inc(c["pT"], 1)

            def c_outputs(n):
                act.wait_ge(c["pv"], 4 * n + 4)
                wait(act, c["bt"], n)
                nc.scalar.copy(cO, bank[:, 7, :]).then_inc(c["oc"], 1)

            def c_oT(g):
                act.wait_ge(c["otr"], g + 1)
                wait(act, c["wo"], g)
                nc.scalar.copy(cOT[:], bank[:, 6, :]).then_inc(c["oT"], 1)

            def c_main(g, par, half, nxt):
                first = isinstance(g, int) and g == 0
                for j in range(16):
                    w = 16 * g + j
                    if j % 4 == 1 and not (first and j == 1):
                        c_outputs(4 * g + j // 4 - 1)
                    act.wait_ge(c["sub"], w + 1)
                    wait(act, c["ptr"], w - 1)
                    nc.scalar.activation(cP[:, j % 2], csub[:, j % 2], ACT.Exp, scale=DK ** -0.5).then_inc(c["exp"], 1)
                    if j or not first:
                        c_turned(w - 1, (j - 1) % 16)
                    if j == 3 and not first:
                        c_oT(g - 1)
                    if j == 6:
                        nxt(0)
                    if j == 8:
                        nxt(1)
                    if j == 10:
                        nxt(2)
            steps(act, [c_xT, c_qT, c_kT], c_main)
            c_turned(16 * G - 1, 15)
            c_outputs(4 * G - 1)
            c_oT(G - 1)

            act.wait_ge(wF_in, 16 * 5)
            act.wait_ge(d["const"], 2)

            def d_xT(g, par, half):
                act.wait_ge(dn["tr"], g + 1)
                wait(act, d["v"], g - 1)
                nc.scalar.copy(xnT[:, par, :], bank[:, 0, :]).then_inc(d["xnT"], 1)

            def d_qT(g, par, half):
                act.wait_ge(d["q"], g + 1)
                wait(act, d["s"], 2 * (g - 1))
                for h in range(H4):
                    i = nc.scalar.activation(q4[:, par, h, :], bank[:, 1, :], ACT.Identity, bias=dbq[:, h:h + 1],
                                             scale=cols_s[:, C_HEAD4 + h:C_HEAD4 + h + 1])
                i.then_inc(d["qT"], 1)
                act.wait_ge(d["k"], g + 1)
                nc.scalar.activation(kT[:, par, :], bank[:, 0, :], ACT.Identity,
                                     bias=cols_s[:, C_MBK:C_MBK + 1]).then_inc(d["kT"], 1)

            def d_yT(g):
                act.wait_ge(d["ytr"], g + 1)
                wait(act, d["logit"], g)
                nc.scalar.copy(yT, bank[:, 3, :]).then_inc(d["yT"], 1)

            def d_main(g, par, half, nxt):
                for m in range(2):
                    act.wait_ge(d["sub"], 2 * g + m + 1)
                    wait(act, d["ptr"], 4 * (g - 1) + 2 * m + 2)
                    for n in range(2):
                        h = slice(n * S, (n + 1) * S)
                        i = nc.scalar.activation(dP[h, 8 * m:8 * m + 8, n * S:(n + 1) * S], dsub[h, m], ACT.Exp,
                                                 scale=D4 ** -0.5)
                    i.then_inc(d["exp"], 1)
                if not (isinstance(g, int) and g == 0):
                    d_yT(g - 1)
                for h in range(H4):
                    w = 4 * g + h
                    act.wait_ge(d["ptr"], w + 1)
                    wait(act, d["pv"], w - 1)
                    nc.scalar.copy(cPT[:, h % 2, :], bank[:, 6 + h % 2, :]).then_inc(d["pT"], 1)
                    if h == 1:
                        nxt(0)
                act.wait_ge(d["otr"], g + 1)
                wait(act, d["wo"], g)
                nc.scalar.copy(cOT[:], bank[:, 2, :]).then_inc(d["oT"], 1)
                nxt(1)
            nc.scalar.activation(dbq[:], cols_s[:, C_HEAD4:C_HEAD4 + 4], ACT.Copy,
                                 scale=cols_s[:, C_MBQ:C_MBQ + 1]).then_inc(d["bq"], 1)
            act.wait_ge(d["bq"], 1)
            steps(act, [d_xT, d_qT], d_main)

            d_yT(G - 1)

            def m_xT(j, par):
                act.wait_ge(m["tr"], j + 1)
                wait(act, m["h"], j - 1)
                nc.scalar.copy(xeT[par], bank[:, 0, 0:P]).then_inc(m["xT"], 1)

            def m_step(j, par, half, left):
                act.wait_ge(m["htr"], j + 1)
                wait(act, m["up"], j - 1)
                nc.scalar.activation(heT[par], bank[:, 3 + par, :], ACT.Relu).then_inc(m["hT"], 1)
                if left > 2:
                    m_xT(j + 2, par)
            m_xT(0, 0)
            m_xT(1, 1)
            tile_steps(act, m_step)

        @block.tensor
        def _(pe):
            def a_kv(g, par, half):
                pe.wait_ge(a["xn"], g + 1)
                wait(pe, a["xnT"], g)
                transpose_xn(pe, a, g, par)
                pe.wait_ge(a["ctx"][par], 16 * (half + 1))
                wait(pe, a["kT"], g)
                nc.tensor.matmul(bank[:, 2, :], wA_s[:, WK, :], ctxb[:, par, :], start=True, stop=True).then_inc(a["k"], 1)
                wait(pe, a["vS"], g)
                for t in range(GT):
                    i = nc.tensor.matmul(bank[:, 3, t * P:(t + 1) * P], ctxb[:, par, t * P:(t + 1) * P],
                                         wA_s[:, WV, :], start=True, stop=True)
                i.then_inc(a["v"], 1)

            def a_q(g, par, half):
                pe.wait_ge(a["xnT"], g + 1)
                wait(pe, a["qT"], g)
                nc.tensor.matmul(bank[:, 1, :], wA_s[:, WQ, :], xnT[:, par, :], start=True, stop=True).then_inc(a["q"], 1)

            def a_main(g, par, half, nxt):
                pe.wait_ge(a["qT"], g + 1)
                pe.wait_ge(a["kT"], g + 1)
                wait(pe, a["sub"], g)
                for t in range(GT):
                    for n in range(2):
                        k = (2 * t + n) * S
                        i = nc.tensor.matmul(bank[n * S:(n + 1) * S, 4, t * S:(t + 1) * S], qT[:, par, k:k + S],
                                             kT[:, par, k:k + S], start=True, stop=True)
                i.then_inc(a["s"], 1)
                nxt(0)
                pe.wait_ge(a["exp"], g + 1)
                wait(pe, a["pT"], g)
                for t in range(GT):
                    i = nc.tensor.transpose(bank[:, 5, t * P:(t + 1) * P], pbd[:, par, t, :], ident[:])
                i.then_inc(a["ptr"], 1)
                nxt(1)
                pe.wait_ge(a["pT"], g + 1)
                pe.wait_ge(a["vS"], g + 1)
                wait(pe, a["xo"], g)
                for t in range(GT):
                    i = nc.tensor.matmul(bank[:, 6, t * P:(t + 1) * P], pT[:, par, t, :], vS[:, par, t, :],
                                         start=True, stop=True)
                i.then_inc(a["o"], 1)
            pe.wait_ge(w_in, 16 * 3)
            pe.wait_ge(id_ready, 1)
            steps(pe, [a_kv, a_q], a_main)

            pe.wait_ge(a["xo"], G)
            pe.wait_ge(wB_in, 16)

            def b_turn(g, par, half):
                pe.wait_ge(b["xn"], g + 1)
                wait(pe, b["xnT"], g)
                transpose_xn(pe, b, g, par)

            def b_router(g, par, half):
                pe.wait_ge(b["xnT"], g + 1)
                wait(pe, b["lsub"], g)
                for t in range(GT):
                    i = nc.tensor.matmul(bank[:, 1, t * E:(t + 1) * E], xnT[:, par, t * P:(t + 1) * P], wrouter,
                                         start=True, stop=True)
                i.then_inc(b["logit"], 1)

            def b_main(g, par, half, nxt):
                def down(u):
                    w, pu = NE * g + u, (par + u) % 2
                    pe.wait_ge(b["h"], w + 1)
                    wait(pe, b["acc"], w - 1)
                    for t in range(GT):
                        i = nc.tensor.matmul(bank[:, 6 + pu, t * P:(t + 1) * P], hT[:, pu, t * P:(t + 1) * P],
                                             wdown[:, u, :], start=True, stop=True)
                    i.then_inc(b["down"], 1)

                if isinstance(g, int):
                    pe.wait_ge(b["xnT"], g + 1)
                for u in range(NE):
                    w, pu = NE * g + u, (par + u) % 2
                    wait(pe, b["act"], w - 1)
                    nc.tensor.matmul(bank[:, 2 + pu, :], wgate[:, u, :], xnT[:, par, :], start=True,
                                     stop=True).then_inc(b["gate"], 1)
                    wait(pe, b["h"], w - 1)
                    nc.tensor.matmul(bank[:, 4 + pu, :], wup[:, u, :], xnT[:, par, :], start=True,
                                     stop=True).then_inc(b["up"], 1)
                    if u:
                        down(u - 1)
                    if u == 3:
                        nxt(0)
                    if u == 5:
                        nxt(1)
                down(E)
            steps(pe, [b_turn, b_router], b_main)

            pe.wait_ge(b["acc"], NE * G)
            pe.wait_ge(c["memrow"], 1)

            def c_turn(g, par, half):
                pe.wait_ge(c["xn"], g + 1)
                wait(pe, c["xo"], g - 1)
                wait(pe, c["vS"], 2 * g)
                transpose_xn(pe, c, g, par)

            def c_q(g, par, half):
                pe.wait_ge(c["xnT"], g + 1)
                nc.tensor.matmul(bank[:, 0, :], wC_s[:, 0, :], xnT[:, par, :], start=True, stop=True).then_inc(c["q"], 1)

            def c_k(g, par, half):
                pe.wait_ge(c["ctx"][par], 16 * (half + 1))
                pe.wait_ge(c["qT"], g + 1)
                nc.tensor.matmul(bank[:, 0, :], wC_s[:, 1, :], ctxb[:, par, :], start=True, stop=True).then_inc(c["k"], 1)

            def c_v(k):
                def part(g, par, half):
                    pe.wait_ge(c["kT"], g + 1)
                    if k:
                        pe.wait_ge(c["vS"], 2 * g + 1)
                    for n in range(NB // 2):
                        m = (k * NB // 2 + n) * S
                        i = nc.tensor.matmul(bank[0:S, 0, n * P:(n + 1) * P], ctxb[:, par, m:m + S], wC_s[:, 2, :],
                                             start=True, stop=True)
                    i.then_inc(c["v"], 1)
                return part

            def c_scores(g, par, j):
                t, r = j // 4, j % 4
                w = 16 * g + j
                wait(pe, c["sub"], w - 3)
                pe.wait_ge(c["qx"], g + 1)
                pe.wait_ge(c["kT"], g + 1)
                pe.wait_ge(c["mask"], g + 1)
                o = bank[:, 2 + r, :].rearrange("p (b u k) -> p b u k", b=2, u=2)
                m = mrow[0:1, par, t * P:(t + 1) * P].rearrange("p (b s) -> p b s", b=2)
                nc.tensor.matmul(o[:, :, :, 0:S], onesb[0:1, :], m.unsqueeze(2).to_broadcast([1, 2, 2, S]),
                                 start=True, stop=False, skip_group_check=True)
                for b1 in range(2):
                    for u in range(2):
                        i = nc.tensor.matmul(o[:, b1, u, :],
                                             qx[:, par, 2 * t + b1, (2 * r + u) * P:(2 * r + u + 1) * P],
                                             kk[:, par, 2 * t + b1, :], start=False,
                                             stop=(b1 == 1 and u == 1), skip_group_check=True)
                i.then_inc(c["s"], 1)

            def c_pv(w, j, par, tiles):
                t, r = j // 4, j % 4
                pe.wait_ge(c["pT"], w + 1)
                wait(pe, c["oc"], tiles)
                for b1 in range(2):
                    for hh in range(4):
                        i = nc.tensor.matmul(bank[32 * hh:32 * hh + VW, 7, r * P + b1 * S:r * P + b1 * S + S],
                                             v1[:, par, 2 * t + b1, (4 * r + hh) * VW:(4 * r + hh + 1) * VW],
                                             cPT[:, j % 2, (4 * b1 + hh) * S:(4 * b1 + hh + 1) * S],
                                             start=True, stop=True)
                i.then_inc(c["pv"], 1)

            def c_back(n):
                pe.wait_ge(c["oc"], n + 1)
                for r in range(4):
                    i = nc.tensor.transpose(bank[:, 6, r * P:(r + 1) * P], cO[:, r * P:(r + 1) * P], ident[:])
                i.then_inc(c["bt"], 1)

            def c_otrans(g, par):
                pe.wait_ge(c["on"], 4 * (g + 1))
                for t in range(GT):
                    i = nc.tensor.transpose(bank[:, 6, t * P:(t + 1) * P], Oa[:, par, t, :], ident[:])
                i.then_inc(c["otr"], 1)

            def c_out(g):
                pe.wait_ge(c["oT"], g + 1)
                for t in range(GT):
                    i = nc.tensor.matmul(bank[:, 0, t * P:(t + 1) * P], cOT[:, t * P:(t + 1) * P], wC_s[:, 3, :],
                                         start=True, stop=True)
                i.then_inc(c["wo"], 1)

            def c_main(g, par, half, nxt):
                first = isinstance(g, int) and g == 0
                last = isinstance(g, int) and g == G - 1
                if first:
                    pe.wait_ge(c["vS"], 2)
                    for j in range(4):
                        c_scores(g, par, j)
                for j in range(16):
                    w = 16 * g + j
                    if j == 4:
                        wait(pe, c["oT"], g)
                    if j % 4 == 2 and not (first and j == 2):
                        wait(pe, c["on"], 4 * g + j // 4)
                    pe.wait_ge(c["exp"], w + 1)
                    wait(pe, c["pT"], w - 1)
                    for u in range(4):
                        i = nc.tensor.transpose(bank[:, 1 if j % 2 else 6, u * P:(u + 1) * P], cP[:, j % 2, u, :],
                                                ident[:])
                    i.then_inc(c["ptr"], 1)
                    if j:
                        pe.wait_ge(c["vS"], 2 * g + 2)
                        c_pv(w - 1, j - 1, par, 4 * g + (j - 1) // 4)
                    elif not first:
                        c_pv(w - 1, 15, 1 - par, 4 * g - 1)
                    if j == 2 and not first:
                        pe.wait_ge(c["pT"], w + 1)
                        c_otrans(g - 1, 1 - par)
                    if j == 3 and not first:
                        pe.wait_ge(c["vS"], 2 * g + 2)
                        c_out(g - 1)
                    if j == 5:
                        nxt(0)
                    if j == 7:
                        nxt(1)
                    if j == 9:
                        nxt(2)
                    if j == 11:
                        nxt(3)
                    if j == 12:
                        nxt(4)
                    if j < 12:
                        c_scores(g, par, j + 4)
                    elif not last:
                        c_scores(g + 1, 1 - par, j - 12)
                    if j % 4 == 1 and not (first and j == 1):
                        c_back(4 * g + j // 4 - 1)
            steps(pe, [c_turn, c_q, c_k, c_v(0), c_v(1)], c_main)
            pe.wait_ge(c["pT"], 16 * G)
            c_pv(16 * G - 1, 15, 1, 4 * G - 1)
            c_back(4 * G - 1)
            c_otrans(G - 1, 1)
            c_out(G - 1)

            pe.wait_ge(c["xo"], G)
            pe.wait_ge(wF_in, 16 * 5)

            def d_turn(g, par, half):
                pe.wait_ge(dn["xn"], g + 1)
                wait(pe, d["kT"], g)
                transpose_xn(pe, dn, g, par)
                wait(pe, d["vS"], g)
                pe.wait_ge(d["xnT"], g + 1)
                nc.tensor.matmul(bank[:, 1, :], wF_s[:, 0:P], xnT[:, par, :], start=True, stop=True).then_inc(d["q"], 1)
                nc.tensor.matmul(bank[:, 0, :], wF_s[:, P:2 * P], xnT[:, par, :], start=True, stop=True).then_inc(d["k"], 1)

            def d_v(g, par, half):
                pe.wait_ge(d["qT"], g + 1)
                for t in range(GT):
                    i = nc.tensor.matmul(bank[:, 1, t * P:(t + 1) * P], xnT[:, par, t * P:(t + 1) * P],
                                         wF_s[:, 2 * P:3 * P], start=True, stop=True)
                i.then_inc(d["v"], 1)

            def d_router(g, par):
                pe.wait_ge(d["normed"], g + 1)
                for t in range(GT):
                    i = nc.tensor.transpose(bank[:, 3, t * P:(t + 1) * P], ys[:, par, t, :], ident[:])
                i.then_inc(d["ytr"], 1)
                pe.wait_ge(d["yT"], g + 1)
                for t in range(GT):
                    i = nc.tensor.matmul(bank[:, 3, t * E:(t + 1) * E], yT[:, t * P:(t + 1) * P], wF_s[:, 4 * P:],
                                         start=True, stop=True)
                i.then_inc(d["logit"], 1)

            def d_main(g, par, half, nxt):
                pe.wait_ge(d["kT"], g + 1)
                wait(pe, d["sub"], 2 * g)
                for m in range(2):
                    for h in range(2):
                        for t in range(GT):
                            for n in range(2):
                                k = (2 * t + n) * S
                                i = nc.tensor.matmul(
                                    bank[n * S:(n + 1) * S, 4 + m, (h * GT + t) * S:(h * GT + t + 1) * S],
                                    q4[:, par, 2 * m + h, k:k + S], kT[:, par, k:k + S], start=True, stop=True)
                    i.then_inc(d["s"], 1)
                if not (isinstance(g, int) and g == 0):
                    d_router(g - 1, 1 - par)

                def pv(h):
                    w = 4 * g + h
                    pe.wait_ge(d["pT"], w + 1)
                    pe.wait_ge(d["vS"], g + 1)
                    wait(pe, d["z"], 2 * g - 1)
                    if h >= 2:
                        wait(pe, d["route"], 5 * g - 3)
                    for t in range(GT):
                        k = (h % 2 * GT + t) * (D4 + 1)
                        i = nc.tensor.matmul(bank[:, 2 + h // 2, k:k + D4 + 1], cPT[:, h % 2, t * P:(t + 1) * P],
                                             v4[:, par, t, h * (D4 + 1):(h + 1) * (D4 + 1)], start=True, stop=True)
                    i.then_inc(d["pv"], 1)
                for h in range(H4):
                    w = 4 * g + h
                    if h % 2 == 0:
                        pe.wait_ge(d["exp"], 2 * g + h // 2 + 1)
                    wait(pe, d["pT"], w - 1)
                    for t in range(GT):
                        i = nc.tensor.transpose(bank[:, 6 + h % 2, t * P:(t + 1) * P], dP[:, h * GT + t, :], ident[:])
                    i.then_inc(d["ptr"], 1)
                    if h:
                        pv(h - 1)
                    if h == 1:
                        nxt(0)
                pv(3)
                pe.wait_ge(d["on"], 2 * g + 2)
                for t in range(GT):
                    i = nc.tensor.transpose(bank[:, 2, t * P:(t + 1) * P], dOa[:, t, :], ident[:])
                i.then_inc(d["otr"], 1)
                pe.wait_ge(d["oT"], g + 1)
                for t in range(GT):
                    i = nc.tensor.matmul(bank[:, 3, t * P:(t + 1) * P], cOT[:, t * P:(t + 1) * P], wF_s[:, 3 * P:4 * P],
                                         start=True, stop=True)
                i.then_inc(d["wo"], 1)
                nxt(1)
            steps(pe, [d_turn, d_v], d_main)

            d_router(G - 1, 1)

            pe.wait_ge(d["route"], 5 * G)
            pe.wait_ge(io_ready, 3)
            has = mall[:].rearrange("p t e -> p e t")
            for n, w in enumerate((before[:], ones[:, 0:P])):
                nc.tensor.matmul(bank[:, n, 0:E * T], w, has, start=True, stop=True).then_inc(r_sums, 1)

            pe.wait_ge(slots_ready, 1)

            def m_turn(j, par, half):
                pe.wait_ge(m["x"][par], 16 * (half + 1))
                wait(pe, m["xT"], j)
                nc.tensor.transpose(bank[:, 0, 0:P], xe[par], ident[:]).then_inc(m["tr"], 1)

            def m_up(j, par):
                expert = pe.value_load(te[0:1, bass.ds(j, 1)], min_val=0, max_val=E - 1)
                pe.wait_ge(m["xT"], j + 1)
                wait(pe, m["hb"], j - 1)
                nc.tensor.matmul(bank[:, 1 + par, :], xeT[par], w1_s[:, bass.ds(expert * 4 * P, 4 * P)],
                                 start=True, stop=True).then_inc(m["h"], 1)

            def m_step(j, par, half, left):
                pe.wait_ge(m["hb"], j + 1)
                wait(pe, m["hT"], j - 1)
                for k in range(4):
                    i = nc.tensor.transpose(bank[:, 3 + par, k * P:(k + 1) * P], he[par][:, k * P:(k + 1) * P],
                                            ident[:])
                i.then_inc(m["htr"], 1)
                if left > 1:
                    m_up(j + 1, 1 - par)
                if left > 2:
                    m_turn(j + 2, par, half + 1)
                expert = pe.value_load(te[0:1, bass.ds(j, 1)], min_val=0, max_val=E - 1)
                pe.wait_ge(m["hT"], j + 1)
                wait(pe, m["o"], j - 1)
                for k in range(4):
                    i = nc.tensor.matmul(bank[:, 5 + par, 0:P], heT[par][:, k * P:(k + 1) * P],
                                         w2_s[:, bass.ds((expert * 4 + k) * P, P)], start=(k == 0), stop=(k == 3))
                i.then_inc(m["up"], 1)
            m_turn(0, 0, 0)
            m_turn(1, 1, 0)
            m_up(0, 0)
            tile_steps(pe, m_step)


def kernel(**inputs):
    import concourse.bacc as bacc
    from concourse.bass_utils import run_bass_kernel_spmd

    a = {k: np.asarray(v) for k, v in inputs.items()}
    cat = lambda parts: np.ascontiguousarray(np.concatenate([p.reshape(P, -1) for p in parts], axis=1))
    bqkv = a["L1_ffn_bqkv"].reshape(3, P)
    arrays = {
        "x": np.ascontiguousarray(a["x"].reshape(N, P)),
        "ctxT": np.ascontiguousarray(a["ctx_1024"].reshape(N, P).T),
        "maskrow": np.ascontiguousarray(a["mask_Bx1x1xS2_bk0"].reshape(1, N)),
        "wA": cat([a["L0_xattn_Wq"], a["L0_xattn_Wk"], a["L0_xattn_Wv"]]),
        "wB": cat([a["L0_ffn_Wg"].transpose(2, 0, 1), a["L0_ffn_Sg"].T, a["L0_ffn_Wu"].transpose(2, 0, 1),
                   a["L0_ffn_Su"].T, a["L0_ffn_Wd"].transpose(2, 0, 1), a["L0_ffn_Sd"].T, a["L0_ffn_Wr"].T]),
        "wC": cat([a["L1_xattn_Wq"].T, a["L1_xattn_Wk"].T, a["L1_xattn_Wv"].T, a["L1_xattn_Wo"].T]),
        "memT": np.ascontiguousarray(a["L1_xattn_m_k"][0].T),
        "mem": np.ascontiguousarray(a["L1_xattn_m_v"][0]),
        "wF": cat([a["L1_ffn_Wqkv"].T, a["L1_ffn_Wo"].T, a["L1_ffn_Wg"].T]),
        "w1": cat([a["L1_ffn_W1"].transpose(1, 0, 2)]),
        "w2": cat([a["L1_ffn_W2"].reshape(E, 4, P, P).transpose(2, 0, 1, 3)]),
        "b1": np.ascontiguousarray(a["L1_ffn_b1"]),
        "b2": np.ascontiguousarray(a["L1_ffn_b2"]),
        "rows": np.ascontiguousarray(np.broadcast_to(np.stack([
            a["L0_xattn_bv"], a["L1_xattn_bv"], a["L1_xattn_bo"], bqkv[2], a["L1_ffn_bo"], a["L1_ffn_g1"],
            a["L1_ffn_be1"], a["L1_ffn_g2"], a["L1_ffn_be2"]]).reshape(1, -1), (P, NROWS * P))),
        "cols": np.ascontiguousarray(np.stack([a["L0_xattn_bq"], a["L0_xattn_bk"], a["L1_xattn_bq"],
                                               a["L1_xattn_bk"], bqkv[0], bqkv[1]]
                                              + [(np.arange(P) // 8 == i).astype(np.float32)
                                                 for i in range(16)]
                                              + [(np.arange(P) // 32 == i).astype(np.float32)
                                                 for i in range(4)], axis=1)),
    }
    nc = bacc.Bacc("TRN2", target_bir_lowering=False, num_devices=1)
    args = [nc.dram_tensor("in_" + n, v.shape, mybir.dt.from_np(v.dtype), kind="ExternalInput").ap()
            for n, v in arrays.items()]
    out = nc.dram_tensor("out", (N, P), F32, kind="ExternalOutput").ap()
    program(nc, *args, out)
    r = run_bass_kernel_spmd(nc, [{"in_" + n: v for n, v in arrays.items()}], core_ids=[0])
    return r.results[0]["out"].reshape(B, S, P)
```

```python
from contextlib import ExitStack

import numpy as np
import concourse.bass as bass
from concourse import mybir

ALU = mybir.AluOpType
ACT = mybir.ActivationFunctionType
AX = mybir.AxisListType
F32 = mybir.dt.float32
BF16 = mybir.dt.bfloat16
U8 = mybir.dt.uint8

P = 128
S = 64
B = 64
N = B * S
T = N // P
GT = 4
GW = GT * P
G = T // GT
EPS = 1e-5
H = 16
DK = P // H
M = 64
VW = DK + 1
NEG = -1e30
E = 8
NT = T + E

WQ, WK, WV = range(3)
R_BV, R_XBV, R_XBO, R_QKVBV, R_BO, R_G1, R_BE1, R_G2, R_BE2 = range(9)
NROWS = 9
C_BQ, C_BK, C_XBQ, C_XBK, C_MBQ, C_MBK, C_HEAD = range(7)
C_HEAD4 = C_HEAD + 16
NCOLS = C_HEAD4 + 4


def wait(eng, sem, value):
    if isinstance(value, int) and value <= 0:
        return
    eng.wait_ge(sem, value)


def program(nc, x, ctxT, maskrow, wA, wB, wC, memT, mem, wF, w1, w2, b1, b2, rows, cols, out):
    with ExitStack() as ctx:
        def sb(name, shape, dt=F32):
            return ctx.enter_context(nc.sbuf_tensor(name, shape, dt))

        def sem(name):
            return ctx.enter_context(nc.semaphore(name))

        def pair(name):
            return [sem(f"{name}{i}") for i in range(2)]

        bank = ctx.enter_context(nc.psum_tensor("bank", [P, 8, 512], F32))
        X = sb("X", [P, T, P])
        wA_s = sb("wA_s", [P, 3, P])
        rows_s = sb("rows_s", [P, NROWS, P])
        cols_s = sb("cols_s", [P, NCOLS])
        ident = sb("ident", [P, P])
        neghalf = sb("neghalf", [P, GT])
        st = sb("st", [P, 2, GT, 6])
        lsum = sb("lsum", [P, 2, GT, 2])
        ldif = sb("ldif", [P, 2, GT])
        mean = sb("mean", [P, 2, GT])
        ve = sb("ve", [P, 2, GT])
        rstd = sb("rstd", [P, 2, GT])
        shift = sb("shift", [P, 2, GT])
        xn = sb("xn", [P, 2, GT, P])
        xnT = sb("xnT", [P, 2, GW])
        ctxb = sb("ctxb", [P, 2, GW])

        qT = sb("qT", [P, 2, GW])
        kT = sb("kT", [P, 2, GW])
        vS = sb("vS", [P, 2, GT, P])
        mx = sb("mx", [P, 2, GT])
        ss = sb("ss", [P, 2, GT, S])
        pbd = sb("pbd", [P, 2, GT, P])
        pT = sb("pT", [P, 2, GT, P])
        rs = sb("rs", [P, 2, GT])
        ri = sb("ri", [P, 2, GT])

        NE = E + 1
        big = sb("big", [P, E * 4 * P])
        wB_s = big[:, 0:3 * NE * P + E]
        wgate, wup, wdown = [wB_s[:, i * NE * P:(i + 1) * NE * P].rearrange("p (e f) -> p e f", e=NE)
                             for i in range(3)]
        wrouter = wB_s[:, 3 * NE * P:]
        desc = sb("desc", [P, GT, E])
        le = sb("le", [P, 2, GT, E])
        r8 = [sb(f"r8{i}", [P, GT, E]) for i in range(4)]
        r1 = [sb(f"r1{i}", [P, GT]) for i in range(6)]
        comb = sb("comb", [P, 2, GT, E])
        th = sb("th", [P, 2, GW])
        NACC, NOD = (NE + 1) // 2 + 1, NE // 2
        ga = sb("ga", [P, 2, GW])
        hT = sb("hT", [P, 2, GW])

        wC_s = sb("wC_s", [P, 4, P])
        maskb = sb("maskb", [P, N], U8)
        mrow = sb("mrow", [P, 2, GW], BF16)
        onesb = sb("onesb", [P, P], BF16)
        memT_s = sb("memT_s", [P, M])
        mem_s = sb("mem_s", [P, P])
        NB = GW // S
        arena = sb("arena", [P, 2 * NB * H * S])
        qx = arena[:].rearrange("p (i b c) -> p i b c", i=2, b=NB)
        kk = sb("kk", [P, 2, NB, S + M])
        v1 = sb("v1", [P, 2, NB, H * VW])
        cmx = sb("cmx", [P, 2, 4])
        csub = sb("csub", [P, 2, 4, P])
        cP = sb("cP", [P, 2, 4, P])
        cPT = sb("cPT", [P, 2, GW])
        crv = sb("crv", [P, H])
        cO = ga[:, 0, :]
        Oa = sb("Oa", [P, 2, GT, P])
        cOT = sb("cOT", [P, GW])

        H4, D4 = 4, P // 4
        x3 = nc.dram_tensor("x3", (N, P), F32, kind="Internal").ap()
        x3_t = x3.rearrange("(t p) d -> p t d", p=P)
        wF_s = sb("wF_s", [P, 4 * P + E])
        at = [0]

        def part(shape):
            n = int(np.prod(shape))
            v = arena[:, at[0]:at[0] + n]
            at[0] += n
            names = "abcd"[:len(shape)]
            return v.rearrange(f"p ({' '.join(names)}) -> p {' '.join(names)}", **dict(zip(names, shape)))
        weighed = arena[:, 0:2 * GW].rearrange("p (i t d) -> p i t d", i=2, t=GT)
        oddsum = arena[:, 2 * GW:4 * GW].rearrange("p (i t d) -> p i t d", i=2, t=GT)
        xg = part([2, GT, P])
        dbq = sb("dbq", [P, 4])
        q4 = part([2, H4, GW])
        v4 = sb("v4", [P, 2, GT, H4 * (D4 + 1)])
        dmx = sb("dmx", [P, 2, 8])
        dsub = part([2, 8, S])
        dP = part([16, P])
        drv = sb("drv", [P, 2, 8])
        dOa = sb("dOa", [P, GT, P])
        z = ss[:].rearrange("p i t k -> p (i t k)").rearrange("p (t d) -> p t d", t=GT)

        ys = cP
        yT = ga[:, 1, :]
        mall = sb("mall", [P, T, E])
        xs = nc.dram_tensor("xs", (NT * P, P), F32, kind="Internal").ap()
        os = nc.dram_tensor("os", (NT * P, P), F32, kind="Internal").ap()
        b1_s = part([E * 4 * P])
        b2_s = hT[:].rearrange("p i w -> p (i w)")
        before = sb("before", [P, P])
        ones = sb("ones", [P, 2 * P])
        zero = sb("zero", [P, P])
        starts_i = sb("starts_i", [P, T], mybir.dt.int32)
        starts = sb("starts", [P, T])
        tiles_i = sb("tiles_i", [P, NT], mybir.dt.int32)
        tiles = sb("tiles", [P, NT])
        flat = csub[:].rearrange("p i u k -> p (i u k)")
        cum, cumx, pos = [flat[:, i * E * T:(i + 1) * E * T].rearrange("p (e t) -> p e t", e=E) for i in range(3)]
        big8 = th[:, 0, 0:NT * E].rearrange("p (j e) -> p j e", e=E)
        n8 = [sb(f"n8{i}", [P, E]) for i in range(5)]
        slotf = sb("slotf", [P, T])
        slot = sb("slot", [P, T], mybir.dt.uint32)
        tef = sb("tef", [P, NT])
        te = sb("te", [P, NT], mybir.dt.int32)
        xe = [xn[:, i, 0:2, :] for i in range(2)]
        xeT = [xnT[:, i, 0:P] for i in range(2)]
        he = [q4[:, i, 0, :] for i in range(2)]
        heT = [q4[:, i, 1, :] for i in range(2)]
        oe = [xn[:, i, 2:4, :] for i in range(2)]
        w1_s = big
        w2_s = part([E * 4 * P])
        og = big[:].rearrange("p (t d) -> p t d", t=T)
        ysum = ys
        yo = vS
        xr = pbd

        w_in = sem("w_in")
        id_zero, id_ready, const_ready = sem("id_zero"), sem("id_ready"), sem("const_ready")
        def sems(prefix, names, **more):
            return {n: sem(f"{prefix}_{n}") for n in names.split()} | more

        wB_in, wC_in = sem("wB_in"), sem("wC_in")
        stats, scales = sem("stats"), sem("scales")
        LN = "xn tr xnT "
        a = sems("a", LN + "q k v qT kT vS s mx sub exp ri ptr pT o xo", ln=stats, rstd=scales, past=0,
                 x=pair("a_x"), ctx=pair("a_ctx"))
        b = sems("b", LN + "logit lmax lsub lexp route comb gate up tanh act h down acc scaled pacc",
                 ln=stats, rstd=scales, past=G)
        c = sems("c", LN + "q k v mask qT kT vS s mx sub exp ptr pT pv oc bt rv on otr oT wo xa xo const memrow qx",
                 ln=stats, rstd=scales, past=2 * G, ctx=pair("c_ctx"))
        d = sems("d", "ln rstd xnT q k v qT kT vS s mx sub exp ptr pT pv rv on otr oT wo "
                 "z lg normed const bq ytr yT logit route ycopy",
                 past=0, x=pair("d_x"))
        dn = sems("dn", "ln rstd xn tr", past=0)
        m = sems("m", "tr xT h hb htr hT up o", x=pair("m_x"), out=pair("m_out"))
        r_step, r_sums, slots_ready = sem("r_step"), sem("r_sums"), sem("slots_ready")
        xs_zero, xs_in, io_ready = sem("xs_zero"), sem("xs_in"), sem("io_ready")
        e = sems("e", "add shift scaled lg y", ln=stats, rstd=scales, past=3 * G, x=pair("e_x"), out=pair("e_out"), rows=pair("e_rows"))
        x3_out, wF_in, wG_in = sem("x3_out"), sem("wF_in"), sem("wG_in")

        x_t = x.rearrange("(t p) d -> p t d", p=P)

        def steps(eng, ahead, main):
            for part in ahead:
                part(0, 0, 0)

            def call(g, par, half, half1, last=False):
                def nxt(k):
                    if not last:
                        ahead[k](g + 1, 1 - par, half1)
                main(g, par, half, nxt)
            call(0, 0, 0, 0)
            with eng.Fori(0, (G - 2) // 2) as i:
                call(2 * i + 1, 1, i, i + 1)
                call(2 * i + 2, 0, i + 1, i + 1)
            call(G - 1, 1, (G - 1) // 2, None, last=True)

        def quad_steps(eng, quad):
            quad(0, 0, False)
            with eng.Fori(1, NT // 4 - 1) as i:
                quad(4 * i, i, False)
            quad(NT - 4, NT // 4 - 1, True)

        def experts_of(eng, j, last):
            return [eng.value_load(te[0:1, bass.ds(j + k, 1)], min_val=0, max_val=E - 1)
                    for k in range(4 if last else 5)]

        def layer_norm_stats(dve, n, g, par, src):
            def then(i, k):
                i.then_inc(n["ln"], 1)
                dve.wait_ge(n["ln"], 5 * (g + n["past"]) + k)
            for t in range(GT):
                i = nc.vector.bn_stats(st[:, par, t, :], src(t))
            then(i, 1)
            even, odd = st[:, par, :, 1:3], st[:, par, :, 4:6]
            nc.vector.tensor_tensor(lsum[:, par], even, odd, ALU.add)
            then(nc.vector.tensor_tensor(ldif[:, par], even[:, :, 0], odd[:, :, 0], ALU.subtract), 2)
            nc.vector.tensor_scalar(mean[:, par], lsum[:, par, :, 0], 0.5, None, ALU.mult)
            then(nc.vector.tensor_tensor(ldif[:, par], ldif[:, par], ldif[:, par], ALU.mult), 3)
            then(nc.vector.scalar_tensor_tensor(ve[:, par], ldif[:, par], P / 4.0, lsum[:, par, :, 1],
                                                ALU.mult, ALU.add), 4)
            nc.vector.tensor_scalar(ve[:, par], ve[:, par], 1.0 / P, EPS, ALU.mult, ALU.add).then_inc(n["ln"], 1)

        def layer_norm_rows(dve, n, g, par, src):
            dve.wait_ge(n["rstd"], g + n["past"] + 1)
            wait(dve, n["tr"], g - 1)
            for t in range(GT):
                i = nc.vector.tensor_scalar(xn[:, par, t, :], src(t), mean[:, par, t:t + 1],
                                            rstd[:, par, t:t + 1], ALU.subtract, ALU.mult)
            i.then_inc(n["xn"], 1)

        def layer_norm_affine(dve, n, g, par, src, tmp, out_rows, r_gain, r_bias):
            dve.wait_ge(n["rstd"], g + n["past"] + 1)
            for t in range(GT):
                i = nc.vector.tensor_scalar(tmp[:, t, :], src(t), mean[:, par, t:t + 1],
                                            rstd[:, par, t:t + 1], ALU.subtract, ALU.mult)
            i.then_inc(n["lg"], 1)
            dve.wait_ge(n["lg"], 2 * g + 1)
            nc.vector.tensor_tensor(tmp, tmp, rows_s[:, r_gain:r_gain + 1, :].to_broadcast([P, GT, P]),
                                    ALU.mult).then_inc(n["lg"], 1)
            dve.wait_ge(n["lg"], 2 * g + 2)
            nc.vector.tensor_tensor(out_rows, tmp, rows_s[:, r_bias:r_bias + 1, :].to_broadcast([P, GT, P]),
                                    ALU.add).then_inc(n["normed"], 1)

        def pool_rstd(pool, n, g, par):
            pool.wait_ge(n["ln"], 5 * (g + n["past"] + 1))
            nc.gpsimd.tensor_tensor(rstd[:, par, :], ve[:, par, :], neghalf[:], ALU.pow).then_inc(n["rstd"], 1)

        def transpose_xn(pe, n, g, par):
            for t in range(GT):
                i = nc.tensor.transpose(bank[:, 0, t * P:(t + 1) * P], xn[:, par, t, :], ident[:])
            i.then_inc(n["tr"], 1)

        block = ctx.enter_context(nc.Block())

        @block.sync
        def _(sp):

            def a_load(g, par, half):
                wait(sp, a["v"], g - 1)
                wait(sp, a["xn"], g - 1)
                sp.dma_start(X[:, bass.ds(g * GT, GT), :], x_t[:, bass.ds(g * GT, GT), :]).then_inc(a["x"][par], 16)
                sp.dma_start(ctxb[:, par, :], ctxT[:, bass.ds(g * GW, GW)]).then_inc(a["ctx"][par], 16)
            steps(sp, [a_load], lambda g, par, half, nxt: nxt(0))
            sp.dma_start(wB_s[:], wB).then_inc(wB_in, 16)
            sp.dma_start(wC_s[:], wC.rearrange("p (i d) -> p i d", i=4)).then_inc(wC_in, 16)
            sp.dma_start(memT_s[:], memT).then_inc(wC_in, 16)
            sp.dma_start(mem_s[M:P, :], mem).then_inc(wC_in, 16)
            sp.dma_start(maskb[:], bass.AP(maskrow.tensor, 0, [[0, P], [1, N]])).then_inc(wC_in, 16)
            sp.wait_ge(const_ready, 3)
            sp.dma_start(xs.rearrange("(j p) d -> p j d", p=P),
                         zero[:].unsqueeze(1).to_broadcast([P, NT, P])).then_inc(xs_zero, 16)
            sp.wait_ge(a["o"], G)

            def c_load(g, par, half):
                wait(sp, c["v"], 2 * g - 2)
                sp.dma_start(ctxb[:, par, :], ctxT[:, bass.ds(g * GW, GW)]).then_inc(c["ctx"][par], 16)
            def c_store(g, par, half, nxt):
                nxt(0)
                sp.wait_ge(c["xo"], g + 1)
                sp.dma_start(x3_t[:, bass.ds(g * GT, GT), :], X[:, bass.ds(g * GT, GT), :]).then_inc(x3_out, 16)
            steps(sp, [c_load], c_store)

            sp.wait_ge(x3_out, 16 * G)

            def rows_of(dram, g, n):
                return dram.rearrange("(b g t n) d -> n b g t d", b=B, g=G, n=2)[n][:, bass.ds(g, 1)].rearrange(
                    "b g t d -> b (g t) d")

            def d_load(g, par, half):
                wait(sp, dn["xn"], g - 1)
                for n in range(2):
                    sp.dma_start(xg[n * S:(n + 1) * S, par], rows_of(x3, g, n)).then_inc(d["x"][par], 16)
            steps(sp, [d_load], lambda g, par, half, nxt: nxt(0))

            def pair_of(dram, p):
                return dram[bass.ds(p * 2 * P, 2 * P), :].rearrange("(n p) d -> p n d", p=P)

            def m_load(p, b):
                wait(sp, m["tr"], 2 * p - 2)
                sp.dma_start(xe[b], pair_of(xs, p)).then_inc(m["x"][b], 16)

            def m_quad(j, q, last):
                for b in range(2):
                    p = 2 * q + b
                    if not last:
                        m_load(p + 2, b)
                    sp.wait_ge(m["o"], 2 * p + 2)
                    sp.dma_start(pair_of(os, p), oe[b]).then_inc(m["out"][b], 16)
            sp.wait_ge(xs_in, 16 * T)
            m_load(0, 0)
            m_load(1, 1)
            quad_steps(sp, m_quad)

            def e_load(g, par, half):
                wait(sp, e["y"], g - 1)
                for n in range(2):
                    sp.dma_start(xr[n * S:(n + 1) * S, par], rows_of(x3, g, n)).then_inc(e["x"][par], 16)

            def e_store(g, par, half, nxt):
                nxt(0)
                sp.wait_ge(e["y"], g + 1)
                for n in range(2):
                    sp.dma_start(rows_of(out, g, n), yo[n * S:(n + 1) * S, par]).then_inc(e["out"][par], 16)
            steps(sp, [e_load], e_store)
            for par in range(2):
                sp.wait_ge(e["out"][par], 16 * G)

        @block.gpsimd
        def _(pool):
            nc.gpsimd.memset(ident[:], 0.0).then_inc(id_zero, 1)
            pool.wait_ge(id_zero, 1)
            nc.gpsimd.affine_select(out=ident[:], in_=ident[:], compare_op=ALU.not_equal, fill=1.0, base=0,
                                    pattern=[[-1, P]], channel_multiplier=1).then_inc(id_ready, 1)
            nc.gpsimd.memset(neghalf[:], -0.5).then_inc(const_ready, 1)
            nc.gpsimd.memset(pbd[:], 0.0).then_inc(const_ready, 1)
            for k in range(E):
                i = nc.gpsimd.memset(desc[:, :, k:k + 1], float(E - k))
            i.then_inc(const_ready, 1)
            nc.gpsimd.memset(zero[:], 0.0)
            nc.gpsimd.memset(ones[:], 1.0).then_inc(io_ready, 1)
            pool.wait_ge(io_ready, 1)
            nc.gpsimd.affine_select(out=before[:], in_=ones[:, 0:P], compare_op=ALU.is_gt, fill=0.0, base=0,
                                    pattern=[[1, P]], channel_multiplier=-1)
            nc.gpsimd.iota(starts_i[:], pattern=[[P, T]], base=0, channel_multiplier=0)
            nc.gpsimd.iota(tiles_i[:], pattern=[[1, NT]], base=0, channel_multiplier=0).then_inc(io_ready, 1)
            pool.wait_ge(io_ready, 2)
            nc.gpsimd.tensor_copy(starts[:], starts_i[:])
            nc.gpsimd.tensor_copy(tiles[:], tiles_i[:]).then_inc(io_ready, 1)
            nc.gpsimd.memset(onesb[:], 1.0)
            nc.gpsimd.memset(v1[:], 1.0).then_inc(c["const"], 1)
            nc.gpsimd.memset(v4[:], 1.0).then_inc(d["const"], 1)
            pool.wait_ge(const_ready, 3)
            steps(pool, [lambda g, par, half: pool_rstd(pool, a, g, par)], lambda g, par, half, nxt: nxt(0))

            def b_main(g, par, half, nxt):
                nxt(0)
                for k in range(1, NOD):
                    pool.wait_ge(b["scaled"], NOD * g + k + 1)
                    if k > 1:
                        pool.wait_ge(b["pacc"], (NOD - 1) * g + k - 1)
                    nc.gpsimd.tensor_tensor(oddsum[:, par], oddsum[:, par], weighed[:, k % 2],
                                            ALU.add).then_inc(b["pacc"], 1)
            steps(pool, [lambda g, par, half: pool_rstd(pool, b, g, par)], b_main)
            steps(pool, [lambda g, par, half: pool_rstd(pool, c, g, par)], lambda g, par, half, nxt: nxt(0))

            pool.wait_ge(c["s"], 16 * G)
            nc.gpsimd.memset(dP[:], 0.0).then_inc(d["const"], 1)

            def d_tail(g, par):
                pool_rstd(pool, d, g, par)
                pool.wait_ge(d["normed"], g + 1)
                nc.gpsimd.tensor_copy(X[:, bass.ds(g * GT, GT), :], ys[:, par]).then_inc(d["ycopy"], 1)

            def d_main(g, par, half, nxt):
                nxt(0)
                if not (isinstance(g, int) and g == 0):
                    d_tail(g - 1, 1 - par)
            steps(pool, [lambda g, par, half: pool_rstd(pool, dn, g, par)], d_main)
            d_tail(G - 1, 1)

            pool.wait_ge(slots_ready, 1)
            pool.wait_ge(xs_zero, 16)
            pool.wait_ge(d["ycopy"], G)
            for t in range(T):
                pool.indirect_dma_start(xs, bass.IndirectOffsetOnAxis(ap=slot[:, t:t + 1], axis=0),
                                        X[:, t, :], None).then_inc(xs_in, 16)
            for par in range(2):
                pool.wait_ge(m["out"][par], 16 * (NT // 4))
            for g in range(G):
                if g >= 2:
                    pool.wait_ge(e["rows"][g % 2], 16 * GT * (g // 2))
                for t in range(g * GT, (g + 1) * GT):
                    pool.indirect_dma_start(og[:, t, :], None, os,
                                            bass.IndirectOffsetOnAxis(ap=slot[:, t:t + 1], axis=0)
                                            ).then_inc(e["rows"][g % 2], 16)
                if g:
                    pool_rstd(pool, e, g - 1, (g - 1) % 2)
            pool_rstd(pool, e, G - 1, 1)

        @block.vector
        def _(dve):
            def a_norm(g, par, half):
                dve.wait_ge(a["x"][par], 16 * (half + 1))
                layer_norm_stats(dve, a, g, par, lambda t: X[:, g * GT + t, :])

            def a_rows(g, par, half):
                layer_norm_rows(dve, a, g, par, lambda t: X[:, g * GT + t, :])

            def a_value(g, par, half):
                dve.wait_ge(w_in, 16 * 3)
                dve.wait_ge(a["v"], g + 1)
                wait(dve, a["o"], g - 1)
                nc.vector.tensor_tensor(vS[:, par], bank[:, 3, :].rearrange("p (t d) -> p t d", t=GT),
                                        rows_s[:, R_BV:R_BV + 1, :].to_broadcast([P, GT, P]), ALU.add).then_inc(a["vS"], 1)

            def a_update(g, par):
                dve.wait_ge(a["ri"], 2 * g + 2)
                dve.wait_ge(a["o"], g + 1)
                for t in range(GT):
                    xt = X[:, g * GT + t, :]
                    i = nc.vector.scalar_tensor_tensor(xt, bank[:, 6, t * P:(t + 1) * P], ri[:, par, t:t + 1], xt,
                                                       ALU.mult, ALU.add)
                i.then_inc(a["xo"], 1)

            def a_main(g, par, half, nxt):
                nxt(0)
                dve.wait_ge(a["s"], g + 1)
                s = bank[:, 4, 0:GT * S].rearrange("p (t k) -> p t k", t=GT)
                nc.vector.tensor_reduce(mx[:, par, :], s, AX.X, ALU.max).then_inc(a["mx"], 1)
                dve.wait_ge(a["mx"], g + 1)
                wait(dve, a["exp"], g - 1)
                nc.vector.tensor_tensor(ss[:, par], s, mx[:, par, :].unsqueeze(2).to_broadcast([P, GT, S]),
                                        ALU.subtract).then_inc(a["sub"], 1)
                nxt(1)
                if not (isinstance(g, int) and g == 0):
                    a_update(g - 1, 1 - par)
                dve.wait_ge(a["exp"], g + 1)
                nc.vector.tensor_reduce(rs[:, par, :], pbd[:, par], AX.X, ALU.add).then_inc(a["ri"], 1)
                dve.wait_ge(a["ri"], 2 * g + 1)
                nc.vector.reciprocal(ri[:, par, :], rs[:, par, :]).then_inc(a["ri"], 1)
                nxt(2)
            steps(dve, [a_norm, a_rows, a_value], a_main)
            a_update(G - 1, 1)

            def b_norm(g, par, half):
                dve.wait_ge(a["xo"], g + 1)
                layer_norm_stats(dve, b, g, par, lambda t: X[:, g * GT + t, :])

            def b_rows(g, par, half):
                layer_norm_rows(dve, b, g, par, lambda t: X[:, g * GT + t, :])

            def b_logits(g, par, half):
                lg = bank[:, 1, 0:GT * E].rearrange("p (t e) -> p t e", t=GT)
                dve.wait_ge(b["logit"], g + 1)
                nc.vector.tensor_reduce(r1[0][:], lg, AX.X, ALU.max).then_inc(b["lmax"], 1)
                dve.wait_ge(b["lmax"], g + 1)
                nc.vector.tensor_tensor(le[:, par], lg, r1[0][:].unsqueeze(2).to_broadcast([P, GT, E]),
                                        ALU.subtract).then_inc(b["lsub"], 1)

            ROUTE = 13

            def b_route(half_of):
                def spread(v):
                    return v[:].unsqueeze(2).to_broadcast([P, GT, E])
                key, one1, rest, one2 = [v[:] for v in r8]
                total, m1, m2, k, den, r = r1

                def first(g, par, half):
                    def then(i, step):
                        i.then_inc(b["route"], 1)
                        dve.wait_ge(b["route"], ROUTE * g + step)
                    e8 = le[:, par]
                    dve.wait_ge(b["lexp"], g + 1)
                    nc.vector.tensor_reduce(total[:], e8, AX.X, ALU.add)
                    then(nc.vector.tensor_reduce(m1[:], e8, AX.X, ALU.max), 1)
                    then(nc.vector.tensor_tensor(key, e8, spread(m1), ALU.is_equal), 2)
                    then(nc.vector.tensor_tensor(key, key, desc[:], ALU.mult), 3)
                    then(nc.vector.tensor_reduce(k[:], key, AX.X, ALU.max), 4)
                    then(nc.vector.tensor_tensor(one1, key, spread(k), ALU.is_equal), 5)
                    then(nc.vector.scalar_tensor_tensor(rest, one1, -2.0, e8, ALU.mult, ALU.add), 6)
                    then(nc.vector.tensor_reduce(m2[:], rest, AX.X, ALU.max), 7)

                def second(g, par, half):
                    def then(i, step):
                        i.then_inc(b["route"], 1)
                        dve.wait_ge(b["route"], ROUTE * g + step)
                    e8 = le[:, par]
                    nc.vector.tensor_tensor(den[:], m1[:], m2[:], ALU.add)
                    then(nc.vector.tensor_tensor(key, rest, spread(m2), ALU.is_equal), 8)
                    nc.vector.scalar_tensor_tensor(den[:], total[:], 1e-8, den[:], ALU.mult, ALU.add)
                    then(nc.vector.tensor_tensor(key, key, desc[:], ALU.mult), 9)
                    nc.vector.reciprocal(r[:], den[:])
                    then(nc.vector.tensor_reduce(k[:], key, AX.X, ALU.max), 10)
                    then(nc.vector.tensor_tensor(one2, key, spread(k), ALU.is_equal), 11)
                    then(nc.vector.tensor_tensor(one2, one2, one1, ALU.add), 12)
                    wait(dve, b["acc"], NACC * (g - 1))
                    wait(dve, b["scaled"], NOD * (g - 1))
                    then(nc.vector.scalar_tensor_tensor(rest, one2, 0.5, e8, ALU.mult, ALU.mult), 13)
                    nc.vector.tensor_tensor(comb[:, par], rest, spread(r), ALU.mult).then_inc(b["comb"], 1)
                return second if half_of else first

            def b_main(g, par, half, nxt):
                def accumulate(u):
                    w, pu = NE * g + u, (par + u) % 2
                    dve.wait_ge(b["down"], w + 1)
                    if u == 0:
                        dve.wait_ge(b["comb"], g + 1)
                    wait(dve, b["acc"], NACC * g + u // 2)
                    if u == E:
                        xt = X[:, bass.ds(g * GT, GT), :] if not isinstance(g, int) else X[:, g * GT:(g + 1) * GT, :]
                        o = bank[:, 6 + pu, :].rearrange("p (t d) -> p t d", t=GT)
                        nc.vector.scalar_tensor_tensor(xt, o, 0.5, xt, ALU.mult, ALU.add).then_inc(b["acc"], 1)
                        dve.wait_ge(b["acc"], NACC * g + NACC - 1)
                        dve.wait_ge(b["pacc"], (NOD - 1) * (g + 1))
                        nc.vector.tensor_tensor(xt, xt, oddsum[:, par], ALU.add).then_inc(b["acc"], 1)
                        return
                    for t in range(GT):
                        xt = X[:, g * GT + t, :]
                        i = nc.vector.scalar_tensor_tensor(xt, bank[:, 6 + pu, t * P:(t + 1) * P],
                                                           comb[:, par, t, u:u + 1], xt, ALU.mult, ALU.add)
                    i.then_inc(b["acc"], 1)

                for u in range(NE):
                    w, pu = NE * g + u, (par + u) % 2
                    dve.wait_ge(b["tanh"], w + 1)
                    nc.vector.scalar_tensor_tensor(ga[:, pu, :], th[:, pu, :], 1.0, bank[:, 2 + pu, :],
                                                   ALU.add, ALU.mult).then_inc(b["act"], 1)
                    dve.wait_ge(b["act"], w + 1)
                    dve.wait_ge(b["up"], w + 1)
                    wait(dve, b["down"], w - 1)
                    nc.vector.tensor_tensor(hT[:, pu, :], ga[:, pu, :], bank[:, 4 + pu, :], ALU.mult).then_inc(b["h"], 1)
                    if u % 2:
                        accumulate(u - 1)
                    if u == 1:
                        nxt(0)
                    if u == 2:
                        nxt(1)
                    if u == 5:
                        nxt(2)
                    if u == 6:
                        nxt(3)
                    if u == 8:
                        nxt(4)
                accumulate(E)
            dve.wait_ge(const_ready, 3)
            steps(dve, [b_norm, b_rows, b_logits, b_route(0), b_route(1)], b_main)

            dve.wait_ge(wC_in, 16 * 4)
            dve.wait_ge(c["const"], 1)
            for par in range(2):
                nc.vector.tensor_scalar(kk[:, par, :, S:], memT_s[:].unsqueeze(1).to_broadcast([P, NB, M]),
                                        DK ** 0.5, None, ALU.mult)
                v = v1[M:P, par].rearrange("p b (h d) -> p b h d", h=H)
                for n in range(NB):
                    nc.vector.tensor_scalar(v[:, n, :, 0:DK], mem_s[M:P, :].rearrange("p (h d) -> p h d", h=H),
                                            M ** 0.5, None, ALU.mult)
            dve.wait_ge(b["acc"], NACC * G)
            nc.vector.memset(bank[:, 7, :], 0.0).then_inc(c["memrow"], 1)

            def c_norm(g, par, half):
                dve.wait_ge(b["acc"], NACC * (g + 1))
                layer_norm_stats(dve, c, g, par, lambda t: X[:, g * GT + t, :])
                wait(dve, c["s"], 16 * (g - 1))
                nc.vector.tensor_scalar(mrow[:, par, :], maskb[:, bass.ds(g * GW, GW)], NEG, None,
                                        ALU.mult).then_inc(c["mask"], 1)

            def c_rows(g, par, half):
                layer_norm_rows(dve, c, g, par, lambda t: X[:, g * GT + t, :])

            def c_heads(k):
                def part(g, par, half):
                    dve.wait_ge(c["qT"], g + 1)
                    wait(dve, c["s"], 16 * (g - 1))
                    for h in range(4 * k, 4 * k + 4):
                        i = nc.vector.tensor_scalar(qx[:, par, :, h * S:(h + 1) * S],
                                                    qT[:, par, :].rearrange("p (b s) -> p b s", b=NB),
                                                    cols_s[:, C_HEAD + h:C_HEAD + h + 1], None, ALU.mult)
                    if k == 3:
                        i.then_inc(c["qx"], 1)
                return part

            def c_value(k):
                def part(g, par, half):
                    dve.wait_ge(c["v"], 2 * g + k + 1)
                    wait(dve, c["pv"], 16 * (g - 1))
                    nb = NB // 2
                    v = v1[0:S, par, k * nb:(k + 1) * nb, :].rearrange("p b (h d) -> p b h d", h=H)
                    bias = rows_s[0:S, R_XBV, :].rearrange("p (h d) -> p h d", h=H).unsqueeze(1)
                    for n in range(nb):
                        i = nc.vector.tensor_tensor(
                            v[:, n, :, 0:DK], bank[0:S, 0, n * P:(n + 1) * P].rearrange("p (h d) -> p h d", h=H),
                            rows_s[0:S, R_XBV, :].rearrange("p (h d) -> p h d", h=H), ALU.add)
                    i.then_inc(c["vS"], 1)
                return part

            def c_normalize(g, par, t):
                n = 4 * g + t
                o = bank[:, 6, :].rearrange("p (h d) -> p h d", h=H)
                dve.wait_ge(c["bt"], n + 1)
                nc.vector.reciprocal(crv[:], o[:, :, DK]).then_inc(c["rv"], 1)
                dve.wait_ge(c["rv"], n + 1)
                if t == 0:
                    wait(dve, c["otr"], g - 1)
                nc.vector.tensor_tensor(Oa[:, par, t, :].rearrange("p (h d) -> p h d", h=H), o[:, :, 0:DK],
                                        crv[:].unsqueeze(2).to_broadcast([P, H, DK]), ALU.mult).then_inc(c["on"], 1)

            def c_update(g):
                xt = X[:, bass.ds(g * GT, GT), :]
                dve.wait_ge(c["wo"], g + 1)
                nc.vector.tensor_tensor(xt, xt, bank[:, 0, :].rearrange("p (t d) -> p t d", t=GT),
                                        ALU.add).then_inc(c["xa"], 1)
                dve.wait_ge(c["xa"], g + 1)
                nc.vector.tensor_tensor(xt, xt, rows_s[:, R_XBO:R_XBO + 1, :].to_broadcast([P, GT, P]),
                                        ALU.add).then_inc(c["xo"], 1)

            def c_main(g, par, half, nxt):
                first = isinstance(g, int) and g == 0
                for j in range(16):
                    w, r = 16 * g + j, j % 4
                    s = bank[:, 2 + r, :].rearrange("p (u k) -> p u k", u=4)
                    dve.wait_ge(c["s"], w + 1)
                    nc.vector.tensor_reduce(cmx[:, j % 2, :], s, AX.X, ALU.max).then_inc(c["mx"], 1)
                    dve.wait_ge(c["mx"], w + 1)
                    wait(dve, c["exp"], w - 1)
                    nc.vector.tensor_tensor(csub[:, j % 2], s, cmx[:, j % 2, :].unsqueeze(2).to_broadcast([P, 4, P]),
                                            ALU.subtract).then_inc(c["sub"], 1)
                    if j == 2 and not first:
                        c_normalize(g - 1, 1 - par, 3)
                    if j == 3:
                        nxt(0)
                    if j == 5 and not first:
                        c_update(g - 1)
                    if j in (6, 10, 14):
                        c_normalize(g, par, j // 4 - 1)
                    if j == 4:
                        nxt(1)
                    if 9 <= j <= 12:
                        nxt(2 + j - 9)
                    if j == 13:
                        nxt(6)
                    if j == 14:
                        nxt(7)
            steps(dve, [c_norm, c_rows, c_heads(0), c_heads(1), c_heads(2), c_heads(3), c_value(0), c_value(1)], c_main)
            c_normalize(G - 1, 1, 3)
            c_update(G - 1)

            dve.wait_ge(d["const"], 2)

            def d_norm(g, par, half):
                dve.wait_ge(d["x"][par], 32 * (half + 1))
                layer_norm_stats(dve, dn, g, par, lambda t: xg[:, par, t, :])

            def d_rows(g, par, half):
                layer_norm_rows(dve, dn, g, par, lambda t: xg[:, par, t, :])

            def d_value(g, par, half):
                dve.wait_ge(d["v"], g + 1)
                wait(dve, d["pv"], 4 * (g - 1))
                bias = rows_s[:, R_QKVBV, :].rearrange("p (h d) -> p h d", h=H4)
                for t in range(GT):
                    i = nc.vector.tensor_tensor(
                        v4[:, par, t, :].rearrange("p (h d) -> p h d", h=H4)[:, :, 0:D4],
                        bank[:, 1, t * P:(t + 1) * P].rearrange("p (h d) -> p h d", h=H4), bias, ALU.add)
                i.then_inc(d["vS"], 1)

            def d_route(g):
                lg = bank[:, 5, 0:GT * E].rearrange("p (t e) -> p t e", t=GT)
                key = r8[0][:]
                dve.wait_ge(d["logit"], g + 1)
                nc.vector.tensor_reduce(r1[0][:], lg, AX.X, ALU.max).then_inc(d["route"], 1)
                dve.wait_ge(d["route"], 5 * g + 1)
                nc.vector.tensor_tensor(key, lg, r1[0][:].unsqueeze(2).to_broadcast([P, GT, E]),
                                        ALU.is_equal).then_inc(d["route"], 1)
                dve.wait_ge(d["route"], 5 * g + 2)
                nc.vector.tensor_tensor(key, key, desc[:], ALU.mult).then_inc(d["route"], 1)
                dve.wait_ge(d["route"], 5 * g + 3)
                nc.vector.tensor_reduce(r1[1][:], key, AX.X, ALU.max).then_inc(d["route"], 1)
                dve.wait_ge(d["route"], 5 * g + 4)
                nc.vector.tensor_tensor(mall[:, bass.ds(g * GT, GT), :], key,
                                        r1[1][:].unsqueeze(2).to_broadcast([P, GT, E]),
                                        ALU.is_equal).then_inc(d["route"], 1)

            def d_add(g, par):
                wait(dve, d["normed"], g)
                dve.wait_ge(d["wo"], g + 1)
                nc.vector.tensor_tensor(z, xn[:, par], bank[:, 3, :].rearrange("p (t d) -> p t d", t=GT),
                                        ALU.add).then_inc(d["z"], 1)
                dve.wait_ge(d["z"], 2 * g + 1)
                nc.vector.tensor_tensor(z, z, rows_s[:, R_BO:R_BO + 1, :].to_broadcast([P, GT, P]),
                                        ALU.add).then_inc(d["z"], 1)
                dve.wait_ge(d["z"], 2 * g + 2)

            def d_affine(g, par):
                wait(dve, d["ytr"], g)
                wait(dve, d["ycopy"], g)
                layer_norm_affine(dve, d, g, par, lambda t: z[:, t, :], z, ys[:, par], R_G1, R_BE1)

            def d_main(g, par, half, nxt):
                first = isinstance(g, int) and g == 0
                for m in range(2):
                    s = bank[:, 4 + m, :].rearrange("p (u k) -> p u k", k=S)
                    dve.wait_ge(d["s"], 2 * g + m + 1)
                    nc.vector.tensor_reduce(dmx[:, m, :], s, AX.X, ALU.max).then_inc(d["mx"], 1)
                    dve.wait_ge(d["mx"], 2 * g + m + 1)
                    wait(dve, d["exp"], 2 * g + m - 1)
                    nc.vector.tensor_tensor(dsub[:, m], s, dmx[:, m, :].unsqueeze(2).to_broadcast([P, 8, S]),
                                            ALU.subtract).then_inc(d["sub"], 1)
                nxt(0)
                if not first:
                    d_add(g - 1, 1 - par)
                nxt(1)
                if not first:
                    layer_norm_stats(dve, d, g - 1, 1 - par, lambda t: z[:, t, :])
                for m in range(2):
                    if m and not first:
                        d_affine(g - 1, 1 - par)
                    o = bank[:, 2 + m, 0:8 * (D4 + 1)].rearrange("p (h t d) -> p h t d", h=2, t=GT)
                    dve.wait_ge(d["pv"], 4 * g + 2 * m + 2)
                    nc.vector.reciprocal(drv[:, m].rearrange("p (h t) -> p h t", h=2), o[:, :, :, D4]).then_inc(d["rv"], 1)
                    dve.wait_ge(d["rv"], 2 * g + m + 1)
                    wait(dve, d["otr"], g)
                    for h in range(2):
                        i = nc.vector.tensor_tensor(
                            dOa[:, :, (2 * m + h) * D4:(2 * m + h + 1) * D4], o[:, h, :, 0:D4],
                            drv[:, m, h * GT:(h + 1) * GT].unsqueeze(2).to_broadcast([P, GT, D4]), ALU.mult)
                    i.then_inc(d["on"], 1)
                if not first:
                    d_route(g - 1)
                nxt(2)
            steps(dve, [d_norm, d_rows, d_value], d_main)
            d_add(G - 1, 1)
            layer_norm_stats(dve, d, G - 1, 1, lambda t: z[:, t, :])
            d_affine(G - 1, 1)
            d_route(G - 1)

            count = [0]

            def then(i):
                count[0] += 1
                i.then_inc(r_step, 1)
                dve.wait_ge(r_step, count[0])
            rank = bank[:, 0, 0:E * T].rearrange("p (e t) -> p e t", e=E)
            total = bank[:, 1, 0:E * T]
            has = mall[:].rearrange("p t e -> p e t")
            n_e, used, upto, adjust, n_tmp = [v[:] for v in n8]
            dve.wait_ge(r_sums, 2)
            dve.wait_ge(io_ready, 3)
            then(nc.vector.tensor_tensor_scan(cum[:].rearrange("p e t -> p (e t)"), ones[:, 0:E * T], total, 0.0,
                                              ALU.mult, ALU.add))
            then(nc.vector.tensor_tensor(cumx[:], cum[:], total.rearrange("p (e t) -> p e t", e=E), ALU.subtract))
            then(nc.vector.tensor_tensor(n_e, cum[:, :, T - 1], cumx[:, :, 0], ALU.subtract))
            then(nc.vector.tensor_tensor(pos[:], n_e.unsqueeze(2).to_broadcast([P, E, T]),
                                         starts[:].unsqueeze(1).to_broadcast([P, E, T]), ALU.is_gt))
            then(nc.vector.tensor_reduce(used, pos[:], AX.X, ALU.add))
            then(nc.vector.tensor_tensor_scan(upto, ones[:, 0:E], used, 0.0, ALU.mult, ALU.add))
            then(nc.vector.tensor_tensor(n_tmp, upto, used, ALU.subtract))
            nc.vector.tensor_tensor(big8[:], upto.unsqueeze(1).to_broadcast([P, NT, E]),
                                    tiles[:].unsqueeze(2).to_broadcast([P, NT, E]), ALU.is_le)
            then(nc.vector.scalar_tensor_tensor(adjust, n_tmp, float(P), cumx[:, :, 0], ALU.mult, ALU.subtract))
            nc.vector.tensor_reduce(tef[:], big8[:], AX.X, ALU.add)
            then(nc.vector.tensor_tensor(pos[:], rank, cumx[:], ALU.add))
            then(nc.vector.tensor_tensor(pos[:], pos[:], adjust.unsqueeze(2).to_broadcast([P, E, T]), ALU.add))
            nc.vector.tensor_scalar(te[:], tef[:], float(E - 1), None, ALU.min)
            then(nc.vector.tensor_tensor(pos[:], pos[:], has, ALU.mult))
            then(nc.vector.tensor_reduce(slotf[:], pos[:].rearrange("p e t -> p t e"), AX.X, ALU.add))
            nc.vector.tensor_copy(slot[:], slotf[:]).then_inc(slots_ready, 1)

            dve.wait_ge(slots_ready, 1)
            dve.wait_ge(wG_in, 16 * 4)

            def m_hidden(j, par, expert):
                dve.wait_ge(m["h"], j + 1)
                wait(dve, m["htr"], j - 1)
                nc.vector.tensor_tensor(he[par], bank[:, 1 + par, :], b1_s[:, bass.ds(expert * 4 * P, 4 * P)],
                                        ALU.add).then_inc(m["hb"], 1)

            def m_quad(j, q, last):
                expert = experts_of(dve, j, last)
                if isinstance(j, int) and j == 0:
                    m_hidden(0, 0, expert[0])
                for k in range(4):
                    par = k % 2
                    if not last or k < 3:
                        m_hidden(j + k + 1, 1 - par, expert[k + 1])
                    dve.wait_ge(m["up"], j + k + 1)
                    if par == 0:
                        wait(dve, m["out"][k // 2], 16 * q)
                    nc.vector.tensor_tensor(oe[k // 2][:, par], bank[:, 5 + par, 0:P],
                                            b2_s[:, bass.ds(expert[k] * P, P)], ALU.add).then_inc(m["o"], 1)
            quad_steps(dve, m_quad)

            def e_sum(g, par, half):
                dve.wait_ge(e["rows"][par], 16 * GT * (half + 1))
                nc.vector.tensor_tensor(ysum[:, par], og[:, bass.ds(g * GT, GT), :], X[:, bass.ds(g * GT, GT), :], ALU.add).then_inc(e["add"], 1)
                dve.wait_ge(e["add"], g + 1)
                layer_norm_stats(dve, e, g, par, lambda t: ysum[:, par, t, :])

            def e_shift(g, par, half):
                dve.wait_ge(e["rstd"], g + e["past"] + 1)
                nc.vector.scalar_tensor_tensor(shift[:, par], mean[:, par], -1.0, rstd[:, par], ALU.mult,
                                               ALU.mult).then_inc(e["shift"], 1)

            def e_main(g, par, half, nxt):
                nxt(0)
                dve.wait_ge(e["scaled"], g + 1)
                nc.vector.tensor_tensor(xn[:, par], xn[:, par], rows_s[:, R_G2:R_G2 + 1, :].to_broadcast([P, GT, P]),
                                        ALU.mult).then_inc(e["lg"], 1)
                dve.wait_ge(e["lg"], 2 * g + 1)
                nc.vector.tensor_tensor(xn[:, par], xn[:, par], rows_s[:, R_BE2:R_BE2 + 1, :].to_broadcast([P, GT, P]),
                                        ALU.add).then_inc(e["lg"], 1)
                nxt(1)
                dve.wait_ge(e["lg"], 2 * g + 2)
                dve.wait_ge(e["x"][par], 32 * (half + 1))
                wait(dve, e["out"][par], 32 * half)
                nc.vector.tensor_tensor(yo[:, par], xn[:, par], xr[:, par], ALU.add).then_inc(e["y"], 1)
            steps(dve, [e_sum, e_shift], e_main)

        @block.scalar
        def _(act):
            act.dma_start(wA_s[:], wA).then_inc(w_in, 16)
            act.dma_start(cols_s[:], cols).then_inc(w_in, 16)
            act.dma_start(rows_s[:], rows).then_inc(w_in, 16)

            def a_xT(g, par, half):
                act.wait_ge(a["tr"], g + 1)
                wait(act, a["q"], g - 1)
                nc.scalar.copy(xnT[:, par, :], bank[:, 0, :]).then_inc(a["xnT"], 1)
                act.wait_ge(a["k"], g + 1)
                nc.scalar.activation(kT[:, par, :], bank[:, 2, :], ACT.Identity,
                                     bias=cols_s[:, C_BK:C_BK + 1]).then_inc(a["kT"], 1)

            def a_qT(g, par, half):
                act.wait_ge(a["q"], g + 1)
                nc.scalar.activation(qT[:, par, :], bank[:, 1, :], ACT.Identity,
                                     bias=cols_s[:, C_BQ:C_BQ + 1]).then_inc(a["qT"], 1)

            def a_main(g, par, half, nxt):
                act.wait_ge(a["sub"], g + 1)
                for n in range(2):
                    h = slice(n * S, (n + 1) * S)
                    i = nc.scalar.activation(pbd[h, par, :, n * S:(n + 1) * S], ss[h, par], ACT.Exp, scale=P ** -0.5)
                i.then_inc(a["exp"], 1)
                nxt(0)
                act.wait_ge(a["ptr"], g + 1)
                wait(act, a["o"], g - 1)
                nc.scalar.copy(pT[:, par].rearrange("p t k -> p (t k)"), bank[:, 5, :]).then_inc(a["pT"], 1)
                nxt(1)
            act.wait_ge(w_in, 16 * 3)
            act.wait_ge(const_ready, 2)
            steps(act, [a_xT, a_qT], a_main)

            def b_xT(g, par, half):
                act.wait_ge(b["tr"], g + 1)
                wait(act, b["up"], NE * (g - 1))
                nc.scalar.copy(xnT[:, par, :], bank[:, 0, :]).then_inc(b["xnT"], 1)

            def b_exp(g, par, half):
                act.wait_ge(b["lsub"], g + 1)
                nc.scalar.activation(le[:, par], le[:, par], ACT.Exp).then_inc(b["lexp"], 1)

            def b_scale(g, par, u):
                k = u // 2
                act.wait_ge(b["down"], NE * g + u + 1)
                act.wait_ge(b["comb"], g + 1)
                if k:
                    wait(act, b["pacc"], (NOD - 1) * g + k - 2)
                else:
                    wait(act, b["acc"], NACC * (g - 1))
                o = weighed[:, k % 2] if k else oddsum[:, par]
                for t in range(GT):
                    i = nc.scalar.activation(o[:, t, :],
                                             bank[:, 6 + (par + u) % 2, t * P:(t + 1) * P], ACT.Copy,
                                             scale=comb[:, par, t, u:u + 1])
                i.then_inc(b["scaled"], 1)

            def b_main(g, par, half, nxt):
                for u in range(NE):
                    w, pu = NE * g + u, (par + u) % 2
                    act.wait_ge(b["gate"], w + 1)
                    wait(act, b["act"], w - 1)
                    nc.scalar.activation(th[:, pu, :], bank[:, 2 + pu, :], ACT.Tanh, scale=0.5).then_inc(b["tanh"], 1)
                    if u and u % 2 == 0:
                        b_scale(g, par, u - 1)
                    if u == 4:
                        nxt(0)
                    if u == 6:
                        nxt(1)
            steps(act, [b_xT, b_exp], b_main)

            act.wait_ge(c["memrow"], 1)
            act.dma_start(wF_s[:], wF).then_inc(wF_in, 16)
            act.dma_start(w1_s[:], w1).then_inc(wG_in, 16)
            act.dma_start(b2_s, bass.AP(b2.tensor, 0, [[0, P], [1, E * P]])).then_inc(wG_in, 16)

            def c_xT(g, par, half):
                act.wait_ge(c["tr"], g + 1)
                wait(act, c["q"], g - 1)
                nc.scalar.copy(xnT[:, par, :], bank[:, 0, :]).then_inc(c["xnT"], 1)

            def c_qT(g, par, half):
                act.wait_ge(c["q"], g + 1)
                wait(act, c["qx"], g - 1)
                nc.scalar.activation(qT[:, par, :], bank[:, 0, :], ACT.Identity,
                                     bias=cols_s[:, C_XBQ:C_XBQ + 1]).then_inc(c["qT"], 1)

            def c_kT(g, par, half):
                act.wait_ge(c["k"], g + 1)
                nc.scalar.activation(kk[:, par, :, 0:S], bank[:, 0, :].rearrange("p (b s) -> p b s", b=NB),
                                     ACT.Identity, bias=cols_s[:, C_XBK:C_XBK + 1]).then_inc(c["kT"], 1)

            def c_turned(w, j):
                act.wait_ge(c["ptr"], w + 1)
                wait(act, c["pv"], w - 1)
                nc.scalar.copy(cPT[:, j % 2, :], bank[:, 1 if j % 2 else 6, :]).then_inc(c["pT"], 1)

            def c_outputs(n):
                act.wait_ge(c["pv"], 4 * n + 4)
                wait(act, c["bt"], n)
                nc.scalar.copy(cO, bank[:, 7, :]).then_inc(c["oc"], 1)

            def c_oT(g):
                act.wait_ge(c["otr"], g + 1)
                wait(act, c["wo"], g)
                nc.scalar.copy(cOT[:], bank[:, 6, :]).then_inc(c["oT"], 1)

            def c_main(g, par, half, nxt):
                first = isinstance(g, int) and g == 0
                for j in range(16):
                    w = 16 * g + j
                    if j % 4 == 1 and not (first and j == 1):
                        c_outputs(4 * g + j // 4 - 1)
                    act.wait_ge(c["sub"], w + 1)
                    wait(act, c["ptr"], w - 1)
                    nc.scalar.activation(cP[:, j % 2], csub[:, j % 2], ACT.Exp, scale=DK ** -0.5).then_inc(c["exp"], 1)
                    if j or not first:
                        c_turned(w - 1, (j - 1) % 16)
                    if j == 3 and not first:
                        c_oT(g - 1)
                    if j == 6:
                        nxt(0)
                    if j == 7:
                        nxt(1)
                    if j == 9:
                        nxt(2)
            steps(act, [c_xT, c_qT, c_kT], c_main)
            c_turned(16 * G - 1, 15)
            c_outputs(4 * G - 1)
            c_oT(G - 1)

            act.wait_ge(c["s"], 16 * G)
            act.dma_start(w2_s, w2).then_inc(wG_in, 16)
            act.dma_start(b1_s, bass.AP(b1.tensor, 0, [[0, P], [1, 4 * E * P]])).then_inc(wG_in, 16)
            act.wait_ge(wF_in, 16)
            act.wait_ge(d["const"], 2)

            def d_xT(g, par, half):
                act.wait_ge(dn["tr"], g + 1)
                wait(act, d["v"], g - 1)
                nc.scalar.copy(xnT[:, par, :], bank[:, 0, :]).then_inc(d["xnT"], 1)

            def d_qT(g, par, half):
                act.wait_ge(d["q"], g + 1)
                wait(act, d["s"], 2 * (g - 1))
                for h in range(H4):
                    i = nc.scalar.activation(q4[:, par, h, :], bank[:, 1, :], ACT.Identity, bias=dbq[:, h:h + 1],
                                             scale=cols_s[:, C_HEAD4 + h:C_HEAD4 + h + 1])
                i.then_inc(d["qT"], 1)
                act.wait_ge(d["k"], g + 1)
                nc.scalar.activation(kT[:, par, :], bank[:, 0, :], ACT.Identity,
                                     bias=cols_s[:, C_MBK:C_MBK + 1]).then_inc(d["kT"], 1)

            def d_yT(g):
                act.wait_ge(d["ytr"], g + 1)
                wait(act, d["logit"], g)
                nc.scalar.copy(yT, bank[:, 4, :]).then_inc(d["yT"], 1)

            def d_oT(g):
                act.wait_ge(d["otr"], g + 1)
                wait(act, d["wo"], g)
                nc.scalar.copy(cOT[:], bank[:, 2, :]).then_inc(d["oT"], 1)

            def d_main(g, par, half, nxt):
                first = isinstance(g, int) and g == 0
                if not first:
                    d_oT(g - 1)
                for m in range(2):
                    act.wait_ge(d["sub"], 2 * g + m + 1)
                    wait(act, d["ptr"], 4 * (g - 1) + 2 * m + 2)
                    for n in range(2):
                        h = slice(n * S, (n + 1) * S)
                        i = nc.scalar.activation(dP[h, 8 * m:8 * m + 8, n * S:(n + 1) * S], dsub[h, m], ACT.Exp,
                                                 scale=D4 ** -0.5)
                    i.then_inc(d["exp"], 1)
                for h in range(H4):
                    w = 4 * g + h
                    act.wait_ge(d["ptr"], w + 1)
                    wait(act, d["pv"], w - 1)
                    nc.scalar.copy(cPT[:, h % 2, :], bank[:, 6 + h % 2, :]).then_inc(d["pT"], 1)
                    if h == 2:
                        nxt(0)
                nxt(1)
                if not first:
                    d_yT(g - 1)
            nc.scalar.activation(dbq[:], cols_s[:, C_HEAD4:C_HEAD4 + 4], ACT.Copy,
                                 scale=cols_s[:, C_MBQ:C_MBQ + 1]).then_inc(d["bq"], 1)
            act.wait_ge(d["bq"], 1)
            steps(act, [d_xT, d_qT], d_main)
            d_oT(G - 1)
            d_yT(G - 1)

            def m_xT(j, par):
                act.wait_ge(m["tr"], j + 1)
                wait(act, m["h"], j - 1)
                nc.scalar.copy(xeT[par], bank[:, 7 * par, 0:P]).then_inc(m["xT"], 1)

            def m_quad(j, q, last):
                for k in range(4):
                    par = k % 2
                    act.wait_ge(m["htr"], j + k + 1)
                    wait(act, m["up"], j + k - 1)
                    nc.scalar.activation(heT[par], bank[:, 3 + par, :], ACT.Relu).then_inc(m["hT"], 1)
                    if not last or k < 2:
                        m_xT(j + k + 2, par)
            m_xT(0, 0)
            m_xT(1, 1)
            quad_steps(act, m_quad)

            def e_scale(g, par, half):
                act.wait_ge(e["shift"], g + 1)
                wait(act, e["y"], g - 1)
                for t in range(GT):
                    i = nc.scalar.activation(xn[:, par, t, :], ysum[:, par, t, :], ACT.Identity,
                                             bias=shift[:, par, t:t + 1], scale=rstd[:, par, t:t + 1])
                i.then_inc(e["scaled"], 1)
            steps(act, [e_scale], lambda g, par, half, nxt: nxt(0))

        @block.tensor
        def _(pe):
            def a_k(g, par, half):
                pe.wait_ge(a["xn"], g + 1)
                wait(pe, a["xnT"], g)
                transpose_xn(pe, a, g, par)
                pe.wait_ge(a["ctx"][par], 16 * (half + 1))
                wait(pe, a["kT"], g)
                nc.tensor.matmul(bank[:, 2, :], wA_s[:, WK, :], ctxb[:, par, :], start=True, stop=True).then_inc(a["k"], 1)

            def a_qv(g, par, half):
                pe.wait_ge(a["xnT"], g + 1)
                wait(pe, a["qT"], g)
                nc.tensor.matmul(bank[:, 1, :], wA_s[:, WQ, :], xnT[:, par, :], start=True, stop=True).then_inc(a["q"], 1)
                wait(pe, a["vS"], g)
                for t in range(GT):
                    i = nc.tensor.matmul(bank[:, 3, t * P:(t + 1) * P], ctxb[:, par, t * P:(t + 1) * P],
                                         wA_s[:, WV, :], start=True, stop=True)
                i.then_inc(a["v"], 1)

            def a_out(g, par):
                pe.wait_ge(a["pT"], g + 1)
                pe.wait_ge(a["vS"], g + 1)
                wait(pe, a["xo"], g)
                for t in range(GT):
                    i = nc.tensor.matmul(bank[:, 6, t * P:(t + 1) * P], pT[:, par, t, :], vS[:, par, t, :],
                                         start=True, stop=True)
                i.then_inc(a["o"], 1)

            def a_main(g, par, half, nxt):
                pe.wait_ge(a["qT"], g + 1)
                pe.wait_ge(a["kT"], g + 1)
                wait(pe, a["sub"], g)
                for t in range(GT):
                    for n in range(2):
                        k = (2 * t + n) * S
                        i = nc.tensor.matmul(bank[n * S:(n + 1) * S, 4, t * S:(t + 1) * S], qT[:, par, k:k + S],
                                             kT[:, par, k:k + S], start=True, stop=True)
                i.then_inc(a["s"], 1)
                nxt(0)
                pe.wait_ge(a["exp"], g + 1)
                wait(pe, a["pT"], g)
                for t in range(GT):
                    i = nc.tensor.transpose(bank[:, 5, t * P:(t + 1) * P], pbd[:, par, t, :], ident[:])
                i.then_inc(a["ptr"], 1)
                nxt(1)
                a_out(g, par)
            pe.wait_ge(w_in, 16 * 3)
            pe.wait_ge(id_ready, 1)
            steps(pe, [a_k, a_qv], a_main)

            pe.wait_ge(a["xo"], G)
            pe.wait_ge(wB_in, 16)

            def b_turn(g, par, half):
                pe.wait_ge(b["xn"], g + 1)
                wait(pe, b["xnT"], g)
                transpose_xn(pe, b, g, par)

            def b_router(g, par, half):
                pe.wait_ge(b["xnT"], g + 1)
                wait(pe, b["lsub"], g)
                for t in range(GT):
                    i = nc.tensor.matmul(bank[:, 1, t * E:(t + 1) * E], xnT[:, par, t * P:(t + 1) * P], wrouter,
                                         start=True, stop=True)
                i.then_inc(b["logit"], 1)

            def b_main(g, par, half, nxt):
                def down(u):
                    w, pu = NE * g + u, (par + u) % 2
                    pe.wait_ge(b["h"], w + 1)
                    if u == 0 or u == 1:
                        wait(pe, b["acc"] if u else b["scaled"], NACC * g - 1 if u else NOD * g)
                    elif u % 2:
                        pe.wait_ge(b["scaled"], NOD * g + u // 2)
                    else:
                        pe.wait_ge(b["acc"], NACC * g + u // 2)
                    for t in range(GT):
                        i = nc.tensor.matmul(bank[:, 6 + pu, t * P:(t + 1) * P], hT[:, pu, t * P:(t + 1) * P],
                                             wdown[:, u, :], start=True, stop=True)
                    i.then_inc(b["down"], 1)

                if isinstance(g, int):
                    pe.wait_ge(b["xnT"], g + 1)
                for u in range(NE):
                    w, pu = NE * g + u, (par + u) % 2
                    wait(pe, b["act"], w - 1)
                    nc.tensor.matmul(bank[:, 2 + pu, :], wgate[:, u, :], xnT[:, par, :], start=True,
                                     stop=True).then_inc(b["gate"], 1)
                    wait(pe, b["h"], w - 1)
                    nc.tensor.matmul(bank[:, 4 + pu, :], wup[:, u, :], xnT[:, par, :], start=True,
                                     stop=True).then_inc(b["up"], 1)
                    if u:
                        down(u - 1)
                    if u == 3:
                        nxt(0)
                    if u == 5:
                        nxt(1)
                down(E)
            steps(pe, [b_turn, b_router], b_main)

            pe.wait_ge(b["acc"], NACC * G)
            pe.wait_ge(c["memrow"], 1)

            def c_turn(g, par, half):
                pe.wait_ge(c["xn"], g + 1)
                wait(pe, c["xo"], g - 1)
                wait(pe, c["vS"], 2 * g)
                transpose_xn(pe, c, g, par)

            def c_q(g, par, half):
                pe.wait_ge(c["xnT"], g + 1)
                nc.tensor.matmul(bank[:, 0, :], wC_s[:, 0, :], xnT[:, par, :], start=True, stop=True).then_inc(c["q"], 1)

            def c_k(g, par, half):
                pe.wait_ge(c["ctx"][par], 16 * (half + 1))
                pe.wait_ge(c["qT"], g + 1)
                nc.tensor.matmul(bank[:, 0, :], wC_s[:, 1, :], ctxb[:, par, :], start=True, stop=True).then_inc(c["k"], 1)

            def c_v(k):
                def part(g, par, half):
                    pe.wait_ge(c["kT"], g + 1)
                    if k:
                        pe.wait_ge(c["vS"], 2 * g + 1)
                    for n in range(NB // 2):
                        m = (k * NB // 2 + n) * S
                        i = nc.tensor.matmul(bank[0:S, 0, n * P:(n + 1) * P], ctxb[:, par, m:m + S], wC_s[:, 2, :],
                                             start=True, stop=True)
                    i.then_inc(c["v"], 1)
                return part

            def c_scores(g, par, j):
                t, r = j // 4, j % 4
                w = 16 * g + j
                wait(pe, c["sub"], w - 3)
                pe.wait_ge(c["qx"], g + 1)
                pe.wait_ge(c["kT"], g + 1)
                pe.wait_ge(c["mask"], g + 1)
                o = bank[:, 2 + r, :].rearrange("p (b u k) -> p b u k", b=2, u=2)
                m = mrow[0:1, par, t * P:(t + 1) * P].rearrange("p (b s) -> p b s", b=2)
                nc.tensor.matmul(o[:, :, :, 0:S], onesb[0:1, :], m.unsqueeze(2).to_broadcast([1, 2, 2, S]),
                                 start=True, stop=False, skip_group_check=True)
                for b1 in range(2):
                    for u in range(2):
                        i = nc.tensor.matmul(o[:, b1, u, :],
                                             qx[:, par, 2 * t + b1, (2 * r + u) * P:(2 * r + u + 1) * P],
                                             kk[:, par, 2 * t + b1, :], start=False,
                                             stop=(b1 == 1 and u == 1), skip_group_check=True)
                i.then_inc(c["s"], 1)

            def c_pv(w, j, par, tiles):
                t, r = j // 4, j % 4
                pe.wait_ge(c["pT"], w + 1)
                wait(pe, c["oc"], tiles)
                for b1 in range(2):
                    for hh in range(4):
                        i = nc.tensor.matmul(bank[32 * hh:32 * hh + VW, 7, r * P + b1 * S:r * P + b1 * S + S],
                                             v1[:, par, 2 * t + b1, (4 * r + hh) * VW:(4 * r + hh + 1) * VW],
                                             cPT[:, j % 2, (4 * b1 + hh) * S:(4 * b1 + hh + 1) * S],
                                             start=True, stop=True)
                i.then_inc(c["pv"], 1)

            def c_back(n):
                pe.wait_ge(c["oc"], n + 1)
                for r in range(4):
                    i = nc.tensor.transpose(bank[:, 6, r * P:(r + 1) * P], cO[:, r * P:(r + 1) * P], ident[:])
                i.then_inc(c["bt"], 1)

            def c_otrans(g, par):
                pe.wait_ge(c["on"], 4 * (g + 1))
                for t in range(GT):
                    i = nc.tensor.transpose(bank[:, 6, t * P:(t + 1) * P], Oa[:, par, t, :], ident[:])
                i.then_inc(c["otr"], 1)

            def c_out(g):
                pe.wait_ge(c["oT"], g + 1)
                for t in range(GT):
                    i = nc.tensor.matmul(bank[:, 0, t * P:(t + 1) * P], cOT[:, t * P:(t + 1) * P], wC_s[:, 3, :],
                                         start=True, stop=True)
                i.then_inc(c["wo"], 1)

            def c_main(g, par, half, nxt):
                first = isinstance(g, int) and g == 0
                last = isinstance(g, int) and g == G - 1
                if first:
                    pe.wait_ge(c["vS"], 2)
                    for j in range(4):
                        c_scores(g, par, j)
                for j in range(16):
                    w = 16 * g + j
                    if j == 4:
                        wait(pe, c["oT"], g)
                    if j % 4 == 2 and not (first and j == 2):
                        wait(pe, c["on"], 4 * g + j // 4)
                    pe.wait_ge(c["exp"], w + 1)
                    wait(pe, c["pT"], w - 1)
                    for u in range(4):
                        i = nc.tensor.transpose(bank[:, 1 if j % 2 else 6, u * P:(u + 1) * P], cP[:, j % 2, u, :],
                                                ident[:])
                    i.then_inc(c["ptr"], 1)
                    if j % 4 == 1 and not (first and j == 1):
                        pe.wait_ge(c["pT"], w)
                        c_back(4 * g + j // 4 - 1)
                    if j:
                        pe.wait_ge(c["vS"], 2 * g + 2)
                        c_pv(w - 1, j - 1, par, 4 * g + (j - 1) // 4)
                    elif not first:
                        c_pv(w - 1, 15, 1 - par, 4 * g - 1)
                    if j == 2 and not first:
                        pe.wait_ge(c["pT"], w + 1)
                        c_otrans(g - 1, 1 - par)
                    if j == 3 and not first:
                        pe.wait_ge(c["vS"], 2 * g + 2)
                        c_out(g - 1)
                    if j == 5:
                        nxt(0)
                    if j == 6:
                        nxt(1)
                    if j == 8:
                        nxt(2)
                    if j == 11:
                        nxt(3)
                    if j == 13:
                        nxt(4)
                    if j < 12:
                        c_scores(g, par, j + 4)
                    elif not last:
                        c_scores(g + 1, 1 - par, j - 12)
            steps(pe, [c_turn, c_q, c_k, c_v(0), c_v(1)], c_main)
            pe.wait_ge(c["pT"], 16 * G)
            c_pv(16 * G - 1, 15, 1, 4 * G - 1)
            c_back(4 * G - 1)
            c_otrans(G - 1, 1)
            c_out(G - 1)

            pe.wait_ge(c["xo"], G)
            pe.wait_ge(wF_in, 16)

            def d_turn(g, par, half):
                pe.wait_ge(dn["xn"], g + 1)
                wait(pe, d["kT"], g)
                transpose_xn(pe, dn, g, par)

            def d_qk(g, par, half):
                wait(pe, d["vS"], g)
                pe.wait_ge(d["xnT"], g + 1)
                nc.tensor.matmul(bank[:, 1, :], wF_s[:, 0:P], xnT[:, par, :], start=True, stop=True).then_inc(d["q"], 1)
                nc.tensor.matmul(bank[:, 0, :], wF_s[:, P:2 * P], xnT[:, par, :], start=True, stop=True).then_inc(d["k"], 1)

            def d_v(g, par, half):
                pe.wait_ge(d["qT"], g + 1)
                for t in range(GT):
                    i = nc.tensor.matmul(bank[:, 1, t * P:(t + 1) * P], xnT[:, par, t * P:(t + 1) * P],
                                         wF_s[:, 2 * P:3 * P], start=True, stop=True)
                i.then_inc(d["v"], 1)

            def d_out(g):
                pe.wait_ge(d["on"], 2 * g + 2)
                for t in range(GT):
                    i = nc.tensor.transpose(bank[:, 2, t * P:(t + 1) * P], dOa[:, t, :], ident[:])
                i.then_inc(d["otr"], 1)
                pe.wait_ge(d["oT"], g + 1)
                for t in range(GT):
                    i = nc.tensor.matmul(bank[:, 3, t * P:(t + 1) * P], cOT[:, t * P:(t + 1) * P], wF_s[:, 3 * P:4 * P],
                                         start=True, stop=True)
                i.then_inc(d["wo"], 1)

            def d_yturn(g, par):
                pe.wait_ge(d["normed"], g + 1)
                for t in range(GT):
                    i = nc.tensor.transpose(bank[:, 4, t * P:(t + 1) * P], ys[:, par, t, :], ident[:])
                i.then_inc(d["ytr"], 1)

            def d_logits(g):
                pe.wait_ge(d["yT"], g + 1)
                for t in range(GT):
                    i = nc.tensor.matmul(bank[:, 5, t * E:(t + 1) * E], yT[:, t * P:(t + 1) * P], wF_s[:, 4 * P:],
                                         start=True, stop=True)
                i.then_inc(d["logit"], 1)

            def d_main(g, par, half, nxt):
                first = isinstance(g, int) and g == 0
                pe.wait_ge(d["kT"], g + 1)
                wait(pe, d["sub"], 2 * g)
                for m in range(2):
                    for h in range(2):
                        for t in range(GT):
                            for n in range(2):
                                k = (2 * t + n) * S
                                i = nc.tensor.matmul(
                                    bank[n * S:(n + 1) * S, 4 + m, (h * GT + t) * S:(h * GT + t + 1) * S],
                                    q4[:, par, 2 * m + h, k:k + S], kT[:, par, k:k + S], start=True, stop=True)
                    i.then_inc(d["s"], 1)
                if not first:
                    d_out(g - 1)

                def turn(h):
                    pe.wait_ge(d["exp"], 2 * g + h // 2 + 1)
                    wait(pe, d["pT"], 4 * g + h - 1)
                    for t in range(GT):
                        i = nc.tensor.transpose(bank[:, 6 + h % 2, t * P:(t + 1) * P], dP[:, h * GT + t, :], ident[:])
                    i.then_inc(d["ptr"], 1)

                def pv(h):
                    pe.wait_ge(d["pT"], 4 * g + h + 1)
                    pe.wait_ge(d["vS"], g + 1)
                    if h == 2:
                        wait(pe, d["z"], 2 * g - 1)
                    for t in range(GT):
                        k = (h % 2 * GT + t) * (D4 + 1)
                        i = nc.tensor.matmul(bank[:, 2 + h // 2, k:k + D4 + 1], cPT[:, h % 2, t * P:(t + 1) * P],
                                             v4[:, par, t, h * (D4 + 1):(h + 1) * (D4 + 1)], start=True, stop=True)
                    i.then_inc(d["pv"], 1)
                turn(0)
                turn(1)
                pv(0)
                turn(2)
                nxt(0)
                pv(1)
                turn(3)
                nxt(1)
                pv(2)
                if not first:
                    d_yturn(g - 1, 1 - par)
                pv(3)
                if not first:
                    d_logits(g - 1)
                nxt(2)
                if not first:
                    pe.wait_ge(d["route"], 5 * g - 3)
            steps(pe, [d_turn, d_qk, d_v], d_main)
            d_out(G - 1)
            d_yturn(G - 1, 1)
            d_logits(G - 1)

            pe.wait_ge(d["route"], 5 * G)
            pe.wait_ge(io_ready, 3)
            has = mall[:].rearrange("p t e -> p e t")
            for n, w in enumerate((before[:], ones[:, 0:P])):
                nc.tensor.matmul(bank[:, n, 0:E * T], w, has, start=True, stop=True).then_inc(r_sums, 1)

            pe.wait_ge(slots_ready, 1)
            pe.wait_ge(wG_in, 16 * 4)

            def m_turn(j, k, q):
                par = k % 2
                if par == 0:
                    pe.wait_ge(m["x"][k // 2], 16 * (q + 1))
                wait(pe, m["xT"], j - 1)
                nc.tensor.transpose(bank[:, 7 * par, 0:P], xe[k // 2][:, par], ident[:]).then_inc(m["tr"], 1)

            def m_up(j, par, expert):
                pe.wait_ge(m["xT"], j + 1)
                wait(pe, m["hb"], j - 1)
                nc.tensor.matmul(bank[:, 1 + par, :], xeT[par], w1_s[:, bass.ds(expert * 4 * P, 4 * P)],
                                 start=True, stop=True).then_inc(m["h"], 1)

            def m_quad(j, q, last):
                expert = experts_of(pe, j, last)
                if isinstance(j, int) and j == 0:
                    m_up(0, 0, expert[0])
                for k in range(4):
                    par = k % 2
                    pe.wait_ge(m["hb"], j + k + 1)
                    wait(pe, m["hT"], j + k - 1)
                    for c in range(4):
                        i = nc.tensor.transpose(bank[:, 3 + par, c * P:(c + 1) * P], he[par][:, c * P:(c + 1) * P],
                                                ident[:])
                    i.then_inc(m["htr"], 1)
                    if not last or k < 3:
                        m_up(j + k + 1, 1 - par, expert[k + 1])
                    if not last or k < 2:
                        m_turn(j + k + 2, (k + 2) % 4, q + (k + 2) // 4)
                    pe.wait_ge(m["hT"], j + k + 1)
                    wait(pe, m["o"], j + k - 1)
                    for c in range(4):
                        i = nc.tensor.matmul(bank[:, 5 + par, 0:P], heT[par][:, c * P:(c + 1) * P],
                                             w2_s[:, bass.ds((expert[k] * 4 + c) * P, P)], start=(c == 0),
                                             stop=(c == 3))
                    i.then_inc(m["up"], 1)
            m_turn(0, 0, 0)
            m_turn(1, 1, 0)
            quad_steps(pe, m_quad)


def kernel(**inputs):
    import concourse.bacc as bacc
    from concourse.bass_utils import run_bass_kernel_spmd

    a = {k: np.asarray(v) for k, v in inputs.items()}
    cat = lambda parts: np.ascontiguousarray(np.concatenate([p.reshape(P, -1) for p in parts], axis=1))
    bqkv = a["L1_ffn_bqkv"].reshape(3, P)
    arrays = {
        "x": np.ascontiguousarray(a["x"].reshape(N, P)),
        "ctxT": np.ascontiguousarray(a["ctx_1024"].reshape(N, P).T),
        "maskrow": np.ascontiguousarray(a["mask_Bx1x1xS2_bk0"].reshape(1, N)),
        "wA": cat([a["L0_xattn_Wq"], a["L0_xattn_Wk"], a["L0_xattn_Wv"]]),
        "wB": cat([a["L0_ffn_Wg"].transpose(2, 0, 1), a["L0_ffn_Sg"].T, a["L0_ffn_Wu"].transpose(2, 0, 1),
                   a["L0_ffn_Su"].T, a["L0_ffn_Wd"].transpose(2, 0, 1), a["L0_ffn_Sd"].T, a["L0_ffn_Wr"].T]),
        "wC": cat([a["L1_xattn_Wq"].T, a["L1_xattn_Wk"].T, a["L1_xattn_Wv"].T, a["L1_xattn_Wo"].T]),
        "memT": np.ascontiguousarray(a["L1_xattn_m_k"][0].T),
        "mem": np.ascontiguousarray(a["L1_xattn_m_v"][0]),
        "wF": cat([a["L1_ffn_Wqkv"].T, a["L1_ffn_Wo"].T, a["L1_ffn_Wg"].T]),
        "w1": cat([a["L1_ffn_W1"].transpose(1, 0, 2)]),
        "w2": cat([a["L1_ffn_W2"].reshape(E, 4, P, P).transpose(2, 0, 1, 3)]),
        "b1": np.ascontiguousarray(a["L1_ffn_b1"]),
        "b2": np.ascontiguousarray(a["L1_ffn_b2"]),
        "rows": np.ascontiguousarray(np.broadcast_to(np.stack([
            a["L0_xattn_bv"], a["L1_xattn_bv"], a["L1_xattn_bo"], bqkv[2], a["L1_ffn_bo"], a["L1_ffn_g1"],
            a["L1_ffn_be1"], a["L1_ffn_g2"], a["L1_ffn_be2"]]).reshape(1, -1), (P, NROWS * P))),
        "cols": np.ascontiguousarray(np.stack([a["L0_xattn_bq"], a["L0_xattn_bk"], a["L1_xattn_bq"],
                                               a["L1_xattn_bk"], bqkv[0], bqkv[1]]
                                              + [(np.arange(P) // 8 == i).astype(np.float32)
                                                 for i in range(16)]
                                              + [(np.arange(P) // 32 == i).astype(np.float32)
                                                 for i in range(4)], axis=1)),
    }
    nc = bacc.Bacc("TRN2", target_bir_lowering=False, num_devices=1)
    args = [nc.dram_tensor("in_" + n, v.shape, mybir.dt.from_np(v.dtype), kind="ExternalInput").ap()
            for n, v in arrays.items()]
    out = nc.dram_tensor("out", (N, P), F32, kind="ExternalOutput").ap()
    program(nc, *args, out)
    r = run_bass_kernel_spmd(nc, [{"in_" + n: v for n, v in arrays.items()}], core_ids=[0])
    return r.results[0]["out"].reshape(B, S, P)
```
